# Optimizing a Trainium2 kernel written in Bass

```python
import numpy as np
import jax
import jax.numpy as jnp

def _softmax(x, axis=-1):
    return jax.nn.softmax(x, axis=axis)

def _gelu(x):
    return jax.nn.gelu(x, approximate=True)

def _silu(x):
    return jax.nn.silu(x)

def _sigmoid(x):
    return jax.nn.sigmoid(x)

def _layernorm(x, axis=-1, eps=1e-05):
    m = jnp.mean(x, axis=axis, keepdims=True)
    v = jnp.var(x, axis=axis, keepdims=True)
    return (x - m) / jnp.sqrt(v + eps)

def _scatter_add(tgt, idx, src, axis=0):
    return tgt.at[idx].add(src)

def _segment_sum(src, seg, n):
    return jax.ops.segment_sum(src, seg, n)
kernel_name = 'mk_prb_d1_jaxref_r4_d49618'

def setup_inputs(seed: int=0):
    np.random.seed(seed)
    _w = jnp.asarray

    def _L0_attn_setup():
        import jax, jax.numpy as jnp
        import numpy as np
        D_MODEL, D_STATE, D_CONV = (256, 16, 4)
        BATCH, SEQ = (4, 512)
        LN_EPS = 1e-05

        def _causal_depthwise_conv(x_btd, conv_w, conv_b):
            x_bdt = jnp.transpose(x_btd, (0, 2, 1))
            y = jax.lax.conv_general_dilated(x_bdt, conv_w, window_strides=(1,), padding=[(D_CONV - 1, 0)], dimension_numbers=('NCH', 'OIH', 'NCH'), feature_group_count=D_MODEL)
            y = y + conv_b[None, :, None]
            return jnp.transpose(y, (0, 2, 1))

        def _mamba_forward(x, W_in, b_in, conv_w, conv_b, W_bc, b_bc, W_dt, b_dt, A_log, D, W_out, b_out, ln_g, ln_b):
            B_, T, _ = x.shape
            proj = x @ W_in + b_in
            x_ssm, x_gate = jnp.split(proj, 2, axis=-1)
            x_conv = jax.nn.silu(_causal_depthwise_conv(x_ssm, conv_w, conv_b))
            BC = x_conv @ W_bc + b_bc
            Bm, Cm = jnp.split(BC, 2, axis=-1)
            dt = jax.nn.softplus(x_conv @ W_dt + b_dt)
            A = -jnp.exp(A_log)

            def step(h, inp):
                xt, dtt, Bt, Ct = inp
                dA = jnp.exp(dtt[:, :, None] * A)
                h = h * dA + (dtt * xt)[:, :, None] * Bt[:, None, :]
                y = jnp.einsum('bdn,bn->bd', h, Ct) + xt * D
                return (h, y)
            h0 = jnp.zeros((B_, D_MODEL, D_STATE), x.dtype)
            xs = (jnp.swapaxes(x_conv, 0, 1), jnp.swapaxes(dt, 0, 1), jnp.swapaxes(Bm, 0, 1), jnp.swapaxes(Cm, 0, 1))
            _, ys = jax.lax.scan(step, h0, xs)
            y = jnp.swapaxes(ys, 0, 1)
            y = y * jax.nn.silu(x_gate)
            out = y @ W_out + b_out
            res = out + x
            mu = jnp.mean(res, axis=-1, keepdims=True)
            var = jnp.var(res, axis=-1, keepdims=True)
            return (res - mu) * jax.lax.rsqrt(var + LN_EPS) * ln_g + ln_b
        key = jax.random.key(seed)
        ks = jax.random.split(key, 16)
        s_in = 1.0 / np.sqrt(D_MODEL)
        inp = {'x': jax.random.normal(ks[0], (BATCH, SEQ, D_MODEL), dtype=jnp.float32), 'W_in': jax.random.normal(ks[1], (D_MODEL, 2 * D_MODEL), dtype=jnp.float32) * s_in, 'b_in': jnp.zeros((2 * D_MODEL,), jnp.float32), 'conv_w': jax.random.normal(ks[2], (D_MODEL, 1, D_CONV), dtype=jnp.float32) * 0.5, 'conv_b': jnp.zeros((D_MODEL,), jnp.float32), 'W_bc': jax.random.normal(ks[3], (D_MODEL, 2 * D_STATE), dtype=jnp.float32) * s_in, 'b_bc': jnp.zeros((2 * D_STATE,), jnp.float32), 'W_dt': jax.random.normal(ks[4], (D_MODEL, D_MODEL), dtype=jnp.float32) * s_in, 'b_dt': jnp.zeros((D_MODEL,), jnp.float32), 'A_log': jax.random.normal(ks[5], (D_MODEL, D_STATE), dtype=jnp.float32), 'D': jnp.ones((D_MODEL,), jnp.float32), 'W_out': jax.random.normal(ks[6], (D_MODEL, D_MODEL), dtype=jnp.float32) * s_in, 'b_out': jnp.zeros((D_MODEL,), jnp.float32), 'ln_g': jnp.ones((D_MODEL,), jnp.float32), 'ln_b': jnp.zeros((D_MODEL,), jnp.float32)}
        return inp
    _L0_attn_in = _L0_attn_setup()

    def _L0_ffn_setup():
        import jax, jax.numpy as jnp
        import numpy as np
        DIM = 256
        E = 8
        K = 2
        EPS = 1e-05

        def _ln(x, g, b):
            mu = jnp.mean(x, axis=-1, keepdims=True)
            var = jnp.mean(jnp.square(x - mu), axis=-1, keepdims=True)
            return (x - mu) * jax.lax.rsqrt(var + EPS) * g + b
        key = jax.random.key(seed)
        ks = jax.random.split(key, 8)
        H = 2 * DIM
        s_in = 1.0 / np.sqrt(DIM)
        s_h = 1.0 / np.sqrt(H)
        return {'x': jax.random.normal(ks[0], (2, 512, DIM), dtype=jnp.float32), 'gate_w': jax.random.uniform(ks[1], (DIM, E), minval=-s_in, maxval=s_in, dtype=jnp.float32), 'w1': jax.random.uniform(ks[2], (E, DIM, H), minval=-s_in, maxval=s_in, dtype=jnp.float32), 'b1': jax.random.uniform(ks[3], (E, H), minval=-s_in, maxval=s_in, dtype=jnp.float32), 'ln1_g': jnp.ones((E, H), dtype=jnp.float32), 'ln1_b': jnp.zeros((E, H), dtype=jnp.float32), 'w2': jax.random.uniform(ks[4], (E, H, DIM), minval=-s_h, maxval=s_h, dtype=jnp.float32), 'b2': jax.random.uniform(ks[5], (E, DIM), minval=-s_h, maxval=s_h, dtype=jnp.float32), 'ln_g': jnp.ones((DIM,), dtype=jnp.float32), 'ln_b': jnp.zeros((DIM,), dtype=jnp.float32)}
    _L0_ffn_in = _L0_ffn_setup()
    _d = {'L0_attn_x': _L0_attn_in['x'], 'L0_attn_W_in': _L0_attn_in['W_in'], 'L0_attn_b_in': _L0_attn_in['b_in'], 'L0_attn_conv_w': _L0_attn_in['conv_w'], 'L0_attn_conv_b': _L0_attn_in['conv_b'], 'L0_attn_W_bc': _L0_attn_in['W_bc'], 'L0_attn_b_bc': _L0_attn_in['b_bc'], 'L0_attn_W_dt': _L0_attn_in['W_dt'], 'L0_attn_b_dt': _L0_attn_in['b_dt'], 'L0_attn_A_log': _L0_attn_in['A_log'], 'L0_attn_D': _L0_attn_in['D'], 'L0_attn_W_out': _L0_attn_in['W_out'], 'L0_attn_b_out': _L0_attn_in['b_out'], 'L0_attn_ln_g': _L0_attn_in['ln_g'], 'L0_attn_ln_b': _L0_attn_in['ln_b'], 'L0_ffn_gate_w': _L0_ffn_in['gate_w'], 'L0_ffn_w1': _L0_ffn_in['w1'], 'L0_ffn_b1': _L0_ffn_in['b1'], 'L0_ffn_ln1_g': _L0_ffn_in['ln1_g'], 'L0_ffn_ln1_b': _L0_ffn_in['ln1_b'], 'L0_ffn_w2': _L0_ffn_in['w2'], 'L0_ffn_b2': _L0_ffn_in['b2'], 'L0_ffn_ln_g': _L0_ffn_in['ln_g'], 'L0_ffn_ln_b': _L0_ffn_in['ln_b']}
    _x0 = _d['L0_attn_x']
    _d['L0_attn_x'] = jax.random.normal(jax.random.fold_in(jax.random.key(seed), 1), (8, 1024, 256), dtype=_x0.dtype)
    del _x0
    return _d

def reference(L0_attn_x, L0_attn_W_in, L0_attn_b_in, L0_attn_conv_w, L0_attn_conv_b, L0_attn_W_bc, L0_attn_b_bc, L0_attn_W_dt, L0_attn_b_dt, L0_attn_A_log, L0_attn_D, L0_attn_W_out, L0_attn_b_out, L0_attn_ln_g, L0_attn_ln_b, L0_ffn_gate_w, L0_ffn_w1, L0_ffn_b1, L0_ffn_ln1_g, L0_ffn_ln1_b, L0_ffn_w2, L0_ffn_b2, L0_ffn_ln_g, L0_ffn_ln_b):

    def _L0_attn_ref(x, W_in, b_in, conv_w, conv_b, W_bc, b_bc, W_dt, b_dt, A_log, D, W_out, b_out, ln_g, ln_b):
        import jax, jax.numpy as jnp
        import numpy as np
        D_MODEL, D_STATE, D_CONV = (256, 16, 4)
        BATCH, SEQ = (4, 512)
        LN_EPS = 1e-05

        def _causal_depthwise_conv(x_btd, conv_w, conv_b):
            x_bdt = jnp.transpose(x_btd, (0, 2, 1))
            y = jax.lax.conv_general_dilated(x_bdt, conv_w, window_strides=(1,), padding=[(D_CONV - 1, 0)], dimension_numbers=('NCH', 'OIH', 'NCH'), feature_group_count=D_MODEL)
            y = y + conv_b[None, :, None]
            return jnp.transpose(y, (0, 2, 1))

        def _mamba_forward(x, W_in, b_in, conv_w, conv_b, W_bc, b_bc, W_dt, b_dt, A_log, D, W_out, b_out, ln_g, ln_b):
            B_, T, _ = x.shape
            proj = x @ W_in + b_in
            x_ssm, x_gate = jnp.split(proj, 2, axis=-1)
            x_conv = jax.nn.silu(_causal_depthwise_conv(x_ssm, conv_w, conv_b))
            BC = x_conv @ W_bc + b_bc
            Bm, Cm = jnp.split(BC, 2, axis=-1)
            dt = jax.nn.softplus(x_conv @ W_dt + b_dt)
            A = -jnp.exp(A_log)

            def step(h, inp):
                xt, dtt, Bt, Ct = inp
                dA = jnp.exp(dtt[:, :, None] * A)
                h = h * dA + (dtt * xt)[:, :, None] * Bt[:, None, :]
                y = jnp.einsum('bdn,bn->bd', h, Ct) + xt * D
                return (h, y)
            h0 = jnp.zeros((B_, D_MODEL, D_STATE), x.dtype)
            xs = (jnp.swapaxes(x_conv, 0, 1), jnp.swapaxes(dt, 0, 1), jnp.swapaxes(Bm, 0, 1), jnp.swapaxes(Cm, 0, 1))
            _, ys = jax.lax.scan(step, h0, xs)
            y = jnp.swapaxes(ys, 0, 1)
            y = y * jax.nn.silu(x_gate)
            out = y @ W_out + b_out
            res = out + x
            mu = jnp.mean(res, axis=-1, keepdims=True)
            var = jnp.var(res, axis=-1, keepdims=True)
            return (res - mu) * jax.lax.rsqrt(var + LN_EPS) * ln_g + ln_b
        return _mamba_forward(x, W_in, b_in, conv_w, conv_b, W_bc, b_bc, W_dt, b_dt, A_log, D, W_out, b_out, ln_g, ln_b)

    def _L0_ffn_ref(x, gate_w, w1, b1, ln1_g, ln1_b, w2, b2, ln_g, ln_b):
        import jax, jax.numpy as jnp
        import numpy as np
        DIM = 256
        E = 8
        K = 2
        EPS = 1e-05

        def _ln(x, g, b):
            mu = jnp.mean(x, axis=-1, keepdims=True)
            var = jnp.mean(jnp.square(x - mu), axis=-1, keepdims=True)
            return (x - mu) * jax.lax.rsqrt(var + EPS) * g + b
        shape = x.shape
        xf = x.reshape(-1, shape[-1])
        gates = jax.nn.softmax(xf @ gate_w, axis=-1)
        topw, topi = jax.lax.top_k(gates, K)
        topw = topw / jnp.sum(topw, axis=-1, keepdims=True)
        combine = jnp.sum(topw[:, :, None] * jax.nn.one_hot(topi, E, dtype=xf.dtype), axis=1)
        h = jnp.einsum('td,edh->teh', xf, w1) + b1
        h = _ln(h, ln1_g, ln1_b)
        h = jax.nn.gelu(h, approximate=False)
        y = jnp.einsum('teh,ehd->ted', h, w2) + b2
        out = jnp.einsum('ted,te->td', y, combine)
        out = _ln(out + xf, ln_g, ln_b)
        return out.reshape(shape)
    x = L0_attn_x
    xn = _layernorm(x, axis=-1)
    x = x + _L0_attn_ref(xn, L0_attn_W_in, L0_attn_b_in, L0_attn_conv_w, L0_attn_conv_b, L0_attn_W_bc, L0_attn_b_bc, L0_attn_W_dt, L0_attn_b_dt, L0_attn_A_log, L0_attn_D, L0_attn_W_out, L0_attn_b_out, L0_attn_ln_g, L0_attn_ln_b) + _L0_ffn_ref(xn, L0_ffn_gate_w, L0_ffn_w1, L0_ffn_b1, L0_ffn_ln1_g, L0_ffn_ln1_b, L0_ffn_w2, L0_ffn_b2, L0_ffn_ln_g, L0_ffn_ln_b)
    return x

_drawn_inputs = setup_inputs


def setup_inputs(seed=0):
    import zlib

    import numpy as np

    out = dict(_drawn_inputs(seed))
    spreads = {'L0_attn_b_in': (0.0, 0.1),
     'L0_attn_conv_b': (0.0, 0.1),
     'L0_attn_b_bc': (0.0, 0.1),
     'L0_attn_b_dt': (0.0, 0.8),
     'L0_attn_D': (1.0, 0.6),
     'L0_attn_b_out': (0.0, 0.299),
     'L0_attn_ln_g': (1.0, 0.2),
     'L0_attn_ln_b': (0.0, 0.1),
     'L0_ffn_ln1_g': (1.0, 0.6),
     'L0_ffn_ln1_b': (0.0, 0.8),
     'L0_ffn_ln_g': (1.0, 0.2),
     'L0_ffn_ln_b': (0.0, 0.1)}
    factors = {'L0_ffn_b1': 8.0, 'L0_ffn_b2': 8.0}
    for name, (base, spread) in spreads.items():
        noise = np.random.default_rng([zlib.crc32(name.encode()), seed]).standard_normal(out[name].shape)
        drawn = base * np.exp(spread * noise) if base else spread * noise
        out[name] = jnp.asarray(drawn.astype(out[name].dtype))
    for name, factor in factors.items():
        out[name] = (out[name] * factor).astype(out[name].dtype)
    return out
```

```python
import numpy as np
import concourse.bass as bass
from concourse import mybir
from contextlib import ExitStack, contextmanager

ALU = mybir.AluOpType
ACT = mybir.ActivationFunctionType
AX = mybir.AxisListType
F32 = mybir.dt.float32
BF16 = mybir.dt.bfloat16
I32 = mybir.dt.int32

BATCH, SEQ, DIM, STATE, TAPS = 8, 1024, 256, 16, 4
EXPERTS, HIDDEN = 8, 512
P = 128
EPS = 1e-5
KD = DIM // P
KH = HIDDEN // P
TOKENS = BATCH * SEQ
TILES = TOKENS // P
CHUNK = 512
TPC = CHUNK // P
CHUNKS = TOKENS // CHUNK
PAIRS = STATE // 2
SORTED = 2 * TILES + EXPERTS
GROUP = 8
TURNS = TILES // GROUP
PARTS = 3
BC = 2 * STATE
CONSTS = 20


class Chain:

    def __init__(self, eng, sem):
        self.eng, self.sem, self.base, self.n = eng, sem, 0, 0

    def mark(self, ins):
        ins.then_inc(self.sem, 1)
        self.n += 1

    def wait(self):
        self.eng.wait_ge(self.sem, self.base + self.n)

    @contextmanager
    def turn(self, i, turns, per_turn):
        base, n = self.base, self.n
        self.base, self.n = base + n + i * per_turn, 0
        yield
        assert self.n == per_turn, (self.n, per_turn)
        self.base, self.n = base, n + turns * per_turn


def build_program(nc, x, W_in, b_in, conv_w, conv_b, W_bc, b_bc, W_dt, b_dt, A_log, D_skip, W_out, b_out,
                  ln_g, ln_b, gate_w, w1, b1, ln1_g, ln1_b, w2, b2, fln_g, fln_b, out):
    x = x.rearrange("b t d -> (b t) d")
    out = out.rearrange("b t d -> (b t) d")
    xnT_d = nc.dram_tensor("xnT_d", [CHUNKS + 1, P, KD * CHUNK], F32).ap()
    sorted_x = nc.dram_tensor("sorted_x", [(SORTED + 1) * P, DIM], F32).ap()
    sorted_y = nc.dram_tensor("sorted_y", [(SORTED + 1) * P, DIM], F32).ap()
    mamba_d = nc.dram_tensor("mamba_d", [TOKENS, DIM], F32).ap()
    b1_parts_d = nc.dram_tensor("b1_parts_d", [PARTS, EXPERTS * HIDDEN], BF16).ap()
    b2_parts_d = nc.dram_tensor("b2_parts_d", [PARTS, EXPERTS * DIM], BF16).ap()

    ctx = ExitStack()
    with ctx:
        def sb(name, shape, dt=F32):
            return ctx.enter_context(nc.sbuf_tensor(name, shape, dt))

        def pb(name, shape):
            return ctx.enter_context(nc.psum_tensor(name, shape, F32))

        def sem(name):
            return ctx.enter_context(nc.semaphore(name))

        w1_sb = sb("w1_sb", [P, EXPERTS, KD, HIDDEN])
        w2_sb = sb("w2_sb", [P, EXPERTS, KH, DIM])
        g1_rep = sb("g1_rep", [P, EXPERTS, HIDDEN])
        be1_rep = sb("be1_rep", [P, EXPERTS, HIDDEN])
        b1_rows = sb("b1_rows", [PARTS, EXPERTS, HIDDEN], BF16)
        b2_rows = sb("b2_rows", [PARTS, EXPERTS, DIM], BF16)
        gate_sb = sb("gate_sb", [P, KD, EXPERTS])
        W_in_sb = sb("W_in_sb", [P, KD, 2 * DIM])
        W_dt_sb = sb("W_dt_sb", [P, KD, DIM])
        W_out_sb = sb("W_out_sb", [P, KD, DIM])
        W_bc_sb = sb("W_bc_sb", [P, KD, PARTS, BC])
        b_in_sb = sb("b_in_sb", [P, 2 * KD])
        conv_w_sb = sb("conv_w_sb", [P, KD, TAPS])
        conv_b_sb = sb("conv_b_sb", [P, KD])
        b_dt_sb = sb("b_dt_sb", [P, KD])
        b_bc_sb = sb("b_bc_sb", [PARTS * BC, 1])
        A_sb = sb("A_sb", [P, KD, STATE])
        D_sb = sb("D_sb", [P, KD])
        diagD = sb("diagD", [P, KD, P])
        ident = sb("ident", [P, P])
        before = sb("before", [P, P])
        ones = sb("ones", [P, P])
        ones_bf = sb("ones_bf", [PARTS, P], BF16)
        pick = sb("pick", [PARTS * BC, BC, P], BF16)
        eps_col = sb("eps_col", [P, 1])
        half_neg = sb("half_neg", [P, 1])
        mean_var = sb("mean_var", [P, TILES, 2])
        rstd = sb("rstd", [P, TILES])
        weight = sb("weight", [P, TILES, 2])
        place = sb("place", [P, TILES, 2], I32)
        place_y = sb("place_y", [P, TILES, 2], I32)
        expert_of = sb("expert_of", [1, SORTED + 1], I32)

        class Carve:

            def __init__(self, tensor, size):
                self.tensor, self.size, self.at = tensor, size, 0

            def take(self, *shape):
                n = int(np.prod(shape))
                v = self.tensor[:, self.at:self.at + n]
                self.at += n
                assert self.at <= self.size, (self.at, self.size)
                if len(shape) == 2:
                    return v.rearrange("p (a b) -> p a b", a=shape[0])
                if len(shape) == 3:
                    return v.rearrange("p (a b c) -> p a b c", a=shape[0], b=shape[1])
                return v

        area = sb("area", [P, TILES * DIM])
        xn_all = area[:, :].rearrange("p (n d) -> p n d", d=DIM)
        scan_area = Carve(area, TILES * DIM)
        decay = scan_area.take(2, KD, CHUNK)
        inflow = scan_area.take(2, KD, CHUNK)
        h_sb = scan_area.take(2, KD, CHUNK)
        hC = scan_area.take(2, KD, CHUNK)
        xT_in = scan_area.take(KD, CHUNK)
        gate_silu = scan_area.take(KD, CHUNK)
        x_conv = scan_area.take(KD, CHUNK)
        dt_sb = scan_area.take(KD, CHUNK)
        dtx = scan_area.take(KD, CHUNK)
        B_rep = scan_area.take(2, CHUNK)
        xpad = scan_area.take(KD, TAPS - 1 + CHUNK)
        bc_f = scan_area.take(CHUNK)[0:PARTS * BC, :]
        bc_parts = scan_area.take(CHUNK // 2)[0:PARTS * BC, :].bitcast(BF16)
        bc_mid = hC[:, 0, 0, 0:CHUNK // 2][0:PARTS * BC, :].bitcast(BF16)
        soft_abs, soft_relu, conv_acc = decay[:, 0], decay[:, 1], inflow[:, 1]
        gated = inflow[:, 0]
        mo_stage = h_sb[:, 0].rearrange("p a b -> p (a b)")
        end_area = Carve(area, TILES * DIM)
        ex, emo, ey1, ey2, exn, er0, er1, eo = ([end_area.take(2, DIM) for _ in range(2)] for _ in range(8))
        e_g0, e_g1, e_bout, e_b0, e_b1 = (end_area.take(DIM) for _ in range(5))
        estats = [end_area.take(2, 2, 6) for _ in range(2)]
        emv = [end_area.take(2, 2, 2) for _ in range(2)]
        ers = [end_area.take(2, 2) for _ in range(2)]
        early = Carve(w1_sb[:, :, :, :].rearrange("p e k h -> p (e k h)"), EXPERTS * KD * HIDDEN)
        stage_T = [early.take(KD, TPC, P) for _ in range(2)]
        ring = Carve(w2_sb[:, :, :, :].rearrange("p e k d -> p (e k d)"), EXPERTS * KH * DIM)
        xn_turn = ring.take(GROUP, DIM)
        logits, probs, top1, top2, scratch = (early.take(TILES, EXPERTS) for _ in range(5))
        not_first = early.take(EXPERTS, TILES)
        slot_cmp = early.take(SORTED, EXPERTS)
        slots = early.take(SORTED)
        ones_e = early.take(EXPERTS)
        bsplit = early.take(48)
        bsplit_bf = early.take(PARTS * 48 // 2).bitcast(BF16).rearrange("p (r n) -> p r n", r=PARTS)
        iota_e, iota_tile = early.take(EXPERTS), early.take(TILES)
        t1, t2, t3 = (early.take(TILES) for _ in range(3))
        place_f = early.take(TILES, 2)
        h_last = sb("h_last", [P, KD, STATE])
        xin = sb("xin", [P, DIM])
        ffn_xT = sb("ffn_xT", [P, KD, P])
        h_norm = sb("h_norm", [P, HIDDEN])
        h_aff = sb("h_aff", [P, HIDDEN])
        h_act = sb("h_act", [P, HIDDEN])
        h_T = sb("h_T", [P, KH, P])
        y_out = sb("y_out", [P, DIM])
        stats = sb("stats", [P, GROUP, 6])
        turn_mv = sb("turn_mv", [P, GROUP, 2])
        hstats = sb("hstats", [P, 6])
        hmv = sb("hmv", [P, 2])
        hve = sb("hve", [P, 1])
        held = sb("held", [P, 1])
        hrs = sb("hrs", [P, 1])
        tiles_of, tiles_end, rows_start = (sb(f"te{i}", [P, EXPERTS]) for i in range(3))

        psY = pb("psY", [P, KD * CHUNK])
        psC = pb("psC", [P, 2 * CHUNK])
        psB = pb("psB", [P, CHUNK])
        psH = pb("psH", [P, HIDDEN])
        psT = pb("psT", [P, HIDDEN])
        psX = pb("psX", [P, HIDDEN])
        psTr = [psH, psT]

        names = """w_small w_mamba w_ffn w_end biases_in b_split b_split_out b_rows_in consts_pool zeros_ready
            zero_fill x_in ve_ready sqrt_ready xn_ready tr_ready T_copied logits_done xT_store0 xT_store1
            scores_ready exp_ready chosen_ready counts_ready placed scattered dve_chain A_exp diag_ready
            xT_loaded ssm_ready gate_ready xpad_ready gate_done conv_ready xc_ready bc_ready dt_ready bcp_ready
            soft_chain soft_ready dtx_ready y_init repB_ready repC_ready B_copied exp_done dbx_done scan_done
            hC_done sum_done y_gated out_ready mo_copied mo_stored
            xin_loaded xin_T xT_copied h_ready bn_done var_ready ve_h rstd_ready ln_a ln_done gelu_done hT_done
            hT_copied y_ready y_copied y_stored pool_consts
            ex_in0 ex_in1 ey_in0 ey_in1 e_chain e_var e_sqrt e_done0 e_done1 e_store0 e_store1""".split()
        S = {n: sem(n) for n in names}
        block = ctx.enter_context(nc.Block())

        def column(v, k):
            return v.rearrange("(k p o) -> k p o", p=P, o=1)[k]

        def everywhere(v):
            return v.rearrange("(a n) -> a n", a=1).to_broadcast([P, v.shape[0]])

        small_loads = [
            (gate_sb[:, :, :], gate_w.rearrange("(k p) e -> p k e", p=P)),
            (A_sb[:, :, :], A_log.rearrange("(k p) n -> p k n", p=P)),
            (conv_w_sb[:, :, :], conv_w.rearrange("(k p) o t -> p k (o t)", p=P)),
        ]
        for dst, src, n in ((b_in_sb, b_in, 2 * KD), (conv_b_sb, conv_b, KD), (b_dt_sb, b_dt, KD), (D_sb, D_skip, KD)):
            small_loads += [(dst[:, k:k + 1], column(src, k)) for k in range(n)]
        small_loads += [(b_bc_sb[r * BC:(r + 1) * BC, :], b_bc.rearrange("(p o) -> p o", o=1)) for r in range(PARTS)]
        mamba_loads = [
            (W_in_sb[:, :, :], W_in.rearrange("(k p) n -> p k n", p=P)),
            (W_dt_sb[:, :, :], W_dt.rearrange("(k p) n -> p k n", p=P)),
            (W_out_sb[:, :, :], W_out.rearrange("(k p) n -> p k n", p=P)),
        ] + [(W_bc_sb[:, :, r, :], W_bc.rearrange("(k p) n -> p k n", p=P)) for r in range(PARTS)]
        w2_loads = [(w2_sb[:, e, :, :], w2[e].rearrange("(k p) d -> p k d", p=P)) for e in range(EXPERTS)]
        w1_loads = [(w1_sb[:, e, :, :], w1[e].rearrange("(k p) h -> p k h", p=P)) for e in range(EXPERTS)]
        rep_loads = [
            (rep[:, :, :].rearrange("p e h -> p (e h)"), everywhere(src.rearrange("e h -> (e h)")))
            for rep, src in ((g1_rep, ln1_g), (be1_rep, ln1_b))
        ]
        end_loads = [(dst, everywhere(v)) for dst, v in
                     ((e_g0, ln_g), (e_g1, fln_g), (e_bout, b_out), (e_b0, ln_b), (e_b1, fln_b))]
        W_SMALL, W_MAMBA = 16 * len(small_loads), 16 * len(mamba_loads)
        W_FFN = 16 * (len(w1_loads) + len(w2_loads) + len(rep_loads))

        @block.sync
        def _(sp):
            for name in ("x_in", "y_stored", "mo_stored"):
                sp.sem_inc(S[name], 16)
            for dst, src in ((bsplit[:, 0:32], b1), (bsplit[:, 32:48], b2)):
                sp.dma_start(dst, src.rearrange("e h -> (e h)").rearrange("(p c) -> p c", p=P)).then_inc(S["biases_in"], 16)
            with sp.Fori(0, TURNS) as j:
                sp.wait_ge(S["x_in"], j * 16 + 16)
                sp.dma_start(xn_all[:, bass.ds(j * GROUP, GROUP), :],
                             x[bass.ds(j * (GROUP * P), GROUP * P), :].rearrange("(n p) d -> p n d", p=P)
                             ).then_inc(S["x_in"], 16)
            for dst, src in mamba_loads:
                sp.dma_start(dst, src).then_inc(S["w_mamba"], 16)
            sp.wait_ge(S["zeros_ready"], 1)
            for n0 in range(0, SORTED + 1, 32):
                n1 = min(SORTED + 1, n0 + 32)
                sp.dma_start(sorted_x[n0 * P:n1 * P, :].rearrange("(n p) d -> p n d", p=P),
                             y_out[:, :].rearrange("p (a d) -> p a d", a=1).to_broadcast([P, n1 - n0, DIM])
                             ).then_inc(S["zero_fill"], 16)
            sp.dma_start(xnT_d[CHUNKS].rearrange("p (n d) -> p n d", d=DIM),
                         y_out[:, :].rearrange("p (a d) -> p a d", a=1).to_broadcast([P, KD * CHUNK // DIM, DIM])
                         ).then_inc(S["zero_fill"], 16)
            for dst, src in rep_loads:
                sp.dma_start(dst, src).then_inc(S["w_ffn"], 16)
            sp.wait_ge(S["b_split"], 5)
            sp.dma_start(b1_parts_d.rearrange("r (p c) -> p r c", p=P), bsplit_bf[:, :, 0:32]).then_inc(S["b_split_out"], 16)
            sp.dma_start(b2_parts_d.rearrange("r (p c) -> p r c", p=P), bsplit_bf[:, :, 32:48]).then_inc(S["b_split_out"], 16)
            sp.wait_ge(S["b_split_out"], 32)
            sp.dma_start(b1_rows[:, :, :].rearrange("r e h -> r (e h)"), b1_parts_d).then_inc(S["b_rows_in"], 16)
            sp.dma_start(b2_rows[:, :, :].rearrange("r e h -> r (e h)"), b2_parts_d).then_inc(S["b_rows_in"], 16)
            sp.wait_ge(S["placed"], 1)
            sp.wait_ge(S["xT_store0"], 16 * TURNS + 16)
            sp.wait_ge(S["xT_store1"], 16 * TURNS + 16)
            for dst, src in w1_loads + w2_loads:
                sp.dma_start(dst, src).then_inc(S["w_ffn"], 16)

            def load_tile(i):
                sp.wait_ge(S["xin_T"], i + 1)
                sp.dma_start(xin[:, :], sorted_x[bass.ds(i * P, P), :]).then_inc(S["xin_loaded"], 16)

            def store_tile(i):
                sp.wait_ge(S["y_copied"], i + 1 + 1)
                sp.dma_start(sorted_y[bass.ds(i * P, P), :], y_out[:, :]).then_inc(S["y_stored"], 16)

            def load_chunk(c):
                sp.dma_start(xT_in, xnT_d[bass.ds(c, 1)].rearrange("o p (k t) -> p (o k) t", k=KD)).then_inc(S["xT_loaded"], 16)

            sp.wait_ge(S["scattered"], 16 * 2 * TILES)
            sp.dma_start(xT_in, xnT_d[0].rearrange("p (k t) -> p k t", k=KD)).then_inc(S["xT_loaded"], 16)
            sp.wait_ge(S["zero_fill"], 16 * 6)
            sp.dma_start(xin[:, :], sorted_x[0:P, :]).then_inc(S["xin_loaded"], 16)
            with sp.Fori(0, CHUNKS) as c:
                sp.wait_ge(S["gate_ready"], c + 1)
                load_chunk(c + 1)
                with sp.Fori(0, PAIRS) as pr:
                    load_tile(c * PAIRS + pr + 1)
                    store_tile(c * PAIRS + pr)
                sp.wait_ge(S["mo_copied"], c + 1 + 1)
                sp.dma_start(mamba_d[bass.ds(c * CHUNK, CHUNK), :].rearrange("(q p) d -> p q d", p=P),
                             mo_stage.rearrange("p (q d) -> p q d", d=DIM)).then_inc(S["mo_stored"], 16)
            with sp.Fori(CHUNKS * PAIRS, SORTED) as i:
                load_tile(i + 1)
                store_tile(i)
            store_tile(SORTED)
            sp.wait_ge(S["xin_loaded"], 16 * (SORTED + 1))
            sp.wait_ge(S["xT_loaded"], 16 * (CHUNKS + 1))
            sp.wait_ge(S["mo_stored"], 16 * CHUNKS + 16)

            for dst, src in end_loads:
                sp.dma_start(dst, src).then_inc(S["w_end"], 16)
            with sp.Fori(0, TILES // 4) as j:
                for q in range(2):
                    t0 = (j * 2 + q) * (2 * P)
                    sp.wait_ge(S[f"e_done{q}"], j + 1)
                    sp.dma_start(ex[q], x[bass.ds(t0, 2 * P), :].rearrange("(n p) d -> p n d", p=P)).then_inc(S[f"ex_in{q}"], 16)
                    sp.dma_start(emo[q], mamba_d[bass.ds(t0, 2 * P), :].rearrange("(n p) d -> p n d", p=P)).then_inc(S[f"ex_in{q}"], 16)
                    
            sp.wait_ge(S["e_store0"], 16 * TILES // 4 + 16)
            sp.wait_ge(S["e_store1"], 16 * TILES // 4 + 16)

        @block.gpsimd
        def _(pool):
            pool.memset(y_out[:, :], 0.0).then_inc(S["zeros_ready"], 1)
            for k in range(2):
                pool.memset([ident, before][k][:, :], 0.0 if k == 0 else 1.0).then_inc(S["pool_consts"], 1)
            pool.memset(pick[:, :, :], 0.0).then_inc(S["pool_consts"], 1)
            pool.wait_ge(S["pool_consts"], 3)
            pool.affine_select(out=ident[:, :], in_=ident[:, :], compare_op=ALU.not_equal, fill=1.0, base=0,
                               pattern=[[-1, P]], channel_multiplier=1).then_inc(S["pool_consts"], 1)
            pool.affine_select(out=before[:, :], in_=before[:, :], compare_op=ALU.is_gt, fill=0.0, base=0,
                               pattern=[[1, P]], channel_multiplier=-1).then_inc(S["pool_consts"], 1)
            for r in range(PARTS):
                pool.wait_ge(S["pool_consts"], 5 + r)
                pool.affine_select(out=pick[:, :, :], in_=pick[:, :, :], compare_op=ALU.not_equal, fill=1.0,
                                   base=-BC * r, pattern=[[-1, BC], [0, P]], channel_multiplier=1
                                   ).then_inc(S["pool_consts"], 1)
            pool.memset(ones[:, :], 1.0).then_inc(S["pool_consts"], 1)
            pool.memset(ones_bf[:, :], 1.0).then_inc(S["pool_consts"], 1)
            pool.memset(eps_col[:, :], EPS).then_inc(S["pool_consts"], 1)
            pool.memset(half_neg[:, :], -0.5).then_inc(S["pool_consts"], 1)
            pool.memset(h_act[:, :], 0.0).then_inc(S["pool_consts"], 1)
            pool.memset(ones_e, 1.0).then_inc(S["pool_consts"], 1)
            pool.memset(not_first, 1.0).then_inc(S["pool_consts"], 1)
            pool.memset(expert_of[:, 0:1], 0).then_inc(S["pool_consts"], 1)
            for v, step in ((iota_e[:, :], 1), (iota_tile[:, :], P), (slots, 1)):
                pool.iota(v, pattern=[[step, v.shape[1]]], base=0, channel_multiplier=0,
                          allow_small_or_imprecise_dtypes=True).then_inc(S["pool_consts"], 1)
            pool.wait_ge(S["pool_consts"], CONSTS - 1)
            pool.memset(not_first[:, :, 0:1], 0.0).then_inc(S["pool_consts"], 1)

            pool.wait_ge(S["zero_fill"], 16 * 6)
            pool.wait_ge(S["placed"], 1)
            for i in range(TILES):
                for k in range(2):
                    pool.indirect_dma_start(
                        out=sorted_x, out_offset=bass.IndirectOffsetOnAxis(ap=place[:, i, k:k + 1], axis=0),
                        in_=xn_all[:, i, :], in_offset=None).then_inc(S["scattered"], 16)

            pool.sem_inc(S["dbx_done"], 2)

            def inflow_of(s, k):
                pool.wait_ge(S["B_copied"], s + 1 + 1)
                pool.wait_ge(S["scan_done"], s + 1)
                pool.tensor_tensor(inflow[:, k], dtx, B_rep[:, k].rearrange("p (a t) -> p a t", a=1).to_broadcast([P, KD, CHUNK]),
                                   ALU.mult).then_inc(S["dbx_done"], 1)

            def rstd_of(i):
                pool.wait_ge(S["var_ready"], i + 1)
                pool.tensor_tensor(hve[:, :], hmv[:, 1:2], eps_col[:, :], ALU.add).then_inc(S["ve_h"], 1)
                pool.wait_ge(S["ve_h"], i + 1)
                pool.tensor_tensor(hrs[:, :], hve[:, :], half_neg[:, :], ALU.pow).then_inc(S["rstd_ready"], 1)

            with pool.Fori(0, CHUNKS) as c:
                pool.wait_ge(S["dtx_ready"], c + 1)
                for k in range(2):
                    inflow_of(c * STATE + k, k)
                with pool.Fori(0, PAIRS - 1) as pr:
                    inflow_of(c * STATE + pr * 2 + 2, 0)
                    rstd_of(c * PAIRS + pr)
                    inflow_of(c * STATE + pr * 2 + 3, 1)
                rstd_of(c * PAIRS + PAIRS - 1)
            with pool.Fori(CHUNKS * PAIRS, SORTED) as i:
                rstd_of(i)

            pool.wait_ge(S["y_stored"], 16 * (SORTED + 1) + 16)
            pool.wait_ge(S["mo_stored"], 16 * CHUNKS + 16)
            pool.wait_ge(S["xT_loaded"], 16 * (CHUNKS + 1))
            for u in range(TILES // 2):
                if u >= 2:
                    pool.wait_ge(S[f"e_done{u % 2}"], u // 2 + 1)
                for t in range(2):
                    for k, dst in enumerate((ey1, ey2)):
                        pool.indirect_dma_start(
                            out=dst[u % 2][:, t, :], out_offset=None, in_=sorted_y,
                            in_offset=bass.IndirectOffsetOnAxis(ap=place_y[:, 2 * u + t, k:k + 1], axis=0)
                        ).then_inc(S[f"ey_in{u % 2}"], 16)

        @block.scalar
        def _(act):
            for name in ("mo_copied", "hT_copied", "y_copied", "B_copied"):
                act.sem_inc(S[name], 1)
            for name in ("xT_store0", "xT_store1", "e_store0", "e_store1"):
                act.sem_inc(S[name], 16)
            for dst, src in small_loads:
                act.dma_start(dst, src).then_inc(S["w_small"], 16)

            act.wait_ge(S["pool_consts"], CONSTS)
            with act.Fori(0, TURNS) as j:
                act.wait_ge(S["ve_ready"], j + 1)
                nc.scalar.activation(rstd[:, bass.ds(j * GROUP, GROUP)], mean_var[:, bass.ds(j * GROUP, GROUP), 1],
                                     ACT.Sqrt, bias=eps_col[:, 0:1]).then_inc(S["sqrt_ready"], 1)
                for q in range(GROUP):
                    half, t = q // TPC, q % TPC
                    if t == 0:
                        act.wait_ge(S[f"xT_store{half}"], j * 16 + 16)
                    act.wait_ge(S["tr_ready"], j * GROUP + q + 1 + 1)
                    nc.scalar.activation(stage_T[half][:, :, t, :], psTr[q % 2][:, 0:KD * P].rearrange("p (k t) -> p k t", k=KD),
                                         ACT.Copy).then_inc(S["T_copied"], 1)
                    if t == TPC - 1:
                        act.wait_ge(S["T_copied"], j * GROUP + q + 1)
                        act.dma_start(xnT_d[bass.ds(j * 2 + half, 1)].rearrange("o p n -> p (o n)"),
                                      stage_T[half].rearrange("p k t n -> p (k t n)")).then_inc(S[f"xT_store{half}"], 16)
            act.wait_ge(S["scores_ready"], 1)
            nc.scalar.activation(probs, scratch, ACT.Exp).then_inc(S["exp_ready"], 1)
            act.wait_ge(S["w_small"], W_SMALL)
            nc.scalar.activation(A_sb[:, :, :], A_sb[:, :, :], ACT.Exp).then_inc(S["A_exp"], 1)
            act.wait_ge(S["A_exp"], 1)
            nc.scalar.activation(A_sb[:, :, :], A_sb[:, :, :], ACT.Copy, scale=-1.0).then_inc(S["A_exp"], 1)
            act.wait_ge(S["A_exp"], 2)
            act.sem_inc(S["gelu_done"], 1)

            def decay_of(s, n, k):
                act.wait_ge(S["repB_ready"], s + 1)
                act.wait_ge(S["dbx_done"], s + 1)
                nc.scalar.activation(B_rep[:, k], psB[:, :], ACT.Copy).then_inc(S["B_copied"], 1)
                act.wait_ge(S["scan_done"], s + 1)
                for hd in range(KD):
                    e = nc.scalar.activation(decay[:, k, hd], dt_sb[:, hd], ACT.Exp, scale=A_sb[:, hd, bass.ds(n, 1)])
                e.then_inc(S["exp_done"], 1)

            def copy_xT(i):
                act.wait_ge(S["xin_T"], i + 1 + 1)
                nc.scalar.activation(ffn_xT[:, :, :], psX[:, 0:KD * P].rearrange("p (k t) -> p k t", k=KD), ACT.Copy
                                     ).then_inc(S["xT_copied"], 1)

            def copy_hT(i):
                act.wait_ge(S["hT_done"], i + 1)
                nc.scalar.activation(h_T[:, :, :], psT[:, :].rearrange("p (k t) -> p k t", k=KH), ACT.Copy
                                     ).then_inc(S["hT_copied"], 1)

            def copy_y(i):
                act.wait_ge(S["y_ready"], i + 1)
                act.wait_ge(S["y_stored"], i * 16 + 16)
                nc.scalar.activation(y_out[:, :], psX[:, 0:DIM], ACT.Copy).then_inc(S["y_copied"], 1)

            def gelu(i):
                act.wait_ge(S["ln_done"], i + 1)
                act.wait_ge(S["hT_done"], i + 1)
                nc.scalar.activation(h_act[:, :], h_aff[:, :], ACT.Gelu).then_inc(S["gelu_done"], 1)

            with act.Fori(0, CHUNKS) as c:
                act.wait_ge(S["ssm_ready"], c + 1)
                for hd in range(KD):
                    e = nc.scalar.activation(xpad[:, hd, TAPS - 1:], psY[:, hd * CHUNK:(hd + 1) * CHUNK], ACT.Identity,
                                             bias=b_in_sb[:, hd:hd + 1])
                e.then_inc(S["xpad_ready"], 1)
                act.wait_ge(S["gate_ready"], c + 1)
                for hd in range(KD):
                    e = nc.scalar.activation(gate_silu[:, hd], psC[:, hd * CHUNK:(hd + 1) * CHUNK], ACT.Silu,
                                             bias=b_in_sb[:, KD + hd:KD + hd + 1])
                e.then_inc(S["gate_done"], 1)
                act.wait_ge(S["conv_ready"], c + 1)
                nc.scalar.activation(x_conv, conv_acc, ACT.Silu).then_inc(S["xc_ready"], 1)
                act.wait_ge(S["dt_ready"], c + 1)
                for hd in range(KD):
                    e = nc.scalar.activation(soft_abs[:, hd], psY[:, hd * CHUNK:(hd + 1) * CHUNK], ACT.Abs,
                                             bias=b_dt_sb[:, hd:hd + 1])
                e.then_inc(S["soft_chain"], 1)
                for hd in range(KD):
                    nc.scalar.activation(soft_relu[:, hd], psY[:, hd * CHUNK:(hd + 1) * CHUNK], ACT.Relu,
                                         bias=b_dt_sb[:, hd:hd + 1])
                act.wait_ge(S["soft_chain"], c * 2 + 1)
                nc.scalar.activation(soft_abs, soft_abs, ACT.Exp, scale=-1.0).then_inc(S["soft_chain"], 1)
                act.wait_ge(S["soft_chain"], c * 2 + 2)
                nc.scalar.activation(soft_abs, soft_abs, ACT.Ln, bias=1.0).then_inc(S["soft_ready"], 1)
                act.wait_ge(S["dtx_ready"], c + 1)
                for k in range(2):
                    decay_of(c * STATE + k, k, k)
                with act.Fori(0, PAIRS - 1) as pr:
                    i = c * PAIRS + pr
                    copy_xT(i)
                    copy_hT(i)
                    decay_of(c * STATE + pr * 2 + 2, pr * 2 + 2, 0)
                    copy_y(i)
                    decay_of(c * STATE + pr * 2 + 3, pr * 2 + 3, 1)
                    gelu(i)
                i = c * PAIRS + PAIRS - 1
                copy_xT(i)
                copy_hT(i)
                copy_y(i)
                gelu(i)
                act.wait_ge(S["out_ready"], c + 1)
                act.wait_ge(S["mo_stored"], c * 16 + 16)
                nc.scalar.activation(mo_stage, psC[:, :], ACT.Copy).then_inc(S["mo_copied"], 1)
            with act.Fori(CHUNKS * PAIRS, SORTED) as i:
                copy_xT(i)
                copy_hT(i)
                copy_y(i)
                gelu(i)
            copy_hT(SORTED)
            copy_y(SORTED)

            with act.Fori(0, TILES // 4) as j:
                for q in range(2):
                    act.wait_ge(S["e_var"], j * 2 + q + 1)
                    nc.scalar.activation(ers[q], emv[q][:, :, :, 1], ACT.Sqrt, bias=eps_col[:, 0:1]).then_inc(S["e_sqrt"], 1)
                    act.wait_ge(S[f"e_done{q}"], j + 1 + 1)
                    act.dma_start(out[bass.ds((j * 2 + q) * (2 * P), 2 * P), :].rearrange("(n p) d -> p n d", p=P), eo[q]
                                  ).then_inc(S[f"e_store{q}"], 16)

        @block.tensor
        def _(pe):
            for name, ahead in (("tr_ready", 1), ("xin_T", 1), ("sum_done", 2)):
                pe.sem_inc(S[name], ahead)
            pe.wait_ge(S["pool_consts"], CONSTS)
            pe.wait_ge(S["w_small"], W_SMALL)

            def logits_of(j, q):
                t = j * GROUP + q
                pe.wait_ge(S["T_copied"], t + 1)
                for k in range(KD):
                    m = nc.tensor.matmul(psX[:, bass.ds(t * EXPERTS, EXPERTS)], stage_T[q // TPC][:, k, q % TPC, :],
                                         gate_sb[:, k, :], start=(k == 0), stop=(k == KD - 1))
                m.then_inc(S["logits_done"], 1)

            with pe.Fori(0, TURNS) as j:
                for q in range(GROUP):
                    pe.wait_ge(S["xn_ready"], j * GROUP + q + 1)
                    if q >= 2:
                        pe.wait_ge(S["T_copied"], j * GROUP + q - 1)
                    for k in range(KD):
                        m = nc.tensor.transpose(psTr[q % 2][:, k * P:(k + 1) * P],
                                                xn_turn[:, q, k * P:(k + 1) * P],
                                                ident[:, :])
                    m.then_inc(S["tr_ready"], 1)
                    if q >= 1:
                        logits_of(j, q - 1)
                logits_of(j, GROUP - 1)
            pe.wait_ge(S["chosen_ready"], 1)
            nc.tensor.matmul(psY[:, 0:CHUNK], before[:, :], scratch.rearrange("p t e -> p (t e)"), start=True, stop=True)
            nc.tensor.matmul(psY[:, CHUNK:], ones[:, :], scratch.rearrange("p t e -> p (t e)"), start=True, stop=True
                             ).then_inc(S["counts_ready"], 1)

            pe.wait_ge(S["w_mamba"], W_MAMBA)
            pe.wait_ge(S["w_ffn"], W_FFN)
            pe.wait_ge(S["b_rows_in"], 32)
            pe.wait_ge(S["diag_ready"], KD)

            def transpose_x(i):
                pe.wait_ge(S["xin_loaded"], 16 * (i + 1))
                pe.wait_ge(S["y_copied"], i + 1)
                for k in range(KD):
                    m = nc.tensor.transpose(psX[:, k * P:(k + 1) * P], xin[:, k * P:(k + 1) * P], ident[:, :])
                m.then_inc(S["xin_T"], 1)

            def transpose_h(i):
                pe.wait_ge(S["gelu_done"], i + 1)
                pe.wait_ge(S["hT_copied"], i + 1)
                for k in range(KH):
                    m = nc.tensor.transpose(psT[:, k * P:(k + 1) * P], h_act[:, k * P:(k + 1) * P], ident[:, :])
                m.then_inc(S["hT_done"], 1)

            def up(i):
                e = pe.value_load(expert_of[0:1, bass.ds(i + 1, 1)], min_val=0, max_val=EXPERTS - 1)
                pe.wait_ge(S["xT_copied"], i + 1)
                pe.wait_ge(S["ln_a"], i + 1)
                for k in range(KD):
                    nc.tensor.matmul(psH[:, :], ffn_xT[:, k, :], w1_sb[:, bass.ds(e, 1), k, :].rearrange("p o h -> p (o h)"),
                                     start=(k == 0), stop=False)
                nc.tensor.matmul(psH[:, :], ones_bf[:, :], b1_rows[:, bass.ds(e, 1), :].rearrange("p o h -> p (o h)"),
                                 start=False, stop=True).then_inc(S["h_ready"], 1)

            def down(i):
                e = pe.value_load(expert_of[0:1, bass.ds(i, 1)], min_val=0, max_val=EXPERTS - 1)
                pe.wait_ge(S["hT_copied"], i + 1 + 1)
                for k in range(KH):
                    nc.tensor.matmul(psX[:, 0:DIM], h_T[:, k, :], w2_sb[:, bass.ds(e, 1), k, :].rearrange("p o d -> p (o d)"),
                                     start=(k == 0), stop=False)
                nc.tensor.matmul(psX[:, 0:DIM], ones_bf[:, :], b2_rows[:, bass.ds(e, 1), :].rearrange("p o d -> p (o d)"),
                                 start=False, stop=True).then_inc(S["y_ready"], 1)

            def spread(s, n, k):
                pe.wait_ge(S["B_copied"], s + 1)
                nc.tensor.matmul(psB[:, :], pick[:, bass.ds(n, 1), :].rearrange("p o m -> p (o m)"), bc_parts,
                                 start=True, stop=True).then_inc(S["repB_ready"], 1)
                pe.wait_ge(S["hC_done"], s + 1)
                nc.tensor.matmul(psC[:, k * CHUNK:(k + 1) * CHUNK],
                                 pick[:, bass.ds(n + STATE, 1), :].rearrange("p o m -> p (o m)"), bc_parts,
                                 start=True, stop=True).then_inc(S["repC_ready"], 1)

            def add_up(s, k):
                pe.wait_ge(S["hC_done"], s + 2 + 1)
                for hd in range(KD):
                    m = nc.tensor.matmul(psY[:, hd * CHUNK:(hd + 1) * CHUNK], ident[:, :], hC[:, k, hd],
                                         start=False, stop=True, skip_group_check=True)
                m.then_inc(S["sum_done"], 1)

            with pe.Fori(0, CHUNKS) as c:
                pe.wait_ge(S["xT_loaded"], 16 * (c + 1))
                pe.wait_ge(S["y_gated"], c + 1)
                pe.wait_ge(S["mo_copied"], c + 1)
                for m4 in range(2 * KD):
                    dst = (psY if m4 < KD else psC)[:, (m4 % KD) * CHUNK:(m4 % KD + 1) * CHUNK]
                    for k in range(KD):
                        m = nc.tensor.matmul(dst, W_in_sb[:, k, m4 * P:(m4 + 1) * P], xT_in[:, k], start=(k == 0), stop=(k == KD - 1))
                    if m4 == KD - 1:
                        m.then_inc(S["ssm_ready"], 1)
                m.then_inc(S["gate_ready"], 1)
                pe.wait_ge(S["xc_ready"], c + 1)
                for k in range(KD):
                    m = nc.tensor.matmul(psB[0:PARTS * BC, :], W_bc_sb[:, k, :, :].rearrange("p r n -> p (r n)"), x_conv[:, k],
                                         start=(k == 0), stop=(k == KD - 1))
                m.then_inc(S["bc_ready"], 1)
                for hd in range(KD):
                    for k in range(KD):
                        m = nc.tensor.matmul(psY[:, hd * CHUNK:(hd + 1) * CHUNK], W_dt_sb[:, k, hd * P:(hd + 1) * P], x_conv[:, k],
                                             start=(k == 0), stop=(k == KD - 1))
                m.then_inc(S["dt_ready"], 1)
                pe.wait_ge(S["bcp_ready"], c + 1)
                for k in range(2):
                    spread(c * STATE + k, k, k)
                pe.wait_ge(S["soft_ready"], c + 1)
                for hd in range(KD):
                    nc.tensor.matmul(psY[:, hd * CHUNK:(hd + 1) * CHUNK], diagD[:, hd, :], x_conv[:, hd], start=True, stop=True)
                with pe.Fori(0, PAIRS - 1) as pr:
                    i = c * PAIRS + pr
                    s = c * STATE + pr * 2
                    transpose_x(i)
                    transpose_h(i)
                    up(i)
                    add_up(s, 0)
                    spread(s + 2, pr * 2 + 2, 0)
                    down(i)
                    add_up(s + 1, 1)
                    spread(s + 3, pr * 2 + 3, 1)
                i = c * PAIRS + PAIRS - 1
                s = c * STATE + STATE - 2
                transpose_x(i)
                transpose_h(i)
                up(i)
                add_up(s, 0)
                down(i)
                add_up(s + 1, 1)
                pe.wait_ge(S["y_gated"], c + 1 + 1)
                for q in range(TPC):
                    for k in range(KD):
                        m = nc.tensor.matmul(psC[:, q * DIM:(q + 1) * DIM], gated[:, k, q * P:(q + 1) * P], W_out_sb[:, k, :],
                                             start=(k == 0), stop=(k == KD - 1))
                m.then_inc(S["out_ready"], 1)
            with pe.Fori(CHUNKS * PAIRS, SORTED) as i:
                transpose_x(i)
                transpose_h(i)
                up(i)
                down(i)
            transpose_h(SORTED)
            down(SORTED)

        @block.vector
        def _(dve):
            V = nc.vector
            chain = Chain(dve, S["dve_chain"])
            one = lambda v, shape: v.to_broadcast(shape)

            def hold():
                V.memset(held[:, :], 0.0)

            for name, ahead in (("y_gated", 1), ("ln_a", 1), ("scan_done", 2), ("hC_done", 2), ("e_done0", 1), ("e_done1", 1)):
                dve.sem_inc(S[name], ahead)

            dve.wait_ge(S["biases_in"], 32)
            for r in range(PARTS):
                V.tensor_copy(bsplit_bf[:, r, :], bsplit[:, :]).then_inc(S["b_split"], 1)
                dve.wait_ge(S["b_split"], 2 * r + 1)
                if r < PARTS - 1:
                    V.tensor_tensor(bsplit[:, :], bsplit[:, :], bsplit_bf[:, r, :], ALU.subtract).then_inc(S["b_split"], 1)
                    dve.wait_ge(S["b_split"], 2 * r + 2)

            with dve.Fori(0, TURNS) as j:
                with chain.turn(j, TURNS, 2 * GROUP + 1):
                    dve.wait_ge(S["x_in"], 16 * (j + 1) + 16)
                    for q in range(GROUP):
                        chain.mark(V.bn_stats(stats[:, q, :], xn_all[:, bass.ds(j * GROUP + q, 1), :].rearrange("p o d -> p (o d)")))
                    chain.wait()
                    hold()
                    for q in range(GROUP):
                        chain.mark(V.bn_aggr(turn_mv[:, q, :], stats[:, q, :]))
                    chain.wait()
                    V.tensor_copy(mean_var[:, bass.ds(j * GROUP, GROUP), :], turn_mv[:, :, :]).then_inc(S["ve_ready"], 1)
                    dve.wait_ge(S["sqrt_ready"], j + 1)
                    r8 = rstd[:, bass.ds(j * GROUP, GROUP)]
                    chain.mark(V.reciprocal(r8, r8))
                    chain.wait()
                    for q in range(GROUP):
                        t = bass.ds(j * GROUP + q, 1)
                        v = xn_all[:, t, :].rearrange("p o d -> p (o d)")
                        if q == 0:
                            dve.wait_ge(S["tr_ready"], j * GROUP + 1)
                        V.tensor_scalar(xn_turn[:, q, :], v, mean_var[:, t, 0], rstd[:, t], ALU.subtract, ALU.mult
                                        ).then_inc(S["xn_ready"], 1)
                    for q in range(GROUP):
                        t = bass.ds(j * GROUP + q, 1)
                        v = xn_all[:, t, :].rearrange("p o d -> p (o d)")
                        V.tensor_scalar(v, v, mean_var[:, t, 0], rstd[:, t], ALU.subtract, ALU.mult)

            def step(ins):
                chain.mark(ins)
                chain.wait()

            big = [P, TILES, EXPERTS]
            per_tile = lambda v: v[:, :].rearrange("p (t o) -> p t o", o=1).to_broadcast(big)
            per_expert = lambda v: v[:, :].rearrange("p (o e) -> p o e", o=1).to_broadcast(big)
            dve.wait_ge(S["logits_done"], TILES)
            dve.wait_ge(S["pool_consts"], CONSTS)
            step(V.tensor_copy(logits.rearrange("p t e -> p (t e)"), psX[:, :]))
            step(V.tensor_reduce(t1[:, :], logits, AX.X, ALU.max))
            V.tensor_tensor(scratch, logits, per_tile(t1), ALU.subtract).then_inc(S["scores_ready"], 1)
            dve.wait_ge(S["exp_ready"], 1)
            step(V.tensor_reduce(t1[:, :], probs, AX.X, ALU.add))
            step(V.reciprocal(t1[:, :], t1[:, :]))
            step(V.tensor_tensor(probs, probs, per_tile(t1), ALU.mult))

            def choose(top, best):
                step(V.tensor_reduce(best[:, :], probs, AX.X, ALU.max))
                step(V.tensor_tensor(scratch, probs, per_tile(best), ALU.is_ge))
                step(V.tensor_scalar(scratch, scratch, -float(EXPERTS), None, ALU.mult))
                step(V.tensor_tensor(scratch, scratch, per_expert(iota_e), ALU.add))
                step(V.tensor_reduce(t3[:, :], scratch, AX.X, ALU.min))
                step(V.tensor_tensor(top, scratch, per_tile(t3), ALU.is_equal))

            choose(top1, t1)
            step(V.tensor_scalar(scratch, top1, -2.0, None, ALU.mult))
            step(V.tensor_tensor(probs, probs, scratch, ALU.add))
            choose(top2, t2)
            V.tensor_tensor(scratch, top1, top2, ALU.add).then_inc(S["chosen_ready"], 1)
            step(V.tensor_tensor(t3[:, :], t1[:, :], t2[:, :], ALU.add))
            step(V.reciprocal(t3[:, :], t3[:, :]))
            step(V.tensor_tensor(weight[:, :, 0], t1[:, :], t3[:, :], ALU.mult))
            step(V.tensor_tensor(weight[:, :, 1], t2[:, :], t3[:, :], ALU.mult))
            dve.wait_ge(S["counts_ready"], 1)
            by_expert = lambda v: v.rearrange("p t e -> p (t e)").rearrange("p (e t) -> p e t", e=EXPERTS)
            count, upto = by_expert(probs), by_expert(logits)
            step(V.tensor_copy(count, psY[:, CHUNK:].rearrange("p (t e) -> p e t", e=EXPERTS)))
            step(V.tensor_tensor_scan(upto.rearrange("p e t -> p (e t)"), not_first.rearrange("p e t -> p (e t)"),
                                      count.rearrange("p e t -> p (e t)"), 0.0, ALU.mult, ALU.add))
            cmp = by_expert(scratch)
            step(V.tensor_tensor(cmp, upto[:, :, TILES - 1:TILES].to_broadcast([P, EXPERTS, TILES]),
                                 iota_tile[:, :].rearrange("p (o t) -> p o t", o=1).to_broadcast([P, EXPERTS, TILES]), ALU.is_gt))
            step(V.tensor_reduce(tiles_of[:, :], cmp, AX.X, ALU.add))
            step(V.tensor_tensor_scan(tiles_end[:, :], ones_e, tiles_of[:, :], 0.0, ALU.mult, ALU.add))
            step(V.tensor_tensor(rows_start[:, :], tiles_end[:, :], tiles_of[:, :], ALU.subtract))
            step(V.tensor_scalar(rows_start[:, :], rows_start[:, :], float(P), None, ALU.mult))
            step(V.tensor_tensor(upto, upto, count, ALU.subtract))
            step(V.tensor_tensor(upto, upto, rows_start[:, :].rearrange("p (e o) -> p e o", o=1).to_broadcast([P, EXPERTS, TILES]), ALU.add))
            step(V.tensor_tensor(probs, psY[:, 0:CHUNK].rearrange("p (t e) -> p t e", e=EXPERTS),
                                 upto.rearrange("p e t -> p t e"), ALU.add))
            for k, top in enumerate((top1, top2)):
                step(V.tensor_tensor(scratch, probs, top, ALU.mult))
                step(V.tensor_reduce(place_f[:, :, k], scratch, AX.X, ALU.add))
            step(V.tensor_copy(place[:, :, :], place_f[:, :, :]))
            step(V.tensor_scalar(place_f[:, :, :], place_f[:, :, :], float(P), None, ALU.add))
            step(V.tensor_copy(place_y[:, :, :], place_f[:, :, :]))
            shape = [1, SORTED, EXPERTS]
            step(V.tensor_tensor(slot_cmp[0:1], slots[0:1, :].rearrange("p (t o) -> p t o", o=1).to_broadcast(shape),
                                 tiles_end[0:1, :].rearrange("p (o e) -> p o e", o=1).to_broadcast(shape), ALU.is_ge))
            step(V.tensor_reduce(slots[0:1, :], slot_cmp[0:1], AX.X, ALU.add))
            step(V.tensor_scalar(slots[0:1, :], slots[0:1, :], float(EXPERTS - 1), None, ALU.min))
            V.tensor_copy(expert_of[:, 1:], slots[0:1, :]).then_inc(S["placed"], 1)
            dve.wait_ge(S["w_small"], W_SMALL)
            for hd in range(KD):
                V.tensor_scalar(diagD[:, hd, :], ident[:, :], D_sb[:, hd:hd + 1], None, ALU.mult).then_inc(S["diag_ready"], 1)

            dve.wait_ge(S["scattered"], 16 * 2 * TILES)
            step(V.memset(xpad[:, :, 0:TAPS - 1], 0.0))
            conv = Chain(dve, chain.sem)
            conv.base, conv.n = chain.base, chain.n
            PER_CHUNK = KD * TAPS - 1 + 6

            def scan_step(s, n, k):
                dve.wait_ge(S["exp_done"], s + 1)
                dve.wait_ge(S["dbx_done"], s + 2 + 1)
                for hd in range(KD):
                    a = V.tensor_tensor_scan(h_sb[:, k, hd], decay[:, k, hd], inflow[:, k, hd], h_last[:, hd, bass.ds(n, 1)],
                                             ALU.mult, ALU.add)
                a.then_inc(S["scan_done"], 1)

            def times_C(s, n, k):
                dve.wait_ge(S["scan_done"], s + 2 + 1)
                V.tensor_scalar(h_last[:, :, bass.ds(n, 1)], h_sb[:, k, :, CHUNK - 1:], 1.0, None, ALU.mult)
                dve.wait_ge(S["repC_ready"], s + 1)
                dve.wait_ge(S["sum_done"], s + 1)
                V.tensor_tensor(hC[:, k], h_sb[:, k], psC[:, k * CHUNK:(k + 1) * CHUNK].rearrange("p (a t) -> p a t", a=1)
                                .to_broadcast([P, KD, CHUNK]), ALU.mult).then_inc(S["hC_done"], 1)

            def hidden_stats(i):
                dve.wait_ge(S["h_ready"], i + 1)
                V.bn_stats(hstats[:, :], psH[:, :]).then_inc(S["bn_done"], 1)
                dve.wait_ge(S["bn_done"], i + 1)
                hold()
                V.bn_aggr(hmv[:, :], hstats[:, :]).then_inc(S["var_ready"], 1)

            def hidden_norm(i):
                e = dve.value_load(expert_of[0:1, bass.ds(i + 1, 1)], min_val=0, max_val=EXPERTS - 1)
                dve.wait_ge(S["var_ready"], i + 1)
                V.scalar_tensor_tensor(h_norm[:, :], psH[:, :], hmv[:, 0:1], g1_rep[:, bass.ds(e, 1), :].rearrange("p o h -> p (o h)"),
                                       ALU.subtract, ALU.mult).then_inc(S["ln_a"], 1)
                dve.wait_ge(S["rstd_ready"], i + 1)
                dve.wait_ge(S["ln_a"], i + 1 + 1)
                dve.wait_ge(S["gelu_done"], i + 1)
                V.scalar_tensor_tensor(h_aff[:, :], h_norm[:, :], hrs[:, 0:1], be1_rep[:, bass.ds(e, 1), :].rearrange("p o h -> p (o h)"),
                                       ALU.mult, ALU.add).then_inc(S["ln_done"], 1)

            with dve.Fori(0, BATCH) as b:
                with conv.turn(b, BATCH, 2 * PER_CHUNK + 3):
                    for half in range(2):
                        c = b * 2 + half
                        dve.wait_ge(S["xpad_ready"], c + 1)
                        for t in range(TAPS):
                            for hd in range(KD):
                                src, w = xpad[:, hd, t:t + CHUNK], conv_w_sb[:, hd, t:t + 1]
                                if t == 0:
                                    a = V.tensor_scalar(conv_acc[:, hd], src, w, conv_b_sb[:, hd:hd + 1], ALU.mult, ALU.add)
                                else:
                                    a = V.scalar_tensor_tensor(conv_acc[:, hd], src, w, conv_acc[:, hd], ALU.mult, ALU.add)
                                if t == TAPS - 1 and hd == KD - 1:
                                    a.then_inc(S["conv_ready"], 1)
                                else:
                                    conv.mark(a)
                            if t < TAPS - 1:
                                conv.wait()
                        if half == 0:
                            conv.mark(V.tensor_copy(xpad[:, :, 0:TAPS - 1], xpad[:, :, CHUNK:]))
                            conv.mark(V.memset(h_last[:, :, :], 0.0))
                        else:
                            conv.mark(V.memset(xpad[:, :, 0:TAPS - 1], 0.0))
                        dve.wait_ge(S["bc_ready"], c + 1)
                        conv.mark(V.tensor_scalar(bc_f, psB[0:PARTS * BC, :], b_bc_sb[:, 0:1], None, ALU.add))
                        conv.wait()
                        conv.mark(V.tensor_copy(bc_parts, bc_f))
                        conv.wait()
                        conv.mark(V.tensor_tensor(bc_f, bc_f, bc_parts, ALU.subtract))
                        conv.wait()
                        conv.mark(V.tensor_copy(bc_mid, bc_f))
                        conv.wait()
                        conv.mark(V.tensor_copy(bc_parts[BC:2 * BC, :], bc_mid[BC:2 * BC, :]))
                        V.tensor_tensor(bc_parts[2 * BC:, :], bc_f[2 * BC:, :], bc_mid[2 * BC:, :], ALU.subtract).then_inc(S["bcp_ready"], 1)
                        dve.wait_ge(S["mo_stored"], 16 * c + 16)
                        dve.wait_ge(S["soft_ready"], c + 1)
                        conv.mark(V.tensor_tensor(dt_sb, soft_abs, soft_relu, ALU.add))
                        conv.wait()
                        V.tensor_tensor(dtx, dt_sb, x_conv, ALU.mult).then_inc(S["dtx_ready"], 1)
                        with dve.Fori(0, PAIRS) as pr:
                            s = c * STATE + pr * 2
                            i = c * PAIRS + pr
                            scan_step(s, pr * 2, 0)
                            times_C(s, pr * 2, 0)
                            hidden_stats(i)
                            scan_step(s + 1, pr * 2 + 1, 1)
                            hidden_norm(i)
                            times_C(s + 1, pr * 2 + 1, 1)
                        dve.wait_ge(S["sum_done"], (c + 1) * STATE + 1 + 1)
                        V.tensor_tensor(gated.rearrange("p a b -> p (a b)"), psY[:, :], gate_silu.rearrange("p a b -> p (a b)"),
                                        ALU.mult).then_inc(S["y_gated"], 1)
            with dve.Fori(CHUNKS * PAIRS, SORTED) as i:
                hidden_stats(i)
                hidden_norm(i)

            dve.wait_ge(S["w_end"], 16 * len(end_loads))
            e_chain = Chain(dve, S["e_chain"])
            e_chain.mark(V.tensor_tensor(e_b0, e_b0, e_b1, ALU.add))
            two = lambda v: v.rearrange("p (o d) -> p o d", o=1).to_broadcast([P, 2, DIM])
            PER_PAIR = 16
            with dve.Fori(0, TILES // 4) as j:
                with e_chain.turn(j, TILES // 4, 2 * PER_PAIR):
                    for q in range(2):
                        tile = j * 4 + q * 2
                        dve.wait_ge(S[f"ex_in{q}"], 32 * (j + 1))
                        e_chain.wait()
                        for t in range(2):
                            at = bass.ds(tile + t, 1)
                            e_chain.mark(V.tensor_scalar(exn[q][:, t, :], ex[q][:, t, :], mean_var[:, at, 0], rstd[:, at],
                                                         ALU.subtract, ALU.mult))
                        e_chain.mark(V.tensor_tensor(er0[q], emo[q], two(e_bout), ALU.add))
                        e_chain.wait()
                        e_chain.mark(V.tensor_tensor(er0[q], er0[q], exn[q], ALU.add))
                        dve.wait_ge(S[f"ey_in{q}"], 64 * (j + 1))
                        for t in range(2):
                            wt = weight[:, bass.ds(tile + t, 1), 0]
                            e_chain.mark(V.scalar_tensor_tensor(er1[q][:, t, :], ey1[q][:, t, :], wt, exn[q][:, t, :], ALU.mult, ALU.add))
                        e_chain.wait()
                        for t in range(2):
                            wt = weight[:, bass.ds(tile + t, 1), 1]
                            e_chain.mark(V.scalar_tensor_tensor(er1[q][:, t, :], ey2[q][:, t, :], wt, er1[q][:, t, :], ALU.mult, ALU.add))
                        e_chain.wait()
                        for t in range(2):
                            for l, v in enumerate((er0, er1)):
                                e_chain.mark(V.bn_stats(estats[q][:, t, l, :], v[q][:, t, :]))
                        e_chain.wait()
                        hold()
                        for t in range(2):
                            for l in range(2):
                                a = V.bn_aggr(emv[q][:, t, l, :], estats[q][:, t, l, :])
                        a.then_inc(S["e_var"], 1)
                        dve.wait_ge(S["e_sqrt"], j * 2 + q + 1)
                        e_chain.mark(V.reciprocal(ers[q], ers[q]))
                        for t in range(2):
                            for l, (v, g) in enumerate(((er0, e_g0), (er1, e_g1))):
                                a = V.scalar_tensor_tensor(v[q][:, t, :], v[q][:, t, :], emv[q][:, t, l, 0:1], g, ALU.subtract, ALU.mult)
                        e_chain.mark(a)
                        e_chain.wait()
                        for t in range(2):
                            V.scalar_tensor_tensor(er0[q][:, t, :], er0[q][:, t, :], ers[q][:, t, 0:1], ex[q][:, t, :], ALU.mult, ALU.add)
                            e_chain.mark(V.scalar_tensor_tensor(er1[q][:, t, :], er1[q][:, t, :], ers[q][:, t, 1:2], e_b0, ALU.mult, ALU.add))
                        e_chain.wait()
                        dve.wait_ge(S[f"e_store{q}"], 16 * j + 16)
                        V.tensor_tensor(eo[q], er0[q], er1[q], ALU.add).then_inc(S[f"e_done{q}"], 1)


_INS = ['L0_attn_x', 'L0_attn_W_in', 'L0_attn_b_in', 'L0_attn_conv_w', 'L0_attn_conv_b', 'L0_attn_W_bc', 'L0_attn_b_bc',
        'L0_attn_W_dt', 'L0_attn_b_dt', 'L0_attn_A_log', 'L0_attn_D', 'L0_attn_W_out', 'L0_attn_b_out', 'L0_attn_ln_g',
        'L0_attn_ln_b', 'L0_ffn_gate_w', 'L0_ffn_w1', 'L0_ffn_b1', 'L0_ffn_ln1_g', 'L0_ffn_ln1_b', 'L0_ffn_w2',
        'L0_ffn_b2', 'L0_ffn_ln_g', 'L0_ffn_ln_b']


def kernel(**inputs):
    import numpy as _np
    import concourse.bacc as _bacc
    from concourse import mybir as _mybir
    from concourse.bass_utils import run_bass_kernel_spmd as _run

    nc = _bacc.Bacc("TRN2", target_bir_lowering=False, num_devices=1)
    arrays, args = {}, []
    for name in _INS:
        a = _np.ascontiguousarray(inputs[name])
        arrays[name] = a
        args.append(nc.dram_tensor(name, a.shape, _mybir.dt.from_np(a.dtype), kind="ExternalInput").ap())
    args.append(nc.dram_tensor("out", (BATCH, SEQ, DIM), F32, kind="ExternalOutput").ap())
    build_program(nc, *args)
    r = _run(nc, [arrays], core_ids=[0])
    return r.results[0]["out"]
```

```python
import numpy as np
import concourse.bass as bass
from concourse import mybir
from contextlib import ExitStack, contextmanager

ALU = mybir.AluOpType
ACT = mybir.ActivationFunctionType
AX = mybir.AxisListType
F32 = mybir.dt.float32
BF16 = mybir.dt.bfloat16
I32 = mybir.dt.int32

BATCH, SEQ, DIM, STATE, TAPS = 8, 1024, 256, 16, 4
EXPERTS, HIDDEN = 8, 512
P = 128
EPS = 1e-5
KD = DIM // P
KH = HIDDEN // P
TOKENS = BATCH * SEQ
TILES = TOKENS // P
CHUNK = 512
TPC = CHUNK // P
CHUNKS = TOKENS // CHUNK
PAIRS = STATE // 2
SORTED = 2 * TILES + EXPERTS
LAG = 2
FFN_TURNS = SORTED + LAG
MAMBA_TURNS = CHUNKS * PAIRS
LOADED = FFN_TURNS + 2
GROUP = 8
TURNS = TILES // GROUP
PARTS = 3
BC = 2 * STATE
TASKS = ["ssm0", "ssm1", "gate0", "bc", "dt0", "dt1", "gate1", None]
CONV_TURN = TASKS.index("ssm1") + 1
DT_TAKEN = TASKS.index("dt1") + 1
CONSTS = 21


class Chain:

    def __init__(self, eng, sem):
        self.eng, self.sem, self.base, self.n = eng, sem, 0, 0

    def mark(self, ins):
        ins.then_inc(self.sem, 1)
        self.n += 1

    def wait(self):
        self.eng.wait_ge(self.sem, self.base + self.n)

    @contextmanager
    def turn(self, i, turns, per_turn):
        base, n = self.base, self.n
        self.base, self.n = base + n + i * per_turn, 0
        yield
        assert self.n == per_turn, (self.n, per_turn)
        self.base, self.n = base, n + turns * per_turn


def build_program(nc, x, W_in, b_in, conv_w, conv_b, W_bc, b_bc, W_dt, b_dt, A_log, D_skip, W_out, b_out,
                  ln_g, ln_b, gate_w, w1, b1, ln1_g, ln1_b, w2, b2, fln_g, fln_b, out):
    x = x.rearrange("b t d -> (b t) d")
    out = out.rearrange("b t d -> (b t) d")
    xnT_d = nc.dram_tensor("xnT_d", [CHUNKS + 2, P, KD * CHUNK], F32).ap()
    sorted_x = nc.dram_tensor("sorted_x", [LOADED * P, DIM], F32).ap()
    sorted_y = nc.dram_tensor("sorted_y", [FFN_TURNS * P, DIM], F32).ap()
    mamba_d = nc.dram_tensor("mamba_d", [TOKENS + CHUNK, DIM], F32).ap()
    b1_parts_d = nc.dram_tensor("b1_parts_d", [PARTS, EXPERTS * HIDDEN], BF16).ap()
    b2_parts_d = nc.dram_tensor("b2_parts_d", [PARTS, EXPERTS * DIM], BF16).ap()

    ctx = ExitStack()
    with ctx:
        def sb(name, shape, dt=F32):
            return ctx.enter_context(nc.sbuf_tensor(name, shape, dt))

        def pb(name, shape):
            return ctx.enter_context(nc.psum_tensor(name, shape, F32))

        def sem(name):
            return ctx.enter_context(nc.semaphore(name))

        w1_sb = sb("w1_sb", [P, EXPERTS, KD, HIDDEN])
        w2_sb = sb("w2_sb", [P, EXPERTS, KH, DIM])
        g1_T = sb("g1_T", [P, EXPERTS * KH])
        be1_T = sb("be1_T", [P, EXPERTS * KH])
        b1_rows = sb("b1_rows", [PARTS, EXPERTS, HIDDEN], BF16)
        b2_rows = sb("b2_rows", [PARTS, EXPERTS, DIM], BF16)
        gate_sb = sb("gate_sb", [P, KD, EXPERTS])
        W_in_sb = sb("W_in_sb", [P, KD, 2 * DIM])
        W_dt_sb = sb("W_dt_sb", [P, KD, DIM])
        W_out_sb = sb("W_out_sb", [P, KD, DIM])
        W_bc_sb = sb("W_bc_sb", [P, KD, PARTS, BC])
        b_in_sb = sb("b_in_sb", [P, 2 * KD])
        conv_w_sb = sb("conv_w_sb", [P, KD, TAPS])
        conv_b_sb = sb("conv_b_sb", [P, KD])
        b_dt_sb = sb("b_dt_sb", [P, KD])
        b_bc_sb = sb("b_bc_sb", [PARTS * BC, 1])
        A_sb = sb("A_sb", [P, KD, STATE])
        D_sb = sb("D_sb", [P, KD])
        diagD = sb("diagD", [P, KD, P])
        ident = sb("ident", [P, P])
        before = sb("before", [P, P])
        ones = sb("ones", [P, P])
        ones_bf = sb("ones_bf", [PARTS, P], BF16)
        pick = sb("pick", [PARTS * BC, BC, P], BF16)
        eps_col = sb("eps_col", [P, 1])
        half_neg = sb("half_neg", [P, 1])
        mean_var = sb("mean_var", [P, TILES, 2])
        rstd = sb("rstd", [P, TILES])
        weight = sb("weight", [P, TILES, 2])
        place = sb("place", [P, TILES, 2], I32)
        place_y = sb("place_y", [P, TILES, 2], I32)
        expert_of = sb("expert_of", [1, LOADED + LAG], I32)

        class Carve:

            def __init__(self, tensor, size):
                self.tensor, self.size, self.at = tensor, size, 0

            def take(self, *shape):
                n = int(np.prod(shape))
                v = self.tensor[:, self.at:self.at + n]
                self.at += n
                assert self.at <= self.size, (self.at, self.size)
                if len(shape) == 2:
                    return v.rearrange("p (a b) -> p a b", a=shape[0])
                if len(shape) == 3:
                    return v.rearrange("p (a b c) -> p a b c", a=shape[0], b=shape[1])
                return v

        area = sb("area", [P, TILES * DIM])
        xn_all = area[:, :].rearrange("p (n d) -> p n d", d=DIM)
        scan_area = Carve(area, TILES * DIM)
        decay = scan_area.take(2, KD, CHUNK)
        inflow = scan_area.take(2, KD, CHUNK)
        h_sb = scan_area.take(4, KD, CHUNK)
        xT_in = scan_area.take(KD, CHUNK)
        gate_silu = [scan_area.take(KD, CHUNK) for _ in range(2)]
        dt_sb = [scan_area.take(KD, CHUNK) for _ in range(2)]
        x_conv = scan_area.take(KD, CHUNK)
        dtx = scan_area.take(KD, CHUNK)
        scan_more = Carve(sb("more", [P, 5800]), 5800)
        B_rep = scan_more.take(2, CHUNK)
        xpad = scan_more.take(KD, TAPS - 1 + CHUNK)
        mid = scan_more.take(KD, CHUNK)
        gated = scan_more.take(KD, CHUNK)
        bc_f = scan_more.take(CHUNK)[0:PARTS * BC, :]
        bc_parts = [scan_more.take(CHUNK // 2)[0:PARTS * BC, :].bitcast(BF16) for _ in range(2)]
        bc_mid = scan_more.take(CHUNK // 2)[0:PARTS * BC, :].bitcast(BF16)
        mo_stage = sb("mo_stage", [P, KD * CHUNK])
        pair_sum = sb("pair_sum", [P, KD, CHUNK])
        end_area = Carve(area, TILES * DIM)
        ex, emo, ey1, ey2, exn, er0, er1, eo = ([end_area.take(2, DIM) for _ in range(2)] for _ in range(8))
        e_g0, e_g1, e_bout, e_b0, e_b1 = (end_area.take(DIM) for _ in range(5))
        estats = [end_area.take(2, 2, 6) for _ in range(2)]
        emv = [end_area.take(2, 2, 2) for _ in range(2)]
        ers = [end_area.take(2, 2) for _ in range(2)]
        early = Carve(w1_sb[:, :, :, :].rearrange("p e k h -> p (e k h)"), EXPERTS * KD * HIDDEN)
        stage_T = [early.take(KD, TPC, P) for _ in range(2)]
        ring = Carve(w2_sb[:, :, :, :].rearrange("p e k d -> p (e k d)"), EXPERTS * KH * DIM)
        xn_turn = ring.take(GROUP, DIM)
        logits, probs, top1, top2, scratch = (early.take(TILES, EXPERTS) for _ in range(5))
        not_first = early.take(EXPERTS, TILES)
        slot_cmp = early.take(LOADED, EXPERTS)
        slots = early.take(LOADED)
        ones_e = early.take(EXPERTS)
        bsplit = early.take(48)
        bsplit_bf = early.take(PARTS * 48 // 2).bitcast(BF16).rearrange("p (r n) -> p r n", r=PARTS)
        iota_e, iota_tile = early.take(EXPERTS), early.take(TILES)
        t1, t2, t3 = (early.take(TILES) for _ in range(3))
        place_f = early.take(TILES, 2)
        h_last = sb("h_last", [P, KD, STATE])
        xin = sb("xin", [P, DIM])
        ffn_xT = sb("ffn_xT", [P, KD, P])
        h_norm = sb("h_norm", [P, HIDDEN])
        h_T = sb("h_T", [P, KH, P])
        y_out = sb("y_out", [P, DIM])
        stats = sb("stats", [P, GROUP, 6])
        turn_mv = sb("turn_mv", [P, GROUP, 2])
        hstats = sb("hstats", [P, 6])
        hmv = sb("hmv", [P, 2])
        hve = sb("hve", [P, 1])
        held = sb("held", [P, 1])
        hrs = sb("hrs", [P, 1])
        tiles_of, tiles_end, rows_start = (sb(f"te{i}", [P, EXPERTS]) for i in range(3))

        psY = pb("psY", [P, KD * CHUNK])
        psC = pb("psC", [P, 2 * CHUNK])
        psB = pb("psB", [P, CHUNK])
        psH = pb("psH", [P, HIDDEN])
        psT = pb("psT", [P, HIDDEN])
        psX = pb("psX", [P, HIDDEN])
        psTr = [psH, psT]

        names = """gate_zero w_small w_mamba w_ffn w_end biases_in b_split b_split_out b_rows_in consts_pool zeros_ready
            zero_fill x_in ve_ready sqrt_ready xn_ready tr_ready T_copied logits_done xT_store0 xT_store1
            scores_ready exp_ready chosen_ready counts_ready placed scattered dve_chain A_exp diag_ready
            xT_loaded ssm_ready gate_ready xpad_free xpad_ready gate_raw gate_done conv_ready xc_ready bc_ready
            bc_taken dt_ready bcp_ready soft_taken soft_exp soft_ready dtx_ready seed_done repB_ready repC_ready
            B_copied exp_done dbx_done scan_done hC_done pair_ready sum_done y_gated out_ready mo_copied mo_stored
            xin_loaded xin_T xT_copied h_ready bn_done var_ready ve_h rstd_ready norm_done hT_done gelu_done
            y_ready y_copied y_stored pool_consts
            ex_in0 ex_in1 ey_in0 ey_in1 e_chain e_var e_sqrt e_done0 e_done1 e_store0 e_store1""".split()
        S = {n: sem(n) for n in names}
        block = ctx.enter_context(nc.Block())

        def column(v, k):
            return v.rearrange("(k p o) -> k p o", p=P, o=1)[k]

        def everywhere(v):
            return v.rearrange("(a n) -> a n", a=1).to_broadcast([P, v.shape[0]])

        small_loads = [
            (gate_sb[:, :, :], gate_w.rearrange("(k p) e -> p k e", p=P)),
            (A_sb[:, :, :], A_log.rearrange("(k p) n -> p k n", p=P)),
            (conv_w_sb[:, :, :], conv_w.rearrange("(k p) o t -> p k (o t)", p=P)),
        ]
        for dst, src, n in ((b_in_sb, b_in, 2 * KD), (conv_b_sb, conv_b, KD), (b_dt_sb, b_dt, KD), (D_sb, D_skip, KD)):
            small_loads += [(dst[:, k:k + 1], column(src, k)) for k in range(n)]
        small_loads += [(b_bc_sb[r * BC:(r + 1) * BC, :], b_bc.rearrange("(p o) -> p o", o=1)) for r in range(PARTS)]
        mamba_loads = [
            (W_in_sb[:, :, :], W_in.rearrange("(k p) n -> p k n", p=P)),
            (W_dt_sb[:, :, :], W_dt.rearrange("(k p) n -> p k n", p=P)),
            (W_out_sb[:, :, :], W_out.rearrange("(k p) n -> p k n", p=P)),
        ] + [(W_bc_sb[:, :, r, :], W_bc.rearrange("(k p) n -> p k n", p=P)) for r in range(PARTS)]
        w2_loads = [(w2_sb[:, e, :, :], w2[e].rearrange("(k p) d -> p k d", p=P)) for e in range(EXPERTS)]
        w1_loads = [(w1_sb[:, e, :, :], w1[e].rearrange("(k p) h -> p k h", p=P)) for e in range(EXPERTS)]
        rep_loads = [(dst[:, :], src.rearrange("e (k p) -> p (e k)", p=P)) for dst, src in ((g1_T, ln1_g), (be1_T, ln1_b))]
        end_loads = [(dst, everywhere(v)) for dst, v in
                     ((e_g0, ln_g), (e_g1, fln_g), (e_bout, b_out), (e_b0, ln_b), (e_b1, fln_b))]
        W_SMALL, W_MAMBA = 16 * len(small_loads), 16 * len(mamba_loads)
        W_FFN = 16 * (len(w1_loads) + len(w2_loads) + len(rep_loads))

        @block.sync
        def _(sp):
            for name in ("x_in", "y_stored", "mo_stored"):
                sp.sem_inc(S[name], 16)
            for dst, src in ((bsplit[:, 0:32], b1), (bsplit[:, 32:48], b2)):
                sp.dma_start(dst, src.rearrange("e h -> (e h)").rearrange("(p c) -> p c", p=P)).then_inc(S["biases_in"], 16)
            with sp.Fori(0, TURNS) as j:
                sp.wait_ge(S["x_in"], j * 16 + 16)
                sp.dma_start(xn_all[:, bass.ds(j * GROUP, GROUP), :],
                             x[bass.ds(j * (GROUP * P), GROUP * P), :].rearrange("(n p) d -> p n d", p=P)
                             ).then_inc(S["x_in"], 16)
            for dst, src in mamba_loads:
                sp.dma_start(dst, src).then_inc(S["w_mamba"], 16)
            sp.wait_ge(S["zeros_ready"], 1)
            for n0 in range(0, LOADED, 35):
                n1 = min(LOADED, n0 + 35)
                sp.dma_start(sorted_x[n0 * P:n1 * P, :].rearrange("(n p) d -> p n d", p=P),
                             y_out[:, :].rearrange("p (a d) -> p a d", a=1).to_broadcast([P, n1 - n0, DIM])
                             ).then_inc(S["zero_fill"], 16)
            for k in range(2):
                sp.dma_start(xnT_d[CHUNKS + k].rearrange("p (n d) -> p n d", d=DIM),
                             y_out[:, :].rearrange("p (a d) -> p a d", a=1).to_broadcast([P, KD * CHUNK // DIM, DIM])
                             ).then_inc(S["zero_fill"], 16)
            for dst, src in rep_loads:
                sp.dma_start(dst, src, allow_slow_non_contiguous=True).then_inc(S["w_ffn"], 16)
            sp.wait_ge(S["b_split"], 5)
            sp.dma_start(b1_parts_d.rearrange("r (p c) -> p r c", p=P), bsplit_bf[:, :, 0:32]).then_inc(S["b_split_out"], 16)
            sp.dma_start(b2_parts_d.rearrange("r (p c) -> p r c", p=P), bsplit_bf[:, :, 32:48]).then_inc(S["b_split_out"], 16)
            sp.wait_ge(S["b_split_out"], 32)
            sp.dma_start(b1_rows[:, :, :].rearrange("r e h -> r (e h)"), b1_parts_d).then_inc(S["b_rows_in"], 16)
            sp.dma_start(b2_rows[:, :, :].rearrange("r e h -> r (e h)"), b2_parts_d).then_inc(S["b_rows_in"], 16)
            sp.wait_ge(S["placed"], 1)
            sp.wait_ge(S["xT_store0"], 16 * TURNS + 16)
            sp.wait_ge(S["xT_store1"], 16 * TURNS + 16)
            for dst, src in w1_loads + w2_loads:
                sp.dma_start(dst, src).then_inc(S["w_ffn"], 16)

            def load_tile(t):
                sp.wait_ge(S["xin_T"], t)
                sp.dma_start(xin[:, :], sorted_x[bass.ds(t * P, P), :]).then_inc(S["xin_loaded"], 16)

            def store_tile(u):
                sp.wait_ge(S["y_copied"], u + 1)
                sp.dma_start(sorted_y[bass.ds(u * P, P), :], y_out[:, :]).then_inc(S["y_stored"], 16)

            def load_chunk(g):
                sp.dma_start(xT_in, xnT_d[bass.ds(g, 1)].rearrange("o p (k t) -> p (o k) t", k=KD)).then_inc(S["xT_loaded"], 16)

            def store_mamba(c):
                sp.wait_ge(S["mo_copied"], c + 1)
                sp.dma_start(mamba_d[bass.ds(c * CHUNK, CHUNK), :].rearrange("(q p) d -> p q d", p=P),
                             mo_stage[:, :].rearrange("p (q d) -> p q d", d=DIM)).then_inc(S["mo_stored"], 16)

            sp.wait_ge(S["scattered"], 16 * 2 * TILES)
            sp.dma_start(xT_in, xnT_d[0].rearrange("p (k t) -> p k t", k=KD)).then_inc(S["xT_loaded"], 16)
            sp.wait_ge(S["zero_fill"], 16 * 6)
            sp.dma_start(xin[:, :], sorted_x[0:P, :]).then_inc(S["xin_loaded"], 16)
            sp.wait_ge(S["gate_ready"], 2)
            load_chunk(1)
            load_tile(1)
            with sp.Fori(0, BATCH) as b:
                for half in range(2):
                    for pr in range(PAIRS):
                        c = b * 2 + half
                        u = c * PAIRS + pr
                        load_tile(u + 2)
                        store_tile(u)
                        if pr == 2:
                            store_mamba(c)
                        if pr == TASKS.index("gate1"):
                            sp.wait_ge(S["gate_ready"], 2 * c + 4)
                            load_chunk(c + 2)
            store_mamba(CHUNKS)
            with sp.Fori(MAMBA_TURNS, FFN_TURNS) as u:
                load_tile(u + 2)
                store_tile(u)
            sp.wait_ge(S["xin_loaded"], 16 * LOADED)
            sp.wait_ge(S["xT_loaded"], 16 * (CHUNKS + 2))
            sp.wait_ge(S["mo_stored"], 16 * (CHUNKS + 1) + 16)
            sp.wait_ge(S["exp_done"], CHUNKS * STATE + 2)
            sp.wait_ge(S["dbx_done"], CHUNKS * STATE + 2 + 2)

            for dst, src in end_loads:
                sp.dma_start(dst, src).then_inc(S["w_end"], 16)
            with sp.Fori(0, TILES // 4) as j:
                for q in range(2):
                    t0 = (j * 2 + q) * (2 * P)
                    sp.wait_ge(S[f"e_done{q}"], j + 1)
                    sp.dma_start(ex[q], x[bass.ds(t0, 2 * P), :].rearrange("(n p) d -> p n d", p=P)).then_inc(S[f"ex_in{q}"], 16)
                    sp.dma_start(emo[q], mamba_d[bass.ds(t0 + CHUNK, 2 * P), :].rearrange("(n p) d -> p n d", p=P)).then_inc(S[f"ex_in{q}"], 16)
            sp.wait_ge(S["e_store0"], 16 * TILES // 4 + 16)
            sp.wait_ge(S["e_store1"], 16 * TILES // 4 + 16)

        @block.gpsimd
        def _(pool):
            pool.memset(y_out[:, :], 0.0).then_inc(S["zeros_ready"], 1)
            for k in range(2):
                pool.memset([ident, before][k][:, :], 0.0 if k == 0 else 1.0).then_inc(S["pool_consts"], 1)
            pool.memset(pick[:, :, :], 0.0).then_inc(S["pool_consts"], 1)
            pool.wait_ge(S["pool_consts"], 3)
            pool.affine_select(out=ident[:, :], in_=ident[:, :], compare_op=ALU.not_equal, fill=1.0, base=0,
                               pattern=[[-1, P]], channel_multiplier=1).then_inc(S["pool_consts"], 1)
            pool.affine_select(out=before[:, :], in_=before[:, :], compare_op=ALU.is_gt, fill=0.0, base=0,
                               pattern=[[1, P]], channel_multiplier=-1).then_inc(S["pool_consts"], 1)
            for r in range(PARTS):
                pool.wait_ge(S["pool_consts"], 5 + r)
                pool.affine_select(out=pick[:, :, :], in_=pick[:, :, :], compare_op=ALU.not_equal, fill=1.0,
                                   base=-BC * r, pattern=[[-1, BC], [0, P]], channel_multiplier=1
                                   ).then_inc(S["pool_consts"], 1)
            pool.memset(ones[:, :], 1.0).then_inc(S["pool_consts"], 1)
            pool.memset(ones_bf[:, :], 1.0).then_inc(S["pool_consts"], 1)
            pool.memset(eps_col[:, :], EPS).then_inc(S["pool_consts"], 1)
            pool.memset(half_neg[:, :], -0.5).then_inc(S["pool_consts"], 1)
            pool.memset(h_norm[:, :], 0.0).then_inc(S["pool_consts"], 1)
            pool.memset(h_T[:, :, :], 0.0).then_inc(S["pool_consts"], 1)
            pool.memset(ones_e, 1.0).then_inc(S["pool_consts"], 1)
            pool.memset(not_first, 1.0).then_inc(S["pool_consts"], 1)
            pool.memset(expert_of[:, 0:LAG], 0).then_inc(S["pool_consts"], 1)
            for v, step in ((iota_e[:, :], 1), (iota_tile[:, :], P), (slots, 1)):
                pool.iota(v, pattern=[[step, v.shape[1]]], base=0, channel_multiplier=0,
                          allow_small_or_imprecise_dtypes=True).then_inc(S["pool_consts"], 1)
            pool.wait_ge(S["pool_consts"], CONSTS - 1)
            pool.memset(not_first[:, :, 0:1], 0.0).then_inc(S["pool_consts"], 1)

            pool.wait_ge(S["zero_fill"], 16 * 6)
            pool.wait_ge(S["placed"], 1)
            for i in range(TILES):
                for k in range(2):
                    pool.indirect_dma_start(
                        out=sorted_x, out_offset=bass.IndirectOffsetOnAxis(ap=place[:, i, k:k + 1], axis=0),
                        in_=xn_all[:, i, :], in_offset=None).then_inc(S["scattered"], 16)

            pool.sem_inc(S["dbx_done"], 2)
            pool.memset(gate_silu[1], 0.0).then_inc(S["gate_zero"], 1)
            pool.memset(h_sb[:, 2:4], 0.0).then_inc(S["gate_zero"], 1)
            pool.wait_ge(S["gate_zero"], 2)
            pool.sem_inc(S["pair_ready"], 1)

            def inflow_of(s, n, k, g):
                pool.wait_ge(S["B_copied"], s + 1 + 1)
                pool.wait_ge(S["scan_done"], s + 1)
                if n == 0:
                    pool.wait_ge(S["dtx_ready"], g + 1)
                pool.tensor_tensor(inflow[:, k], dtx, B_rep[:, k].rearrange("p (a t) -> p a t", a=1).to_broadcast([P, KD, CHUNK]),
                                   ALU.mult).then_inc(S["dbx_done"], 1)

            def sum_pair(u, before):
                pool.wait_ge(S["hC_done"], 2 * u + 2)
                pool.wait_ge(S["sum_done"], u + 1)
                pool.tensor_tensor(pair_sum[:, :, :], h_sb[:, 2 * before], h_sb[:, 2 * before + 1], ALU.add
                                   ).then_inc(S["pair_ready"], 1)

            def rstd_of(u):
                pool.wait_ge(S["var_ready"], u + 1)
                pool.tensor_tensor(hve[:, :], hmv[:, 1:2], eps_col[:, :], ALU.add).then_inc(S["ve_h"], 1)
                pool.wait_ge(S["ve_h"], u + 1)
                pool.tensor_tensor(hrs[:, :], hve[:, :], half_neg[:, :], ALU.pow).then_inc(S["rstd_ready"], 1)

            for k in range(2):
                inflow_of(k, k, k, 0)
            with pool.Fori(0, BATCH) as b:
                for half in range(2):
                    for pr in range(PAIRS):
                        c = b * 2 + half
                        s = c * STATE + pr * 2
                        sum_pair(c * PAIRS + pr, 1 - pr % 2)
                        inflow_of(s + 2, (pr * 2 + 2) % STATE, 0, c + 1)
                        rstd_of(c * PAIRS + pr)
                        inflow_of(s + 3, (pr * 2 + 3) % STATE, 1, c + 1)
            sum_pair(MAMBA_TURNS, 1)
            with pool.Fori(MAMBA_TURNS, FFN_TURNS) as u:
                rstd_of(u)

            pool.wait_ge(S["y_stored"], 16 * FFN_TURNS + 16)
            pool.wait_ge(S["mo_stored"], 16 * (CHUNKS + 1) + 16)
            pool.wait_ge(S["xT_loaded"], 16 * (CHUNKS + 2))
            pool.wait_ge(S["exp_done"], CHUNKS * STATE + 2)
            pool.wait_ge(S["dbx_done"], CHUNKS * STATE + 2 + 2)
            for u in range(TILES // 2):
                if u >= 2:
                    pool.wait_ge(S[f"e_done{u % 2}"], u // 2 + 1)
                for t in range(2):
                    for k, dst in enumerate((ey1, ey2)):
                        pool.indirect_dma_start(
                            out=dst[u % 2][:, t, :], out_offset=None, in_=sorted_y,
                            in_offset=bass.IndirectOffsetOnAxis(ap=place_y[:, 2 * u + t, k:k + 1], axis=0)
                        ).then_inc(S[f"ey_in{u % 2}"], 16)

        @block.scalar
        def _(act):
            act.sem_inc(S["B_copied"], 1)
            for name in ("xT_store0", "xT_store1", "e_store0", "e_store1"):
                act.sem_inc(S[name], 16)
            for dst, src in small_loads:
                act.dma_start(dst, src).then_inc(S["w_small"], 16)

            act.wait_ge(S["pool_consts"], CONSTS)
            with act.Fori(0, TURNS) as j:
                act.wait_ge(S["ve_ready"], j + 1)
                nc.scalar.activation(rstd[:, bass.ds(j * GROUP, GROUP)], mean_var[:, bass.ds(j * GROUP, GROUP), 1],
                                     ACT.Sqrt, bias=eps_col[:, 0:1]).then_inc(S["sqrt_ready"], 1)
                for q in range(GROUP):
                    half, t = q // TPC, q % TPC
                    if t == 0:
                        act.wait_ge(S[f"xT_store{half}"], j * 16 + 16)
                    act.wait_ge(S["tr_ready"], j * GROUP + q + 1 + 1)
                    nc.scalar.activation(stage_T[half][:, :, t, :], psTr[q % 2][:, 0:KD * P].rearrange("p (k t) -> p k t", k=KD),
                                         ACT.Copy).then_inc(S["T_copied"], 1)
                    if t == TPC - 1:
                        act.wait_ge(S["T_copied"], j * GROUP + q + 1)
                        act.dma_start(xnT_d[bass.ds(j * 2 + half, 1)].rearrange("o p n -> p (o n)"),
                                      stage_T[half].rearrange("p k t n -> p (k t n)")).then_inc(S[f"xT_store{half}"], 16)
            act.wait_ge(S["scores_ready"], 1)
            nc.scalar.activation(probs, scratch, ACT.Exp).then_inc(S["exp_ready"], 1)
            act.wait_ge(S["w_small"], W_SMALL)
            nc.scalar.activation(A_sb[:, :, :], A_sb[:, :, :], ACT.Exp).then_inc(S["A_exp"], 1)
            act.wait_ge(S["A_exp"], 1)
            nc.scalar.activation(A_sb[:, :, :], A_sb[:, :, :], ACT.Copy, scale=-1.0).then_inc(S["A_exp"], 1)
            act.wait_ge(S["A_exp"], 2)
            act.sem_inc(S["gelu_done"], 1)
            act.wait_ge(S["gate_zero"], 2)
            act.sem_inc(S["gate_done"], 1)

            def copy_B(s, k):
                act.wait_ge(S["repB_ready"], s + 1)
                act.wait_ge(S["dbx_done"], s + 1)
                nc.scalar.activation(B_rep[:, k], psB[:, :], ACT.Copy).then_inc(S["B_copied"], 1)

            def decay_of(s, n, k, g, par):
                if n == 0:
                    act.wait_ge(S["dtx_ready"], g + 1)
                act.wait_ge(S["scan_done"], s + 1)
                for hd in range(KD):
                    e = nc.scalar.activation(decay[:, k, hd], dt_sb[par][:, hd], ACT.Exp, scale=A_sb[:, hd, n:n + 1])
                e.then_inc(S["exp_done"], 1)

            def copy_xT(t):
                act.wait_ge(S["xin_T"], t + 1)
                nc.scalar.activation(ffn_xT[:, :, :], psX[:, 0:KD * P].rearrange("p (k t) -> p k t", k=KD), ACT.Copy
                                     ).then_inc(S["xT_copied"], 1)

            def copy_y(u):
                act.wait_ge(S["y_ready"], u + 1)
                act.wait_ge(S["y_stored"], u * 16 + 16)
                nc.scalar.activation(y_out[:, :], psX[:, 0:DIM], ACT.Copy).then_inc(S["y_copied"], 1)

            def gelu(u):
                e = act.value_load(expert_of[0:1, bass.ds(u - 1 + LAG, 1)], min_val=0, max_val=EXPERTS - 1)
                act.wait_ge(S["y_ready"], u + 1)
                act.wait_ge(S["hT_done"], u + 1)
                for k in range(KH):
                    a = nc.scalar.activation(h_T[:, k, :], psT[:, k * P:(k + 1) * P], ACT.Gelu,
                                             scale=g1_T[:, bass.ds(e * KH + k, 1)], bias=be1_T[:, bass.ds(e * KH + k, 1)])
                a.then_inc(S["gelu_done"], 1)

            def take_dt(hd, g, par):
                act.wait_ge(S["dt_ready"], 2 * g + hd + 1)
                nc.scalar.activation(mid[:, hd], psX[:, :], ACT.Abs, bias=b_dt_sb[:, hd:hd + 1])
                nc.scalar.activation(dt_sb[par][:, hd], psX[:, :], ACT.Relu, bias=b_dt_sb[:, hd:hd + 1]
                                     ).then_inc(S["soft_taken"], 1)

            def conv_silu(g):
                act.wait_ge(S["conv_ready"], g + 1)
                nc.scalar.activation(x_conv, mid, ACT.Silu).then_inc(S["xc_ready"], 1)

            def gate_silu_of(g, par):
                act.wait_ge(S["gate_raw"], 2 * g + 2)
                nc.scalar.activation(gate_silu[par], gate_silu[par], ACT.Silu).then_inc(S["gate_done"], 1)

            def soft_exp(g):
                act.wait_ge(S["soft_taken"], 2 * g + 2)
                nc.scalar.activation(mid, mid, ACT.Exp, scale=-1.0).then_inc(S["soft_exp"], 1)

            def soft_ln(g):
                act.wait_ge(S["soft_exp"], g + 1)
                nc.scalar.activation(mid, mid, ACT.Ln, bias=1.0).then_inc(S["soft_ready"], 1)

            conv_silu(0)
            gate_silu_of(0, 0)
            take_dt(0, 0, 0)
            take_dt(1, 0, 0)
            soft_exp(0)
            soft_ln(0)
            for k in range(2):
                copy_B(k, k)
                decay_of(k, k, k, 0, 0)
            copy_xT(0)
            with act.Fori(0, BATCH) as b:
                for half in range(2):
                    for pr in range(PAIRS):
                        c = b * 2 + half
                        u = c * PAIRS + pr
                        s = c * STATE + pr * 2
                        g, ahead = c + 1, 1 - half
                        state = [(pr * 2 + 2 + k) % STATE for k in range(2)]
                        par = half if pr < PAIRS - 1 else ahead
                        if TASKS[pr - 1] in ("dt0", "dt1"):
                            take_dt(int(TASKS[pr - 1][-1]), g, ahead)
                        copy_B(s + 2, 0)
                        decay_of(s + 2, state[0], 0, g, par)
                        copy_y(u)
                        copy_B(s + 3, 1)
                        copy_xT(u + 1)
                        if pr == DT_TAKEN:
                            soft_exp(g)
                            soft_ln(g)
                        gelu(u)
                        if pr == CONV_TURN:
                            act.wait_ge(S["seed_done"], g + 1)
                            conv_silu(g)
                        if pr == PAIRS - 1:
                            gate_silu_of(g, ahead)
                        decay_of(s + 3, state[1], 1, g, par)
            with act.Fori(MAMBA_TURNS, FFN_TURNS) as u:
                copy_y(u)
                copy_xT(u + 1)
                gelu(u)

            with act.Fori(0, TILES // 4) as j:
                for q in range(2):
                    act.wait_ge(S["e_var"], j * 2 + q + 1)
                    nc.scalar.activation(ers[q], emv[q][:, :, :, 1], ACT.Sqrt, bias=eps_col[:, 0:1]).then_inc(S["e_sqrt"], 1)
                    act.wait_ge(S[f"e_done{q}"], j + 1 + 1)
                    act.dma_start(out[bass.ds((j * 2 + q) * (2 * P), 2 * P), :].rearrange("(n p) d -> p n d", p=P), eo[q]
                                  ).then_inc(S[f"e_store{q}"], 16)

        @block.tensor
        def _(pe):
            for name, ahead in (("tr_ready", 1), ("sum_done", 1)):
                pe.sem_inc(S[name], ahead)
            pe.wait_ge(S["pool_consts"], CONSTS)
            pe.wait_ge(S["w_small"], W_SMALL)

            def logits_of(j, q):
                t = j * GROUP + q
                pe.wait_ge(S["T_copied"], t + 1)
                for k in range(KD):
                    m = nc.tensor.matmul(psX[:, bass.ds(t * EXPERTS, EXPERTS)], stage_T[q // TPC][:, k, q % TPC, :],
                                         gate_sb[:, k, :], start=(k == 0), stop=(k == KD - 1))
                m.then_inc(S["logits_done"], 1)

            with pe.Fori(0, TURNS) as j:
                for q in range(GROUP):
                    pe.wait_ge(S["xn_ready"], j * GROUP + q + 1)
                    if q >= 2:
                        pe.wait_ge(S["T_copied"], j * GROUP + q - 1)
                    for k in range(KD):
                        m = nc.tensor.transpose(psTr[q % 2][:, k * P:(k + 1) * P],
                                                xn_turn[:, q, k * P:(k + 1) * P],
                                                ident[:, :])
                    m.then_inc(S["tr_ready"], 1)
                    if q >= 1:
                        logits_of(j, q - 1)
                logits_of(j, GROUP - 1)
            pe.wait_ge(S["chosen_ready"], 1)
            nc.tensor.matmul(psY[:, 0:CHUNK], before[:, :], scratch.rearrange("p t e -> p (t e)"), start=True, stop=True)
            nc.tensor.matmul(psY[:, CHUNK:], ones[:, :], scratch.rearrange("p t e -> p (t e)"), start=True, stop=True
                             ).then_inc(S["counts_ready"], 1)

            pe.wait_ge(S["w_mamba"], W_MAMBA)
            pe.wait_ge(S["w_ffn"], W_FFN)
            pe.wait_ge(S["b_rows_in"], 32)
            pe.wait_ge(S["diag_ready"], KD)

            def transpose_x(t):
                pe.wait_ge(S["xin_loaded"], 16 * (t + 1))
                for k in range(KD):
                    m = nc.tensor.transpose(psX[:, k * P:(k + 1) * P], xin[:, k * P:(k + 1) * P], ident[:, :])
                m.then_inc(S["xin_T"], 1)

            def transpose_h(u):
                pe.wait_ge(S["norm_done"], u + 1)
                pe.wait_ge(S["gelu_done"], u + 1)
                for k in range(KH):
                    m = nc.tensor.transpose(psT[:, k * P:(k + 1) * P], h_norm[:, k * P:(k + 1) * P], ident[:, :])
                m.then_inc(S["hT_done"], 1)

            def up(t):
                e = pe.value_load(expert_of[0:1, bass.ds(t + LAG, 1)], min_val=0, max_val=EXPERTS - 1)
                pe.wait_ge(S["xT_copied"], t + 1)
                pe.wait_ge(S["norm_done"], t + 1)
                for k in range(KD):
                    nc.tensor.matmul(psH[:, :], ffn_xT[:, k, :], w1_sb[:, bass.ds(e, 1), k, :].rearrange("p o h -> p (o h)"),
                                     start=(k == 0), stop=False)
                nc.tensor.matmul(psH[:, :], ones_bf[:, :], b1_rows[:, bass.ds(e, 1), :].rearrange("p o h -> p (o h)"),
                                 start=False, stop=True).then_inc(S["h_ready"], 1)

            def down(u, taken=None, g=None):
                e = pe.value_load(expert_of[0:1, bass.ds(u, 1)], min_val=0, max_val=EXPERTS - 1)
                if taken is not None:
                    wait_taken(taken, g)
                pe.wait_ge(S["xT_copied"], u + 1)
                pe.wait_ge(S["gelu_done"], u + 1)
                for k in range(KH):
                    nc.tensor.matmul(psX[:, 0:DIM], h_T[:, k, :], w2_sb[:, bass.ds(e, 1), k, :].rearrange("p o d -> p (o d)"),
                                     start=(k == 0), stop=False)
                nc.tensor.matmul(psX[:, 0:DIM], ones_bf[:, :], b2_rows[:, bass.ds(e, 1), :].rearrange("p o d -> p (o d)"),
                                 start=False, stop=True).then_inc(S["y_ready"], 1)

            def spread_B(s, n, par, g):
                if n == 0:
                    pe.wait_ge(S["bcp_ready"], g + 1)
                pe.wait_ge(S["B_copied"], s + 1)
                nc.tensor.matmul(psB[:, :], pick[:, n, :], bc_parts[par], start=True, stop=True).then_inc(S["repB_ready"], 1)

            def spread_C(s, n, k, par):
                pe.wait_ge(S["hC_done"], s + 1)
                nc.tensor.matmul(psC[:, k * CHUNK:(k + 1) * CHUNK], pick[:, n + STATE, :], bc_parts[par],
                                 start=True, stop=True).then_inc(S["repC_ready"], 1)

            def add_up(u):
                pe.wait_ge(S["pair_ready"], u + 1 + 1)
                for hd in range(KD):
                    m = nc.tensor.matmul(psY[:, hd * CHUNK:(hd + 1) * CHUNK], ident[:, :], pair_sum[:, hd],
                                         start=False, stop=True, skip_group_check=True)
                m.then_inc(S["sum_done"], 1)

            def seed():
                for hd in range(KD):
                    m = nc.tensor.matmul(psY[:, hd * CHUNK:(hd + 1) * CHUNK], diagD[:, hd, :], x_conv[:, hd], start=True, stop=True)
                m.then_inc(S["seed_done"], 1)

            def project(dst, weights, src, done):
                for k in range(KD):
                    m = nc.tensor.matmul(dst, weights[k], src[:, k], start=(k == 0), stop=(k == KD - 1))
                m.then_inc(S[done], 1)

            def task(name, g):
                hd = int(name[-1]) if name[-1].isdigit() else 0
                if name[:3] == "ssm":
                    pe.wait_ge(S["xT_loaded"], 16 * (g + 1))
                    project(psX[:, :], [W_in_sb[:, k, hd * P:(hd + 1) * P] for k in range(KD)], xT_in, "ssm_ready")
                elif name[:4] == "gate":
                    project(psX[:, :], [W_in_sb[:, k, DIM + hd * P:DIM + (hd + 1) * P] for k in range(KD)], xT_in, "gate_ready")
                elif name == "bc":
                    pe.wait_ge(S["xc_ready"], g + 1)
                    project(psX[0:PARTS * BC, :], [W_bc_sb[:, k, :, :].rearrange("p r n -> p (r n)") for k in range(KD)],
                            x_conv, "bc_ready")
                elif name[:2] == "dt":
                    project(psX[:, :], [W_dt_sb[:, k, hd * P:(hd + 1) * P] for k in range(KD)], x_conv, "dt_ready")

            def wait_taken(name, g):
                sem_of, count = {"ssm0": ("xpad_ready", 2 * g + 1), "ssm1": ("xpad_ready", 2 * g + 2),
                                 "gate0": ("gate_raw", 2 * g + 1), "gate1": ("gate_raw", 2 * g + 2),
                                 "bc": ("bc_taken", g + 1),
                                 "dt0": ("soft_taken", 2 * g + 1), "dt1": ("soft_taken", 2 * g + 2)}[name]
                pe.wait_ge(S[sem_of], count)

            def project_out(c):
                pe.wait_ge(S["y_gated"], c + 1)
                for q in range(TPC):
                    for k in range(KD):
                        m = nc.tensor.matmul(psY[:, q * DIM:(q + 1) * DIM], gated[:, k, q * P:(q + 1) * P], W_out_sb[:, k, :],
                                             start=(k == 0), stop=(k == KD - 1))
                m.then_inc(S["out_ready"], 1)

            order = ["ssm0", "ssm1", "gate0", "gate1", "bc", "dt0", "dt1"]
            for at, name in enumerate(order):
                if at:
                    wait_taken(order[at - 1], 0)
                task(name, 0)
            wait_taken("dt1", 0)
            seed()
            spread_B(0, 0, 0, 0)
            spread_C(0, 0, 0, 0)
            spread_B(1, 1, 0, 0)
            transpose_x(0)
            up(0)
            with pe.Fori(0, BATCH) as b:
                for half in range(2):
                    for pr in range(PAIRS):
                        c = b * 2 + half
                        u = c * PAIRS + pr
                        s = c * STATE + pr * 2
                        g, ahead = c + 1, 1 - half
                        state = [(pr * 2 + 2 + k) % STATE for k in range(2)]
                        par = half if pr < PAIRS - 1 else ahead
                        spread_B(s + 2, state[0], par, g)
                        down(u, TASKS[pr - 1] if pr > 0 else None, g)
                        transpose_h(u)
                        spread_B(s + 3, state[1], par, g)
                        spread_C(s + 1, pr * 2 + 1, 1, half)
                        pe.wait_ge(S["y_copied"], u + 1)
                        transpose_x(u + 1)
                        if pr == 1:
                            pe.wait_ge(S["mo_copied"], c + 1)
                            seed()
                        add_up(u)
                        spread_C(s + 2, state[0], 0, par)
                        pe.wait_ge(S["xT_copied"], u + 1 + 1)
                        if TASKS[pr] is not None:
                            task(TASKS[pr], g)
                        up(u + 1)
                        if pr == 0:
                            project_out(c)
            add_up(MAMBA_TURNS)
            project_out(CHUNKS)
            with pe.Fori(MAMBA_TURNS, FFN_TURNS) as u:
                transpose_h(u)
                down(u)
                pe.wait_ge(S["y_copied"], u + 1)
                transpose_x(u + 1)
                up(u + 1)

        @block.vector
        def _(dve):
            V = nc.vector
            chain = Chain(dve, S["dve_chain"])
            one = lambda v, shape: v.to_broadcast(shape)

            def hold():
                V.memset(held[:, :], 0.0)

            for name, ahead in (("norm_done", 1), ("scan_done", 2), ("hC_done", 2), ("e_done0", 1), ("e_done1", 1)):
                dve.sem_inc(S[name], ahead)

            dve.wait_ge(S["biases_in"], 32)
            for r in range(PARTS):
                V.tensor_copy(bsplit_bf[:, r, :], bsplit[:, :]).then_inc(S["b_split"], 1)
                dve.wait_ge(S["b_split"], 2 * r + 1)
                if r < PARTS - 1:
                    V.tensor_tensor(bsplit[:, :], bsplit[:, :], bsplit_bf[:, r, :], ALU.subtract).then_inc(S["b_split"], 1)
                    dve.wait_ge(S["b_split"], 2 * r + 2)

            with dve.Fori(0, TURNS) as j:
                with chain.turn(j, TURNS, 2 * GROUP + 1):
                    dve.wait_ge(S["x_in"], 16 * (j + 1) + 16)
                    for q in range(GROUP):
                        chain.mark(V.bn_stats(stats[:, q, :], xn_all[:, bass.ds(j * GROUP + q, 1), :].rearrange("p o d -> p (o d)")))
                    chain.wait()
                    hold()
                    for q in range(GROUP):
                        chain.mark(V.bn_aggr(turn_mv[:, q, :], stats[:, q, :]))
                    chain.wait()
                    V.tensor_copy(mean_var[:, bass.ds(j * GROUP, GROUP), :], turn_mv[:, :, :]).then_inc(S["ve_ready"], 1)
                    dve.wait_ge(S["sqrt_ready"], j + 1)
                    r8 = rstd[:, bass.ds(j * GROUP, GROUP)]
                    chain.mark(V.reciprocal(r8, r8))
                    chain.wait()
                    for q in range(GROUP):
                        t = bass.ds(j * GROUP + q, 1)
                        v = xn_all[:, t, :].rearrange("p o d -> p (o d)")
                        if q == 0:
                            dve.wait_ge(S["tr_ready"], j * GROUP + 1)
                        V.tensor_scalar(xn_turn[:, q, :], v, mean_var[:, t, 0], rstd[:, t], ALU.subtract, ALU.mult
                                        ).then_inc(S["xn_ready"], 1)
                    for q in range(GROUP):
                        t = bass.ds(j * GROUP + q, 1)
                        v = xn_all[:, t, :].rearrange("p o d -> p (o d)")
                        V.tensor_scalar(v, v, mean_var[:, t, 0], rstd[:, t], ALU.subtract, ALU.mult)

            def step(ins):
                chain.mark(ins)
                chain.wait()

            big = [P, TILES, EXPERTS]
            per_tile = lambda v: v[:, :].rearrange("p (t o) -> p t o", o=1).to_broadcast(big)
            per_expert = lambda v: v[:, :].rearrange("p (o e) -> p o e", o=1).to_broadcast(big)
            dve.wait_ge(S["logits_done"], TILES)
            dve.wait_ge(S["pool_consts"], CONSTS)
            step(V.tensor_copy(logits.rearrange("p t e -> p (t e)"), psX[:, :]))
            step(V.tensor_reduce(t1[:, :], logits, AX.X, ALU.max))
            V.tensor_tensor(scratch, logits, per_tile(t1), ALU.subtract).then_inc(S["scores_ready"], 1)
            dve.wait_ge(S["exp_ready"], 1)
            step(V.tensor_reduce(t1[:, :], probs, AX.X, ALU.add))
            step(V.reciprocal(t1[:, :], t1[:, :]))
            step(V.tensor_tensor(probs, probs, per_tile(t1), ALU.mult))

            def choose(top, best):
                step(V.tensor_reduce(best[:, :], probs, AX.X, ALU.max))
                step(V.tensor_tensor(scratch, probs, per_tile(best), ALU.is_ge))
                step(V.tensor_scalar(scratch, scratch, -float(EXPERTS), None, ALU.mult))
                step(V.tensor_tensor(scratch, scratch, per_expert(iota_e), ALU.add))
                step(V.tensor_reduce(t3[:, :], scratch, AX.X, ALU.min))
                step(V.tensor_tensor(top, scratch, per_tile(t3), ALU.is_equal))

            choose(top1, t1)
            step(V.tensor_scalar(scratch, top1, -2.0, None, ALU.mult))
            step(V.tensor_tensor(probs, probs, scratch, ALU.add))
            choose(top2, t2)
            V.tensor_tensor(scratch, top1, top2, ALU.add).then_inc(S["chosen_ready"], 1)
            step(V.tensor_tensor(t3[:, :], t1[:, :], t2[:, :], ALU.add))
            step(V.reciprocal(t3[:, :], t3[:, :]))
            step(V.tensor_tensor(weight[:, :, 0], t1[:, :], t3[:, :], ALU.mult))
            step(V.tensor_tensor(weight[:, :, 1], t2[:, :], t3[:, :], ALU.mult))
            dve.wait_ge(S["counts_ready"], 1)
            by_expert = lambda v: v.rearrange("p t e -> p (t e)").rearrange("p (e t) -> p e t", e=EXPERTS)
            count, upto = by_expert(probs), by_expert(logits)
            step(V.tensor_copy(count, psY[:, CHUNK:].rearrange("p (t e) -> p e t", e=EXPERTS)))
            step(V.tensor_tensor_scan(upto.rearrange("p e t -> p (e t)"), not_first.rearrange("p e t -> p (e t)"),
                                      count.rearrange("p e t -> p (e t)"), 0.0, ALU.mult, ALU.add))
            cmp = by_expert(scratch)
            step(V.tensor_tensor(cmp, upto[:, :, TILES - 1:TILES].to_broadcast([P, EXPERTS, TILES]),
                                 iota_tile[:, :].rearrange("p (o t) -> p o t", o=1).to_broadcast([P, EXPERTS, TILES]), ALU.is_gt))
            step(V.tensor_reduce(tiles_of[:, :], cmp, AX.X, ALU.add))
            step(V.tensor_tensor_scan(tiles_end[:, :], ones_e, tiles_of[:, :], 0.0, ALU.mult, ALU.add))
            step(V.tensor_tensor(rows_start[:, :], tiles_end[:, :], tiles_of[:, :], ALU.subtract))
            step(V.tensor_scalar(rows_start[:, :], rows_start[:, :], float(P), None, ALU.mult))
            step(V.tensor_tensor(upto, upto, count, ALU.subtract))
            step(V.tensor_tensor(upto, upto, rows_start[:, :].rearrange("p (e o) -> p e o", o=1).to_broadcast([P, EXPERTS, TILES]), ALU.add))
            step(V.tensor_tensor(probs, psY[:, 0:CHUNK].rearrange("p (t e) -> p t e", e=EXPERTS),
                                 upto.rearrange("p e t -> p t e"), ALU.add))
            for k, top in enumerate((top1, top2)):
                step(V.tensor_tensor(scratch, probs, top, ALU.mult))
                step(V.tensor_reduce(place_f[:, :, k], scratch, AX.X, ALU.add))
            step(V.tensor_copy(place[:, :, :], place_f[:, :, :]))
            step(V.tensor_scalar(place_f[:, :, :], place_f[:, :, :], float(LAG * P), None, ALU.add))
            step(V.tensor_copy(place_y[:, :, :], place_f[:, :, :]))
            shape = [1, LOADED, EXPERTS]
            step(V.tensor_tensor(slot_cmp[0:1], slots[0:1, :].rearrange("p (t o) -> p t o", o=1).to_broadcast(shape),
                                 tiles_end[0:1, :].rearrange("p (o e) -> p o e", o=1).to_broadcast(shape), ALU.is_ge))
            step(V.tensor_reduce(slots[0:1, :], slot_cmp[0:1], AX.X, ALU.add))
            step(V.tensor_scalar(slots[0:1, :], slots[0:1, :], float(EXPERTS - 1), None, ALU.min))
            V.tensor_copy(expert_of[:, LAG:], slots[0:1, :]).then_inc(S["placed"], 1)
            dve.wait_ge(S["w_small"], W_SMALL)
            for hd in range(KD):
                V.tensor_scalar(diagD[:, hd, :], ident[:, :], D_sb[:, hd:hd + 1], None, ALU.mult).then_inc(S["diag_ready"], 1)

            dve.wait_ge(S["scattered"], 16 * 2 * TILES)
            prep = Chain(dve, chain.sem)
            prep.base, prep.n = chain.base, chain.n

            def scan_of(u, n, k, half):
                s = 2 * u + k
                buf = 2 * (n // 2 % 2) + k
                if k == 0:
                    dve.wait_ge(S["pair_ready"], u + 1)
                dve.wait_ge(S["exp_done"], s + 1)
                dve.wait_ge(S["dbx_done"], s + 2 + 1)
                for hd in range(KD):
                    start = 0.0 if half == 0 else h_last[:, hd, n:n + 1]
                    a = V.tensor_tensor_scan(h_sb[:, buf, hd], decay[:, k, hd], inflow[:, k, hd], start, ALU.mult, ALU.add)
                a.then_inc(S["scan_done"], 1)

            def keep_last(u, n):
                buf = 2 * (n // 2 % 2)
                dve.wait_ge(S["scan_done"], 2 * u + 2 + 2)
                prep.mark(V.tensor_copy(h_last[:, :, n:n + 2].rearrange("p h n -> p n h"), h_sb[:, buf:buf + 2, :, CHUNK - 1]))

            def times_C(u, n, k, half):
                s = 2 * u + k
                h = h_sb[:, 2 * (n // 2 % 2) + k]
                dve.wait_ge(S["scan_done"], s + 2 + 1)
                if half == 0 and k == 0:
                    prep.wait()
                dve.wait_ge(S["repC_ready"], s + 1)
                V.tensor_tensor(h, h, psC[:, k * CHUNK:(k + 1) * CHUNK].rearrange("p (a t) -> p a t", a=1)
                                .to_broadcast([P, KD, CHUNK]), ALU.mult).then_inc(S["hC_done"], 1)

            def hidden_stats(u):
                dve.wait_ge(S["h_ready"], u + 1)
                V.bn_stats(hstats[:, :], psH[:, :]).then_inc(S["bn_done"], 1)
                dve.wait_ge(S["bn_done"], u + 1)

            def hidden_aggregate():
                V.bn_aggr(hmv[:, :], hstats[:, :]).then_inc(S["var_ready"], 1)

            def hidden_norm(u):
                dve.wait_ge(S["rstd_ready"], u + 1)
                dve.wait_ge(S["hT_done"], u + 1)
                V.tensor_scalar(h_norm[:, :], psH[:, :], hmv[:, 0:1], hrs[:, 0:1], ALU.subtract, ALU.mult
                                ).then_inc(S["norm_done"], 1)

            def pad_left(zero):
                if zero:
                    V.memset(xpad[:, :, 0:TAPS - 1], 0.0).then_inc(S["xpad_free"], 1)
                else:
                    V.tensor_copy(xpad[:, :, 0:TAPS - 1], xpad[:, :, CHUNK:]).then_inc(S["xpad_free"], 1)

            def take(name, g, par):
                if name in ("ssm0", "ssm1"):
                    hd = int(name[-1])
                    dve.wait_ge(S["ssm_ready"], 2 * g + hd + 1)
                    dve.wait_ge(S["xpad_free"], g + 1)
                    V.tensor_scalar(xpad[:, hd, TAPS - 1:], psX[:, :], b_in_sb[:, hd:hd + 1], None, ALU.add
                                    ).then_inc(S["xpad_ready"], 1)
                elif name in ("gate0", "gate1"):
                    hd = int(name[-1])
                    dve.wait_ge(S["gate_ready"], 2 * g + hd + 1)
                    V.tensor_scalar(gate_silu[par][:, hd], psX[:, :], b_in_sb[:, KD + hd:KD + hd + 1], None, ALU.add
                                    ).then_inc(S["gate_raw"], 1)
                elif name == "bc":
                    dve.wait_ge(S["bc_ready"], g + 1)
                    V.tensor_scalar(bc_f, psX[0:PARTS * BC, :], b_bc_sb[:, 0:1], None, ALU.add).then_inc(S["bc_taken"], 1)

            def copy_mo(c):
                dve.wait_ge(S["out_ready"], c + 1)
                dve.wait_ge(S["mo_stored"], c * 16 + 16)
                V.tensor_copy(mo_stage[:, :], psY[:, :]).then_inc(S["mo_copied"], 1)

            def convolve(g, hd):
                dve.wait_ge(S["xpad_ready"], 2 * g + hd + 1)
                for t in range(TAPS):
                    src, w = xpad[:, hd, t:t + CHUNK], conv_w_sb[:, hd, t:t + 1]
                    if t == 0:
                        a = V.tensor_scalar(mid[:, hd], src, w, conv_b_sb[:, hd:hd + 1], ALU.mult, ALU.add)
                    else:
                        prep.wait()
                        a = V.scalar_tensor_tensor(mid[:, hd], src, w, mid[:, hd], ALU.mult, ALU.add)
                    if t == TAPS - 1 and hd == KD - 1:
                        a.then_inc(S["conv_ready"], 1)
                    else:
                        prep.mark(a)

            def split_bc(g, par):
                parts = bc_parts[par]
                dve.wait_ge(S["bc_taken"], g + 1)
                prep.mark(V.tensor_copy(parts, bc_f))
                prep.wait()
                prep.mark(V.tensor_tensor(bc_f, bc_f, parts, ALU.subtract))
                prep.wait()
                prep.mark(V.tensor_copy(bc_mid, bc_f))
                prep.wait()
                prep.mark(V.tensor_copy(parts[BC:2 * BC, :], bc_mid[BC:2 * BC, :]))
                V.tensor_tensor(parts[2 * BC:, :], bc_f[2 * BC:, :], bc_mid[2 * BC:, :], ALU.subtract).then_inc(S["bcp_ready"], 1)

            def finish_dt(g, par):
                dve.wait_ge(S["soft_ready"], g + 1)
                prep.mark(V.tensor_tensor(dt_sb[par], dt_sb[par], mid, ALU.add))
                prep.wait()
                dve.wait_ge(S["dbx_done"], g * STATE + 2)
                V.tensor_tensor(dtx, dt_sb[par], x_conv, ALU.mult).then_inc(S["dtx_ready"], 1)

            def gate(c, par):
                dve.wait_ge(S["sum_done"], c * PAIRS + 2)
                dve.wait_ge(S["gate_done"], c + 1)
                V.tensor_tensor(gated, psY[:, :].rearrange("p (a t) -> p a t", a=KD), gate_silu[par], ALU.mult
                                ).then_inc(S["y_gated"], 1)

            pad_left(True)
            for name in ("ssm0", "ssm1", "gate0", "gate1"):
                take(name, 0, 0)
            for hd in range(KD):
                convolve(0, hd)
            take("bc", 0, 0)
            split_bc(0, 0)
            finish_dt(0, 0)
            dve.wait_ge(S["seed_done"], 1)
            PER_CHUNK = KD * TAPS - 1 + 4 + 1
            with dve.Fori(0, BATCH) as b:
                with prep.turn(b, BATCH, 2 * PER_CHUNK + PAIRS):
                    for half in range(2):
                        for pr in range(PAIRS):
                            c = b * 2 + half
                            u = c * PAIRS + pr
                            g, ahead = c + 1, 1 - half
                            if pr > 0 and TASKS[pr - 1] is not None:
                                take(TASKS[pr - 1], g, ahead)
                            scan_of(u, pr * 2, 0, half)
                            scan_of(u, pr * 2 + 1, 1, half)
                            if half == 0:
                                keep_last(u, pr * 2)
                            if pr == 1:
                                copy_mo(c)
                            hidden_stats(u)
                            times_C(u, pr * 2, 0, half)
                            hidden_aggregate()
                            if pr == 0:
                                pad_left(ahead == 0)
                            if pr in (CONV_TURN - 1, CONV_TURN):
                                convolve(g, pr - CONV_TURN + 1)
                            times_C(u, pr * 2 + 1, 1, half)
                            if pr == 0:
                                gate(c, ahead)
                            hidden_norm(u)
                            if pr == TASKS.index("bc") + 1:
                                split_bc(g, ahead)
                            if pr == DT_TAKEN:
                                finish_dt(g, ahead)
            gate(CHUNKS, 1)
            copy_mo(CHUNKS)
            with dve.Fori(MAMBA_TURNS, FFN_TURNS) as u:
                hidden_stats(u)
                hold()
                hidden_aggregate()
                hidden_norm(u)

            dve.wait_ge(S["w_end"], 16 * len(end_loads))
            e_chain = Chain(dve, S["e_chain"])
            e_chain.mark(V.tensor_tensor(e_b0, e_b0, e_b1, ALU.add))
            two = lambda v: v.rearrange("p (o d) -> p o d", o=1).to_broadcast([P, 2, DIM])
            PER_PAIR = 16
            with dve.Fori(0, TILES // 4) as j:
                with e_chain.turn(j, TILES // 4, 2 * PER_PAIR):
                    for q in range(2):
                        tile = j * 4 + q * 2
                        dve.wait_ge(S[f"ex_in{q}"], 32 * (j + 1))
                        e_chain.wait()
                        for t in range(2):
                            at = bass.ds(tile + t, 1)
                            e_chain.mark(V.tensor_scalar(exn[q][:, t, :], ex[q][:, t, :], mean_var[:, at, 0], rstd[:, at],
                                                         ALU.subtract, ALU.mult))
                        e_chain.mark(V.tensor_tensor(er0[q], emo[q], two(e_bout), ALU.add))
                        e_chain.wait()
                        e_chain.mark(V.tensor_tensor(er0[q], er0[q], exn[q], ALU.add))
                        dve.wait_ge(S[f"ey_in{q}"], 64 * (j + 1))
                        for t in range(2):
                            wt = weight[:, bass.ds(tile + t, 1), 0]
                            e_chain.mark(V.scalar_tensor_tensor(er1[q][:, t, :], ey1[q][:, t, :], wt, exn[q][:, t, :], ALU.mult, ALU.add))
                        e_chain.wait()
                        for t in range(2):
                            wt = weight[:, bass.ds(tile + t, 1), 1]
                            e_chain.mark(V.scalar_tensor_tensor(er1[q][:, t, :], ey2[q][:, t, :], wt, er1[q][:, t, :], ALU.mult, ALU.add))
                        e_chain.wait()
                        for t in range(2):
                            for l, v in enumerate((er0, er1)):
                                e_chain.mark(V.bn_stats(estats[q][:, t, l, :], v[q][:, t, :]))
                        e_chain.wait()
                        hold()
                        for t in range(2):
                            for l in range(2):
                                a = V.bn_aggr(emv[q][:, t, l, :], estats[q][:, t, l, :])
                        a.then_inc(S["e_var"], 1)
                        dve.wait_ge(S["e_sqrt"], j * 2 + q + 1)
                        e_chain.mark(V.reciprocal(ers[q], ers[q]))
                        for t in range(2):
                            for l, (v, g) in enumerate(((er0, e_g0), (er1, e_g1))):
                                a = V.scalar_tensor_tensor(v[q][:, t, :], v[q][:, t, :], emv[q][:, t, l, 0:1], g, ALU.subtract, ALU.mult)
                        e_chain.mark(a)
                        e_chain.wait()
                        for t in range(2):
                            V.scalar_tensor_tensor(er0[q][:, t, :], er0[q][:, t, :], ers[q][:, t, 0:1], ex[q][:, t, :], ALU.mult, ALU.add)
                            e_chain.mark(V.scalar_tensor_tensor(er1[q][:, t, :], er1[q][:, t, :], ers[q][:, t, 1:2], e_b0, ALU.mult, ALU.add))
                        e_chain.wait()
                        dve.wait_ge(S[f"e_store{q}"], 16 * j + 16)
                        V.tensor_tensor(eo[q], er0[q], er1[q], ALU.add).then_inc(S[f"e_done{q}"], 1)


_INS = ['L0_attn_x', 'L0_attn_W_in', 'L0_attn_b_in', 'L0_attn_conv_w', 'L0_attn_conv_b', 'L0_attn_W_bc', 'L0_attn_b_bc',
        'L0_attn_W_dt', 'L0_attn_b_dt', 'L0_attn_A_log', 'L0_attn_D', 'L0_attn_W_out', 'L0_attn_b_out', 'L0_attn_ln_g',
        'L0_attn_ln_b', 'L0_ffn_gate_w', 'L0_ffn_w1', 'L0_ffn_b1', 'L0_ffn_ln1_g', 'L0_ffn_ln1_b', 'L0_ffn_w2',
        'L0_ffn_b2', 'L0_ffn_ln_g', 'L0_ffn_ln_b']


def kernel(**inputs):
    import numpy as _np
    import concourse.bacc as _bacc
    from concourse import mybir as _mybir
    from concourse.bass_utils import run_bass_kernel_spmd as _run

    nc = _bacc.Bacc("TRN2", target_bir_lowering=False, num_devices=1)
    arrays, args = {}, []
    for name in _INS:
        a = _np.ascontiguousarray(inputs[name])
        arrays[name] = a
        args.append(nc.dram_tensor(name, a.shape, _mybir.dt.from_np(a.dtype), kind="ExternalInput").ap())
    args.append(nc.dram_tensor("out", (BATCH, SEQ, DIM), F32, kind="ExternalOutput").ap())
    build_program(nc, *args)
    r = _run(nc, [arrays], core_ids=[0])
    return r.results[0]["out"]
```

```python
import numpy as np
import concourse.bass as bass
from concourse import mybir
from contextlib import ExitStack, contextmanager

ALU = mybir.AluOpType
ACT = mybir.ActivationFunctionType
AX = mybir.AxisListType
F32 = mybir.dt.float32
BF16 = mybir.dt.bfloat16
I32 = mybir.dt.int32

BATCH, SEQ, DIM, STATE, TAPS = 8, 1024, 256, 16, 4
EXPERTS, HIDDEN = 8, 512
P = 128
EPS = 1e-5
KD = DIM // P
KH = HIDDEN // P
TOKENS = BATCH * SEQ
TILES = TOKENS // P
CHUNK = 512
TPC = CHUNK // P
CHUNKS = TOKENS // CHUNK
PAIRS = STATE // 2
SORTED = 2 * TILES + EXPERTS
LAG = 2
REGION = TILES + 1
FFN_TURNS = SORTED + LAG
MAMBA_TURNS = CHUNKS * PAIRS
LOADED = FFN_TURNS + 2
IDLE_BLOCKS = LOADED - 2 * TILES
BLOCKS = EXPERTS * REGION + IDLE_BLOCKS
GROUP = 8
TURNS = TILES // GROUP
PARTS = 3
BC = 2 * STATE
TASKS = ["ssm0", "ssm1", "gate0", "bc", "dt0", "dt1", "gate1", None]
CONV_TURN = TASKS.index("ssm1") + 1
GATE_TURN = 3
DT_TAKEN = TASKS.index("dt1") + 1
END_BUFS = 4
CONSTS = 23


class Chain:

    def __init__(self, eng, sem):
        self.eng, self.sem, self.base, self.n = eng, sem, 0, 0

    def mark(self, ins):
        ins.then_inc(self.sem, 1)
        self.n += 1

    def wait(self):
        self.eng.wait_ge(self.sem, self.base + self.n)

    @contextmanager
    def turn(self, i, turns, per_turn):
        base, n = self.base, self.n
        self.base, self.n = base + n + i * per_turn, 0
        yield
        assert self.n == per_turn, (self.n, per_turn)
        self.base, self.n = base, n + turns * per_turn


def build_program(nc, x, W_in, b_in, conv_w, conv_b, W_bc, b_bc, W_dt, b_dt, A_log, D_skip, W_out, b_out,
                  ln_g, ln_b, gate_w, w1, b1, ln1_g, ln1_b, w2, b2, fln_g, fln_b, out):
    x = x.rearrange("b t d -> (b t) d")
    out = out.rearrange("b t d -> (b t) d")
    xnT_d = nc.dram_tensor("xnT_d", [CHUNKS + 2, P, KD * CHUNK], F32).ap()
    sorted_x = nc.dram_tensor("sorted_x", [BLOCKS * P, DIM], F32).ap()
    sorted_y = nc.dram_tensor("sorted_y", [FFN_TURNS * P, DIM], F32).ap()
    mamba_d = nc.dram_tensor("mamba_d", [TOKENS + CHUNK, DIM], F32).ap()
    B_rows_d = nc.dram_tensor("B_rows_d", [CHUNKS + 1, STATE, CHUNK], F32).ap()
    b1_parts_d = nc.dram_tensor("b1_parts_d", [PARTS, EXPERTS * HIDDEN], BF16).ap()
    b2_parts_d = nc.dram_tensor("b2_parts_d", [PARTS, EXPERTS * DIM], BF16).ap()

    ctx = ExitStack()
    with ctx:
        def sb(name, shape, dt=F32):
            return ctx.enter_context(nc.sbuf_tensor(name, shape, dt))

        def pb(name, shape):
            return ctx.enter_context(nc.psum_tensor(name, shape, F32))

        def sem(name):
            return ctx.enter_context(nc.semaphore(name))

        w1_sb = sb("w1_sb", [P, EXPERTS, KD, HIDDEN])
        w2_sb = sb("w2_sb", [P, EXPERTS, KH, DIM])
        g1_T = sb("g1_T", [P, EXPERTS * KH])
        be1_T = sb("be1_T", [P, EXPERTS * KH])
        b1_rows = sb("b1_rows", [PARTS, EXPERTS, HIDDEN], BF16)
        b2_rows = sb("b2_rows", [PARTS, EXPERTS, DIM], BF16)
        gate_sb = sb("gate_sb", [P, KD, EXPERTS])
        W_in_sb = sb("W_in_sb", [P, KD, 2 * DIM])
        W_dt_sb = sb("W_dt_sb", [P, KD, DIM])
        W_out_sb = sb("W_out_sb", [P, KD, DIM])
        W_bc_sb = sb("W_bc_sb", [P, KD, PARTS, BC])
        b_in_sb = sb("b_in_sb", [P, 2 * KD])
        conv_w_sb = sb("conv_w_sb", [P, KD, TAPS])
        conv_b_sb = sb("conv_b_sb", [P, KD])
        b_dt_sb = sb("b_dt_sb", [P, KD])
        b_bc_sb = sb("b_bc_sb", [PARTS * BC, 1])
        A_sb = sb("A_sb", [P, KD, STATE])
        D_sb = sb("D_sb", [P, KD])
        diagD = sb("diagD", [P, KD, P])
        ident = sb("ident", [P, P])
        before = sb("before", [P, P])
        ones = sb("ones", [P, P])
        ones_bf = sb("ones_bf", [PARTS, P], BF16)
        pick = sb("pick", [PARTS * BC, STATE, P], BF16)
        eps_col = sb("eps_col", [P, 1])
        half_neg = sb("half_neg", [P, 1])
        mean_var = sb("mean_var", [P, TILES, 2])
        rstd = sb("rstd", [P, TILES])
        shift = sb("shift", [P, TILES])
        b_out_rep = sb("b_out_rep", [P, DIM])
        weight = sb("weight", [P, TILES, 2])
        place = sb("place", [P, TILES, 2], I32)
        place_y = sb("place_y", [P, TILES, 2], I32)
        pad_row = sb("pad_row", [1, EXPERTS], I32)
        row_of = sb("row_of", [1, LOADED], I32)
        expert_of = sb("expert_of", [1, LOADED + LAG], I32)

        class Carve:

            def __init__(self, tensor, size):
                self.tensor, self.size, self.at = tensor, size, 0

            def take(self, *shape):
                n = int(np.prod(shape))
                v = self.tensor[:, self.at:self.at + n]
                self.at += n
                assert self.at <= self.size, (self.at, self.size)
                if len(shape) == 2:
                    return v.rearrange("p (a b) -> p a b", a=shape[0])
                if len(shape) == 3:
                    return v.rearrange("p (a b c) -> p a b c", a=shape[0], b=shape[1])
                return v

        area = sb("area", [P, TILES * DIM])
        xn_all = area[:, :].rearrange("p (n d) -> p n d", d=DIM)
        scan_area = Carve(area, TILES * DIM)
        xT_in = scan_area.take(KD, CHUNK)
        x_conv = scan_area.take(KD, CHUNK)
        dtx = scan_area.take(KD, CHUNK)
        gate_silu = [scan_area.take(KD, CHUNK)]
        dt_sb = [scan_area.take(KD, CHUNK)]
        FIRST = -(-scan_area.at // DIM)
        gate_silu.append(scan_area.take(KD, CHUNK))
        dt_sb.append(scan_area.take(KD, CHUNK))
        decay = scan_area.take(2, KD, CHUNK)
        inflow = scan_area.take(2, KD, CHUNK)
        h_sb = scan_area.take(4, KD, CHUNK)
        scan_more = Carve(sb("more", [P, 7300]), 7300)
        B_rep = [scan_more.take(2, CHUNK) for _ in range(2)]
        xpad = scan_more.take(KD, TAPS - 1 + CHUNK)
        mid = scan_more.take(KD, CHUNK)
        gated = scan_more.take(KD, CHUNK)
        bc_f = scan_more.take(CHUNK)[0:PARTS * BC, :]
        bc_rest = scan_more.take(CHUNK)[0:PARTS * BC, :]
        bc_parts = [scan_more.take(CHUNK // 2)[0:PARTS * BC, :].bitcast(BF16) for _ in range(2)]
        bc_mid = scan_more.take(CHUNK // 2)[0:PARTS * BC, :].bitcast(BF16)
        mo_stage = sb("mo_stage", [P, KD * CHUNK])
        pair_sum = sb("pair_sum", [P, KD, CHUNK])
        end_area = Carve(area, TILES * DIM)
        ex, emo, ey1, ey2, exn, er0, er1, eo = ([end_area.take(2, DIM) for _ in range(END_BUFS)] for _ in range(8))
        more_again = Carve(scan_more.tensor, 7300)
        e_g0, e_g1, e_b0, e_b1 = (more_again.take(DIM) for _ in range(4))
        estats = [more_again.take(2, 2, 6) for _ in range(END_BUFS)]
        emv = [more_again.take(2, 2, 2) for _ in range(END_BUFS)]
        ers, enm = ([more_again.take(2, 2) for _ in range(END_BUFS)] for _ in range(2))
        early = Carve(w1_sb[:, :, :, :].rearrange("p e k h -> p (e k h)"), EXPERTS * KD * HIDDEN)
        stage_T = [early.take(KD, TPC, P) for _ in range(2)]
        ring = Carve(w2_sb[:, :, :, :].rearrange("p e k d -> p (e k d)"), EXPERTS * KH * DIM)
        xn_turn = ring.take(GROUP, DIM)
        logits, probs, top1, top2, scratch = (early.take(GROUP, EXPERTS) for _ in range(5))
        count, upto, not_first = (early.take(EXPERTS, GROUP) for _ in range(3))
        row_next, row_base = early.take(EXPERTS), early.take(EXPERTS)
        in_use = early.take(EXPERTS, TILES)
        expert_f, block_f = early.take(LOADED), early.take(LOADED)
        slot_cmp = early.take(LOADED, EXPERTS)
        slots = early.take(LOADED)
        ones_e = early.take(EXPERTS)
        bsplit = early.take(48)
        bsplit_bf = early.take(PARTS * 48 // 2).bitcast(BF16).rearrange("p (r n) -> p r n", r=PARTS)
        iota_e, iota_tile = early.take(EXPERTS), early.take(TILES)
        t1, t2, t3 = (early.take(GROUP) for _ in range(3))
        place_f = early.take(GROUP, 2)
        results = Carve(mo_stage, KD * CHUNK)
        result_row, region_shift, place_step = (results.take(TILES, 2) for _ in range(3))
        h_last = sb("h_last", [P, KD, STATE])
        xin = sb("xin", [P, DIM])
        ffn_xT = sb("ffn_xT", [P, KD, P])
        h_norm = sb("h_norm", [P, HIDDEN])
        h_T = sb("h_T", [P, KH, P])
        y_out = sb("y_out", [P, DIM])
        stats = sb("stats", [P, GROUP, 6])
        turn_mv = sb("turn_mv", [P, GROUP, 2])
        hstats = sb("hstats", [P, 6])
        hmv = sb("hmv", [P, 2])
        hve = sb("hve", [P, 1])
        held = sb("held", [P, 1])
        hrs = sb("hrs", [P, 1])
        tiles_of, tiles_end, skipped = (sb(f"te{i}", [P, EXPERTS]) for i in range(3))

        psY = pb("psY", [P, KD * CHUNK])
        psC = pb("psC", [P, 2 * CHUNK])
        psB = pb("psB", [P, CHUNK])
        psH = pb("psH", [P, HIDDEN])
        psT = pb("psT", [P, HIDDEN])
        psX = pb("psX", [P, HIDDEN])
        psTr = [psH, psT]

        names = """gate_zero w_small w_mamba w_ffn w_end biases_in pads_found pad_fill b_split b_split_out b_rows_in consts_pool zeros_ready
            zero_fill x_in ve_ready sqrt_ready xn_ready tr_ready T_copied logits_done xT_store0 xT_store1
            scores_ready exp_ready chosen_ready counts_ready logits_taken placed xn_kept tables_ready results_placed scattered_first scattered dve_chain A_exp diag_ready
            xT_loaded ssm_ready gate_ready xpad_free xpad_ready gate_raw gate_done conv_ready xc_ready bc_ready
            bc_taken dt_ready bcp_ready soft_taken soft_exp soft_ready dtx_ready seed_done B_stored B_loaded0 B_loaded1 repC_ready
            exp_done dbx_done scan_done hC_done pair_ready sum_done y_gated out_ready mo_copied mo_stored
            xin_loaded xin_T xT_copied h_ready bn_done var_ready ve_h rstd_ready norm_done hT_done gelu_done
            y_ready y_copied y_stored pool_consts
            e_bias e_xb e_mamba exn_ready e_chain e_var e_sqrt e_scale e_norm""".split()
        names += [f"{n}{q}" for n in ("ex_in", "ey_in", "e_done", "e_store") for q in range(END_BUFS)]
        S = {n: sem(n) for n in names}
        block = ctx.enter_context(nc.Block())

        def column(v, k):
            return v.rearrange("(k p o) -> k p o", p=P, o=1)[k]

        def everywhere(v):
            return v.rearrange("(a n) -> a n", a=1).to_broadcast([P, v.shape[0]])

        small_loads = [
            (gate_sb[:, :, :], gate_w.rearrange("(k p) e -> p k e", p=P)),
            (A_sb[:, :, :], A_log.rearrange("(k p) n -> p k n", p=P)),
            (conv_w_sb[:, :, :], conv_w.rearrange("(k p) o t -> p k (o t)", p=P)),
            (b_out_rep[:, :], everywhere(b_out)),
        ]
        for dst, src, n in ((b_in_sb, b_in, 2 * KD), (conv_b_sb, conv_b, KD), (b_dt_sb, b_dt, KD), (D_sb, D_skip, KD)):
            small_loads += [(dst[:, k:k + 1], column(src, k)) for k in range(n)]
        small_loads += [(b_bc_sb[r * BC:(r + 1) * BC, :], b_bc.rearrange("(p o) -> p o", o=1)) for r in range(PARTS)]
        mamba_loads = [
            (W_in_sb[:, :, :], W_in.rearrange("(k p) n -> p k n", p=P)),
            (W_dt_sb[:, :, :], W_dt.rearrange("(k p) n -> p k n", p=P)),
            (W_out_sb[:, :, :], W_out.rearrange("(k p) n -> p k n", p=P)),
        ] + [(W_bc_sb[:, :, r, :], W_bc.rearrange("(k p) n -> p k n", p=P)) for r in range(PARTS)]
        w2_loads = [(w2_sb[:, e, :, :], w2[e].rearrange("(k p) d -> p k d", p=P)) for e in range(EXPERTS)]
        w1_loads = [(w1_sb[:, e, :, :], w1[e].rearrange("(k p) h -> p k h", p=P)) for e in range(EXPERTS)]
        rep_loads = [(dst[:, :], src.rearrange("e (k p) -> p (e k)", p=P)) for dst, src in ((g1_T, ln1_g), (be1_T, ln1_b))]
        end_loads = [(dst, everywhere(v)) for dst, v in
                     ((e_g0, ln_g), (e_g1, fln_g), (e_b0, ln_b), (e_b1, fln_b))]
        w1_after, w2_after = -(-early.at // (KD * HIDDEN)), -(-ring.at // (KH * DIM))
        W_SMALL, W_MAMBA = 16 * len(small_loads), 16 * len(mamba_loads)
        W_FFN = 16 * (len(w1_loads) + len(w2_loads) + len(rep_loads))

        @block.sync
        def _(sp):
            for name in ["x_in", "y_stored", "mo_stored"] + [f"e_store{q}" for q in range(END_BUFS)]:
                sp.sem_inc(S[name], 16)
            for dst, src in ((bsplit[:, 0:32], b1), (bsplit[:, 32:48], b2)):
                sp.dma_start(dst, src.rearrange("e h -> (e h)").rearrange("(p c) -> p c", p=P)).then_inc(S["biases_in"], 16)
            with sp.Fori(0, TURNS) as j:
                sp.wait_ge(S["x_in"], j * 16 + 16)
                sp.dma_start(xn_all[:, bass.ds(j * GROUP, GROUP), :],
                             x[bass.ds(j * (GROUP * P), GROUP * P), :].rearrange("(n p) d -> p n d", p=P)
                             ).then_inc(S["x_in"], 16)
            for dst, src in mamba_loads:
                sp.dma_start(dst, src).then_inc(S["w_mamba"], 16)
            sp.wait_ge(S["zeros_ready"], 1)
            sp.dma_start(sorted_x[EXPERTS * REGION * P:, :].rearrange("(n p) d -> p n d", p=P),
                         y_out[:, :].rearrange("p (a d) -> p a d", a=1).to_broadcast([P, IDLE_BLOCKS, DIM])
                         ).then_inc(S["zero_fill"], 16)
            for k in range(2):
                sp.dma_start(xnT_d[CHUNKS + k].rearrange("p (n d) -> p n d", d=DIM),
                             y_out[:, :].rearrange("p (a d) -> p a d", a=1).to_broadcast([P, KD * CHUNK // DIM, DIM])
                             ).then_inc(S["zero_fill"], 16)
            for dst, src in rep_loads:
                sp.dma_start(dst, src, allow_slow_non_contiguous=True).then_inc(S["w_ffn"], 16)
            sp.wait_ge(S["b_split"], 5)
            sp.dma_start(b1_parts_d.rearrange("r (p c) -> p r c", p=P), bsplit_bf[:, :, 0:32]).then_inc(S["b_split_out"], 16)
            sp.dma_start(b2_parts_d.rearrange("r (p c) -> p r c", p=P), bsplit_bf[:, :, 32:48]).then_inc(S["b_split_out"], 16)
            sp.wait_ge(S["b_split_out"], 32)
            sp.dma_start(b1_rows[:, :, :].rearrange("r e h -> r (e h)"), b1_parts_d).then_inc(S["b_rows_in"], 16)
            sp.dma_start(b2_rows[:, :, :].rearrange("r e h -> r (e h)"), b2_parts_d).then_inc(S["b_rows_in"], 16)
            for dst, src in w1_loads[w1_after:] + w2_loads[w2_after:]:
                sp.dma_start(dst, src).then_inc(S["w_ffn"], 16)
            sp.wait_ge(S["scattered_first"], 16 * 2 * FIRST)
            sp.wait_ge(S["xT_store0"], 16 + 16)
            sp.dma_start(xT_in, xnT_d[0].rearrange("p (k t) -> p k t", k=KD)).then_inc(S["xT_loaded"], 16)
            sp.wait_ge(S["pads_found"], 1)
            for e in range(EXPERTS):
                row = sp.value_load(pad_row[0:1, e:e + 1], min_val=0, max_val=EXPERTS * REGION * P - P)
                sp.dma_start(sorted_x[bass.ds(row, P), :], y_out[:, :]).then_inc(S["pad_fill"], 16)
            sp.wait_ge(S["tables_ready"], 1)
            sp.wait_ge(S["xT_store0"], 16 * TURNS + 16)
            sp.wait_ge(S["xT_store1"], 16 * TURNS + 16)
            for dst, src in w1_loads[:w1_after] + w2_loads[:w2_after]:
                sp.dma_start(dst, src).then_inc(S["w_ffn"], 16)

            def load_tile(t):
                row = sp.value_load(row_of[0:1, bass.ds(t, 1)], min_val=0, max_val=BLOCKS * P - P)
                if not (isinstance(t, int) and t == 0):
                    sp.wait_ge(S["xin_T"], t)
                sp.dma_start(xin[:, :], sorted_x[bass.ds(row, P), :]).then_inc(S["xin_loaded"], 16)

            def store_tile(u):
                sp.wait_ge(S["y_copied"], u + 1)
                sp.dma_start(sorted_y[bass.ds(u * P, P), :], y_out[:, :]).then_inc(S["y_stored"], 16)

            def load_chunk(g):
                sp.dma_start(xT_in, xnT_d[bass.ds(g, 1)].rearrange("o p (k t) -> p (o k) t", k=KD)).then_inc(S["xT_loaded"], 16)

            def store_B(g):
                sp.wait_ge(S["bc_taken"], g + 1)
                sp.dma_start(B_rows_d[bass.ds(g, 1)].rearrange("o n t -> (o n) t"), bc_f[0:STATE, :]).then_inc(S["B_stored"], 16)

            def load_B(p, g, pr):
                if pr == 0:
                    sp.wait_ge(S["B_stored"], 16 * (g + 1))
                if not isinstance(p, int):
                    sp.wait_ge(S["dbx_done"], 2 * p)
                sp.dma_start(B_rep[pr % 2], B_rows_d[bass.ds(g, 1), 2 * pr:2 * pr + 2, :].to_broadcast([P, 2, CHUNK])
                             ).then_inc(S[f"B_loaded{pr % 2}"], 16)

            def store_mamba(c):
                sp.wait_ge(S["mo_copied"], c + 1)
                sp.dma_start(mamba_d[bass.ds(c * CHUNK, CHUNK), :].rearrange("(q p) d -> p q d", p=P),
                             mo_stage[:, :].rearrange("p (q d) -> p q d", d=DIM)).then_inc(S["mo_stored"], 16)

            sp.wait_ge(S["gate_ready"], 2)
            sp.wait_ge(S["zero_fill"], 16 * 3)
            load_chunk(1)
            store_B(0)
            load_B(0, 0, 0)
            load_B(1, 0, 1)
            sp.wait_ge(S["scattered"], 16 * 2 * (TILES - FIRST))
            sp.wait_ge(S["pad_fill"], 16 * EXPERTS)
            load_tile(0)
            load_tile(1)
            with sp.Fori(0, BATCH) as b:
                for half in range(2):
                    for pr in range(PAIRS):
                        c = b * 2 + half
                        u = c * PAIRS + pr
                        if pr == TASKS.index("bc") + 1:
                            store_B(c + 1)
                        load_B(u + 2, c + (pr + 2) // PAIRS, (pr + 2) % PAIRS)
                        load_tile(u + 2)
                        store_tile(u)
                        if pr == 2:
                            store_mamba(c)
                        if pr == TASKS.index("gate1"):
                            sp.wait_ge(S["gate_ready"], 2 * c + 4)
                            load_chunk(c + 2)
            store_mamba(CHUNKS)
            with sp.Fori(MAMBA_TURNS, FFN_TURNS) as u:
                load_tile(u + 2)
                store_tile(u)
            sp.wait_ge(S["xin_loaded"], 16 * LOADED)
            sp.wait_ge(S["xT_loaded"], 16 * (CHUNKS + 2))
            sp.wait_ge(S["mo_stored"], 16 * (CHUNKS + 1) + 16)
            sp.wait_ge(S["exp_done"], CHUNKS * STATE + 2)
            sp.wait_ge(S["dbx_done"], CHUNKS * STATE + 2 + 2)

            for dst, src in end_loads:
                sp.dma_start(dst, src).then_inc(S["w_end"], 16)
            def load_pair(k, q):
                t0 = (k * END_BUFS + q) * (2 * P)
                sp.wait_ge(S[f"e_done{q}"], k + 1)
                sp.dma_start(ex[q], x[bass.ds(t0, 2 * P), :].rearrange("(n p) d -> p n d", p=P)).then_inc(S[f"ex_in{q}"], 16)
                sp.dma_start(emo[q], mamba_d[bass.ds(t0 + CHUNK, 2 * P), :].rearrange("(n p) d -> p n d", p=P)).then_inc(S[f"ex_in{q}"], 16)

            def store_pair(k, q):
                t0 = (k * END_BUFS + q) * (2 * P)
                sp.wait_ge(S[f"e_done{q}"], k + 1 + 1)
                sp.dma_start(out[bass.ds(t0, 2 * P), :].rearrange("(n p) d -> p n d", p=P), eo[q]).then_inc(S[f"e_store{q}"], 16)

            for q in range(END_BUFS):
                load_pair(0, q)
            with sp.Fori(0, TILES // 2 // END_BUFS - 1) as k:
                for q in range(END_BUFS):
                    store_pair(k, q)
                    load_pair(k + 1, q)
            for q in range(END_BUFS):
                store_pair(TILES // 2 // END_BUFS - 1, q)
            for q in range(END_BUFS):
                sp.wait_ge(S[f"e_store{q}"], 16 * TILES // 2 // END_BUFS + 16)

        @block.gpsimd
        def _(pool):
            pool.memset(y_out[:, :], 0.0).then_inc(S["zeros_ready"], 1)
            for k in range(2):
                pool.memset([ident, before][k][:, :], 0.0 if k == 0 else 1.0).then_inc(S["pool_consts"], 1)
            pool.memset(pick[:, :, :], 0.0).then_inc(S["pool_consts"], 1)
            pool.wait_ge(S["pool_consts"], 3)
            pool.affine_select(out=ident[:, :], in_=ident[:, :], compare_op=ALU.not_equal, fill=1.0, base=0,
                               pattern=[[-1, P]], channel_multiplier=1).then_inc(S["pool_consts"], 1)
            pool.affine_select(out=before[:, :], in_=before[:, :], compare_op=ALU.is_gt, fill=0.0, base=0,
                               pattern=[[1, P]], channel_multiplier=-1).then_inc(S["pool_consts"], 1)
            for r in range(PARTS):
                pool.wait_ge(S["pool_consts"], 5 + r)
                pool.affine_select(out=pick[:, :, :], in_=pick[:, :, :], compare_op=ALU.not_equal, fill=1.0,
                                   base=-(BC * r + STATE), pattern=[[-1, STATE], [0, P]], channel_multiplier=1
                                   ).then_inc(S["pool_consts"], 1)
            pool.memset(ones[:, :], 1.0).then_inc(S["pool_consts"], 1)
            pool.memset(ones_bf[:, :], 1.0).then_inc(S["pool_consts"], 1)
            pool.memset(eps_col[:, :], EPS).then_inc(S["pool_consts"], 1)
            pool.memset(half_neg[:, :], -0.5).then_inc(S["pool_consts"], 1)
            pool.memset(h_norm[:, :], 0.0).then_inc(S["pool_consts"], 1)
            pool.memset(h_T[:, :, :], 0.0).then_inc(S["pool_consts"], 1)
            pool.memset(ones_e, 1.0).then_inc(S["pool_consts"], 1)
            pool.memset(not_first, 1.0).then_inc(S["pool_consts"], 1)
            pool.memset(expert_of[:, 0:LAG], 0).then_inc(S["pool_consts"], 1)
            for v, step in ((iota_e[:, :], 1), (iota_tile[:, :], P), (slots, 1), (row_next, REGION * P), (row_base, REGION * P)):
                pool.iota(v, pattern=[[step, v.shape[1]]], base=0, channel_multiplier=0,
                          allow_small_or_imprecise_dtypes=True).then_inc(S["pool_consts"], 1)
            pool.wait_ge(S["pool_consts"], CONSTS - 1)
            pool.memset(not_first[:, :, 0:1], 0.0).then_inc(S["pool_consts"], 1)

            for i in range(TILES):
                if i % GROUP == 0:
                    pool.wait_ge(S["xn_kept"], i // GROUP + 1 + 1)
                    pool.wait_ge(S["placed"], i // GROUP + 1)
                for k in range(2):
                    pool.indirect_dma_start(
                        out=sorted_x, out_offset=bass.IndirectOffsetOnAxis(ap=place[:, i, k:k + 1], axis=0),
                        in_=xn_all[:, i, :], in_offset=None).then_inc(S["scattered_first" if i < FIRST else "scattered"], 16)

            pool.sem_inc(S["dbx_done"], 2)
            pool.wait_ge(S["scattered"], 16 * 2 * (TILES - FIRST))
            pool.memset(gate_silu[1], 0.0).then_inc(S["gate_zero"], 1)
            pool.memset(h_sb[:, 2:4], 0.0).then_inc(S["gate_zero"], 1)
            pool.wait_ge(S["gate_zero"], 2)
            pool.sem_inc(S["pair_ready"], 1)

            def inflow_of(s, n, k, g, chunk):
                par = n // 2 % 2
                pool.wait_ge(S[f"B_loaded{par}"], 16 * (chunk * (PAIRS // 2) + n // 4 + 1))
                pool.wait_ge(S["scan_done"], s + 1)
                if n == 0:
                    pool.wait_ge(S["dtx_ready"], g + 1)
                pool.tensor_tensor(inflow[:, k], dtx, B_rep[par][:, k].rearrange("p (a t) -> p a t", a=1).to_broadcast([P, KD, CHUNK]),
                                   ALU.mult).then_inc(S["dbx_done"], 1)

            def sum_pair(u, before):
                pool.wait_ge(S["hC_done"], 2 * u + 2)
                pool.wait_ge(S["sum_done"], u + 1)
                pool.tensor_tensor(pair_sum[:, :, :], h_sb[:, 2 * before], h_sb[:, 2 * before + 1], ALU.add
                                   ).then_inc(S["pair_ready"], 1)

            def rstd_of(u):
                pool.wait_ge(S["var_ready"], u + 1)
                pool.tensor_tensor(hve[:, :], hmv[:, 1:2], eps_col[:, :], ALU.add).then_inc(S["ve_h"], 1)
                pool.wait_ge(S["ve_h"], u + 1)
                pool.tensor_tensor(hrs[:, :], hve[:, :], half_neg[:, :], ALU.pow).then_inc(S["rstd_ready"], 1)

            for k in range(2):
                inflow_of(k, k, k, 0, 0)
            with pool.Fori(0, BATCH) as b:
                for half in range(2):
                    for pr in range(PAIRS):
                        c = b * 2 + half
                        s = c * STATE + pr * 2
                        chunk = c + (pr + 1) // PAIRS
                        sum_pair(c * PAIRS + pr, 1 - pr % 2)
                        inflow_of(s + 2, (pr * 2 + 2) % STATE, 0, c + 1, chunk)
                        inflow_of(s + 3, (pr * 2 + 3) % STATE, 1, c + 1, chunk)
                        rstd_of(c * PAIRS + pr)
            sum_pair(MAMBA_TURNS, 1)
            with pool.Fori(MAMBA_TURNS, FFN_TURNS) as u:
                rstd_of(u)

            pool.wait_ge(S["y_stored"], 16 * FFN_TURNS + 16)
            pool.wait_ge(S["mo_stored"], 16 * (CHUNKS + 1) + 16)
            pool.wait_ge(S["xT_loaded"], 16 * (CHUNKS + 2))
            pool.wait_ge(S["exp_done"], CHUNKS * STATE + 2)
            pool.wait_ge(S["dbx_done"], CHUNKS * STATE + 2 + 2)
            pool.wait_ge(S["w_end"], 16 * len(end_loads))
            pool.tensor_tensor(e_b0, e_b0, e_b1, ALU.add).then_inc(S["e_bias"], 1)
            pool.wait_ge(S["e_bias"], 1)
            for u in range(TILES // 2):
                q, k = u % END_BUFS, u // END_BUFS
                if k > 0:
                    pool.wait_ge(S[f"e_done{q}"], k + 1)
                for t in range(2):
                    for e, dst in enumerate((ey1, ey2)):
                        pool.indirect_dma_start(
                            out=dst[q][:, t, :], out_offset=None, in_=sorted_y,
                            in_offset=bass.IndirectOffsetOnAxis(ap=place_y[:, 2 * u + t, e:e + 1], axis=0)
                        ).then_inc(S[f"ey_in{q}"], 16)
                pool.wait_ge(S[f"ex_in{q}"], 32 * (k + 1))
                pool.wait_ge(S[f"e_store{q}"], 16 * k + 16)
                pool.tensor_tensor(eo[q], ex[q], e_b0.rearrange("p (o d) -> p o d", o=1).to_broadcast([P, 2, DIM]), ALU.add
                                   ).then_inc(S["e_xb"], 1)
                pool.wait_ge(S["exn_ready"], u + 1)
                pool.tensor_tensor(er0[q], emo[q], exn[q], ALU.add).then_inc(S["e_mamba"], 1)

        @block.scalar
        def _(act):
            for name in ("xT_store0", "xT_store1"):
                act.sem_inc(S[name], 16)
            for dst, src in small_loads:
                act.dma_start(dst, src).then_inc(S["w_small"], 16)

            act.wait_ge(S["pool_consts"], CONSTS)
            def root_of(j):
                act.wait_ge(S["ve_ready"], j + 1)
                nc.scalar.activation(rstd[:, bass.ds(j * GROUP, GROUP)], mean_var[:, bass.ds(j * GROUP, GROUP), 1],
                                     ACT.Sqrt, bias=eps_col[:, 0:1]).then_inc(S["sqrt_ready"], 1)

            def exp_of(j):
                act.wait_ge(S["scores_ready"], j + 1)
                nc.scalar.activation(probs, scratch, ACT.Exp).then_inc(S["exp_ready"], 1)

            def copy_T(j):
                for q in range(GROUP):
                    half, t = q // TPC, q % TPC
                    if t == 0:
                        act.wait_ge(S[f"xT_store{half}"], j * 16 + 16)
                    act.wait_ge(S["tr_ready"], j * GROUP + q + 1 + 1)
                    nc.scalar.activation(stage_T[half][:, :, t, :], psTr[q % 2][:, 0:KD * P].rearrange("p (k t) -> p k t", k=KD),
                                         ACT.Copy).then_inc(S["T_copied"], 1)
                    if t == TPC - 1:
                        act.wait_ge(S["T_copied"], j * GROUP + q + 1)
                        act.dma_start(xnT_d[bass.ds(j * 2 + half, 1)].rearrange("o p n -> p (o n)"),
                                      stage_T[half].rearrange("p k t n -> p (k t n)")).then_inc(S[f"xT_store{half}"], 16)

            def keep(j):
                act.wait_ge(S["xn_ready"], (j + 1) * GROUP)
                nc.scalar.activation(xn_all[:, bass.ds(j * GROUP, GROUP), :], xn_turn[:, :, :], ACT.Copy
                                     ).then_inc(S["xn_kept"], 1)

            act.sem_inc(S["xn_kept"], 1)
            root_of(0)
            copy_T(0)
            keep(0)
            with act.Fori(0, TURNS - 1) as j:
                root_of(j + 1)
                exp_of(j)
                copy_T(j + 1)
                keep(j + 1)
            exp_of(TURNS - 1)
            act.wait_ge(S["w_small"], W_SMALL)
            nc.scalar.activation(A_sb[:, :, :], A_sb[:, :, :], ACT.Exp).then_inc(S["A_exp"], 1)
            act.wait_ge(S["A_exp"], 1)
            nc.scalar.activation(A_sb[:, :, :], A_sb[:, :, :], ACT.Copy, scale=-1.0).then_inc(S["A_exp"], 1)
            act.wait_ge(S["A_exp"], 2)
            act.sem_inc(S["gelu_done"], 1)

            def decay_of(s, n, k, g, par):
                if n == 0:
                    act.wait_ge(S["dtx_ready"], g + 1)
                act.wait_ge(S["scan_done"], s + 1)
                for hd in range(KD):
                    e = nc.scalar.activation(decay[:, k, hd], dt_sb[par][:, hd], ACT.Exp, scale=A_sb[:, hd, n:n + 1])
                e.then_inc(S["exp_done"], 1)

            def copy_xT(t):
                act.wait_ge(S["xin_T"], t + 1)
                nc.scalar.activation(ffn_xT[:, :, :], psX[:, 0:KD * P].rearrange("p (k t) -> p k t", k=KD), ACT.Copy
                                     ).then_inc(S["xT_copied"], 1)

            def copy_y(u, src=psX):
                act.wait_ge(S["y_ready"], u + 1)
                act.wait_ge(S["y_stored"], u * 16 + 16)
                nc.scalar.activation(y_out[:, :], src[:, 0:DIM], ACT.Copy).then_inc(S["y_copied"], 1)

            def expert(u):
                return act.value_load(expert_of[0:1, bass.ds(u - 1 + LAG, 1)], min_val=0, max_val=EXPERTS - 1)

            def gelu(u, e):
                act.wait_ge(S["y_ready"], u + 1)
                act.wait_ge(S["hT_done"], u + 1)
                for k in range(KH):
                    a = nc.scalar.activation(h_T[:, k, :], psT[:, k * P:(k + 1) * P], ACT.Gelu,
                                             scale=g1_T[:, bass.ds(e * KH + k, 1)], bias=be1_T[:, bass.ds(e * KH + k, 1)])
                a.then_inc(S["gelu_done"], 1)

            def take_dt(hd, g, par):
                act.wait_ge(S["dt_ready"], 2 * g + hd + 1)
                nc.scalar.activation(mid[:, hd], psB[:, :], ACT.Abs, bias=b_dt_sb[:, hd:hd + 1])
                nc.scalar.activation(dt_sb[par][:, hd], psB[:, :], ACT.Relu, bias=b_dt_sb[:, hd:hd + 1]
                                     ).then_inc(S["soft_taken"], 1)

            def conv_silu(g):
                act.wait_ge(S["conv_ready"], g + 1)
                nc.scalar.activation(x_conv, mid, ACT.Silu).then_inc(S["xc_ready"], 1)

            def gate_silu_of(g, par):
                act.wait_ge(S["gate_raw"], 2 * g + 2)
                nc.scalar.activation(gate_silu[par], gate_silu[par], ACT.Silu).then_inc(S["gate_done"], 1)

            def soft_exp(g):
                act.wait_ge(S["soft_taken"], 2 * g + 2)
                nc.scalar.activation(mid, mid, ACT.Exp, scale=-1.0).then_inc(S["soft_exp"], 1)

            def soft_ln(g):
                act.wait_ge(S["soft_exp"], g + 1)
                nc.scalar.activation(mid, mid, ACT.Ln, bias=1.0).then_inc(S["soft_ready"], 1)

            conv_silu(0)
            take_dt(0, 0, 0)
            take_dt(1, 0, 0)
            soft_exp(0)
            soft_ln(0)
            act.wait_ge(S["gate_zero"], 2)
            act.sem_inc(S["gate_done"], 1)
            for k in range(2):
                decay_of(k, k, k, 0, 0)
            copy_xT(0)
            with act.Fori(0, BATCH) as b:
                for half in range(2):
                    for pr in range(PAIRS):
                        c = b * 2 + half
                        u = c * PAIRS + pr
                        s = c * STATE + pr * 2
                        g, ahead = c + 1, 1 - half
                        state = [(pr * 2 + 2 + k) % STATE for k in range(2)]
                        par = half if pr < PAIRS - 1 else ahead
                        e = expert(u)
                        if TASKS[pr - 1] in ("dt0", "dt1"):
                            take_dt(int(TASKS[pr - 1][-1]), g, ahead)
                        decay_of(s + 2, state[0], 0, g, par)
                        copy_y(u)
                        decay_of(s + 3, state[1], 1, g, par)
                        copy_xT(u + 1)
                        if pr == DT_TAKEN:
                            soft_exp(g)
                            soft_ln(g)
                        gelu(u, e)
                        if pr == CONV_TURN:
                            act.wait_ge(S["seed_done"], g + 1)
                            conv_silu(g)
                        if pr == GATE_TURN:
                            gate_silu_of(c, half)
            with act.Fori(MAMBA_TURNS, FFN_TURNS) as u:
                copy_xT(u + 1)
                copy_y(u, psC)
                gelu(u, expert(u))

            def normalise_x(k, off):
                q, n = off % END_BUFS, k + off // END_BUFS
                act.wait_ge(S[f"ex_in{q}"], 32 * (n + 1))
                for t in range(2):
                    at = bass.ds((k * END_BUFS + off) * 2 + t, 1)
                    a = nc.scalar.activation(exn[q][:, t, :], ex[q][:, t, :], ACT.Identity, scale=rstd[:, at], bias=shift[:, at])
                a.then_inc(S["exn_ready"], 1)

            def root(k, off):
                q = off % END_BUFS
                act.wait_ge(S["e_var"], k * END_BUFS + off + 1)
                nc.scalar.activation(ers[q], emv[q][:, :, :, 1], ACT.Sqrt, bias=eps_col[:, 0:1]).then_inc(S["e_sqrt"], 1)

            def normalise_sums(k, off):
                q = off % END_BUFS
                act.wait_ge(S["e_scale"], k * END_BUFS + off + 1)
                for t in range(2):
                    for l, v in enumerate((er0, er1)):
                        a = nc.scalar.activation(v[q][:, t, :], v[q][:, t, :], ACT.Identity,
                                                 scale=ers[q][:, t, l:l + 1], bias=enm[q][:, t, l:l + 1])
                a.then_inc(S["e_norm"], 1)

            PAIRS_E = TILES // 2
            normalise_x(0, 0)
            normalise_x(0, 1)
            root(0, 0)
            with act.Fori(0, (PAIRS_E - END_BUFS) // END_BUFS) as k:
                for q in range(END_BUFS):
                    root(k, q + 1)
                    normalise_x(k, q + 2)
                    normalise_sums(k, q)
            for p in range(PAIRS_E - END_BUFS, PAIRS_E):
                if p + 1 < PAIRS_E:
                    root(0, p + 1)
                if p + 2 < PAIRS_E:
                    normalise_x(0, p + 2)
                normalise_sums(0, p)

        @block.tensor
        def _(pe):
            for name, ahead in (("tr_ready", 1), ("sum_done", 1)):
                pe.sem_inc(S[name], ahead)
            pe.wait_ge(S["pool_consts"], CONSTS)
            pe.wait_ge(S["w_small"], W_SMALL)

            def logits_of(j, q):
                t = j * GROUP + q
                if q == 0:
                    pe.wait_ge(S["logits_taken"], j + 1)
                pe.wait_ge(S["T_copied"], t + 1)
                for k in range(KD):
                    m = nc.tensor.matmul(psX[:, q * EXPERTS:(q + 1) * EXPERTS], stage_T[q // TPC][:, k, q % TPC, :],
                                         gate_sb[:, k, :], start=(k == 0), stop=(k == KD - 1))
                m.then_inc(S["logits_done"], 1)

            RANKS_AFTER = GROUP - 3

            def transposes(j, ranks_too):
                for q in range(GROUP):
                    pe.wait_ge(S["xn_ready"], j * GROUP + q + 1)
                    if q >= 2:
                        pe.wait_ge(S["T_copied"], j * GROUP + q - 1)
                    for k in range(KD):
                        m = nc.tensor.transpose(psTr[q % 2][:, k * P:(k + 1) * P],
                                                xn_turn[:, q, k * P:(k + 1) * P],
                                                ident[:, :])
                    m.then_inc(S["tr_ready"], 1)
                    if q >= 1:
                        logits_of(j, q - 1)
                    if q == RANKS_AFTER and ranks_too:
                        ranks(j - 1)
                logits_of(j, GROUP - 1)

            def ranks(j):
                pe.wait_ge(S["chosen_ready"], j + 1)
                n = GROUP * EXPERTS
                nc.tensor.matmul(psY[:, 0:n], before[:, :], scratch.rearrange("p t e -> p (t e)"), start=True, stop=True)
                nc.tensor.matmul(psY[:, CHUNK:CHUNK + n], ones[:, :], scratch.rearrange("p t e -> p (t e)"), start=True, stop=True
                                 ).then_inc(S["counts_ready"], 1)

            transposes(0, False)
            with pe.Fori(0, TURNS - 1) as j:
                transposes(j + 1, True)
            pe.wait_ge(S["w_mamba"], W_MAMBA)
            pe.wait_ge(S["diag_ready"], KD)

            def transpose_x(t):
                pe.wait_ge(S["xin_loaded"], 16 * (t + 1))
                for k in range(KD):
                    m = nc.tensor.transpose(psX[:, k * P:(k + 1) * P], xin[:, k * P:(k + 1) * P], ident[:, :])
                m.then_inc(S["xin_T"], 1)

            def transpose_h(u):
                pe.wait_ge(S["norm_done"], u + 1)
                pe.wait_ge(S["gelu_done"], u + 1)
                for k in range(KH):
                    m = nc.tensor.transpose(psT[:, k * P:(k + 1) * P], h_norm[:, k * P:(k + 1) * P], ident[:, :])
                m.then_inc(S["hT_done"], 1)

            def expert(t):
                return pe.value_load(expert_of[0:1, bass.ds(t + LAG, 1)], min_val=0, max_val=EXPERTS - 1)

            def up(t, e):
                pe.wait_ge(S["xT_copied"], t + 1)
                pe.wait_ge(S["norm_done"], t + 1)
                for k in range(KD):
                    nc.tensor.matmul(psH[:, :], ffn_xT[:, k, :], w1_sb[:, bass.ds(e, 1), k, :].rearrange("p o h -> p (o h)"),
                                     start=(k == 0), stop=False)
                nc.tensor.matmul(psH[:, :], ones_bf[:, :], b1_rows[:, bass.ds(e, 1), :].rearrange("p o h -> p (o h)"),
                                 start=False, stop=True).then_inc(S["h_ready"], 1)

            def down(u, e, dst=psX):
                pe.wait_ge(S["xT_copied"], u + 1)
                pe.wait_ge(S["gelu_done"], u + 1)
                for k in range(KH):
                    nc.tensor.matmul(dst[:, 0:DIM], h_T[:, k, :], w2_sb[:, bass.ds(e, 1), k, :].rearrange("p o d -> p (o d)"),
                                     start=(k == 0), stop=False)
                nc.tensor.matmul(dst[:, 0:DIM], ones_bf[:, :], b2_rows[:, bass.ds(e, 1), :].rearrange("p o d -> p (o d)"),
                                 start=False, stop=True).then_inc(S["y_ready"], 1)

            def spread_C(s, n, k, par, g):
                if n == 0:
                    pe.wait_ge(S["bcp_ready"], g + 1)
                pe.wait_ge(S["hC_done"], s + 1)
                nc.tensor.matmul(psC[:, k * CHUNK:(k + 1) * CHUNK], pick[:, n, :], bc_parts[par],
                                 start=True, stop=True).then_inc(S["repC_ready"], 1)

            def add_up(u):
                pe.wait_ge(S["pair_ready"], u + 1 + 1)
                for hd in range(KD):
                    m = nc.tensor.matmul(psY[:, hd * CHUNK:(hd + 1) * CHUNK], ident[:, :], pair_sum[:, hd],
                                         start=False, stop=True, skip_group_check=True)
                m.then_inc(S["sum_done"], 1)

            def seed():
                for hd in range(KD):
                    m = nc.tensor.matmul(psY[:, hd * CHUNK:(hd + 1) * CHUNK], diagD[:, hd, :], x_conv[:, hd], start=True, stop=True)
                m.then_inc(S["seed_done"], 1)

            def project(dst, weights, src, done):
                for k in range(KD):
                    m = nc.tensor.matmul(dst, weights[k], src[:, k], start=(k == 0), stop=(k == KD - 1))
                m.then_inc(S[done], 1)

            def task(name, g):
                hd = int(name[-1]) if name[-1].isdigit() else 0
                if name[:3] == "ssm":
                    pe.wait_ge(S["xT_loaded"], 16 * (g + 1))
                    project(psB[:, :], [W_in_sb[:, k, hd * P:(hd + 1) * P] for k in range(KD)], xT_in, "ssm_ready")
                elif name[:4] == "gate":
                    project(psB[:, :], [W_in_sb[:, k, DIM + hd * P:DIM + (hd + 1) * P] for k in range(KD)], xT_in, "gate_ready")
                elif name == "bc":
                    pe.wait_ge(S["xc_ready"], g + 1)
                    project(psB[0:PARTS * BC, :], [W_bc_sb[:, k, :, :].rearrange("p r n -> p (r n)") for k in range(KD)],
                            x_conv, "bc_ready")
                elif name[:2] == "dt":
                    project(psB[:, :], [W_dt_sb[:, k, hd * P:(hd + 1) * P] for k in range(KD)], x_conv, "dt_ready")

            def wait_taken(name, g):
                sem_of, count = {"ssm0": ("xpad_ready", 2 * g + 1), "ssm1": ("xpad_ready", 2 * g + 2),
                                 "gate0": ("gate_raw", 2 * g + 1), "gate1": ("gate_raw", 2 * g + 2),
                                 "bc": ("bc_taken", g + 1),
                                 "dt0": ("soft_taken", 2 * g + 1), "dt1": ("soft_taken", 2 * g + 2)}[name]
                pe.wait_ge(S[sem_of], count)

            def project_out(c):
                pe.wait_ge(S["y_gated"], c + 1)
                for q in range(TPC):
                    for k in range(KD):
                        m = nc.tensor.matmul(psY[:, q * DIM:(q + 1) * DIM], gated[:, k, q * P:(q + 1) * P], W_out_sb[:, k, :],
                                             start=(k == 0), stop=(k == KD - 1))
                m.then_inc(S["out_ready"], 1)

            order = ["ssm0", "ssm1", "gate0", "gate1", "bc", "dt0", "dt1"]
            for at, name in enumerate(order):
                if at:
                    wait_taken(order[at - 1], 0)
                task(name, 0)
                if name == "bc":
                    ranks(TURNS - 1)
            wait_taken("dt1", 0)
            pe.wait_ge(S["tables_ready"], 1)
            seed()
            spread_C(0, 0, 0, 0, 0)
            transpose_x(0)
            pe.wait_ge(S["w_ffn"], W_FFN)
            pe.wait_ge(S["b_rows_in"], 32)
            up(0, expert(0))
            with pe.Fori(0, BATCH) as b:
                for half in range(2):
                    for pr in range(PAIRS):
                        c = b * 2 + half
                        u = c * PAIRS + pr
                        s = c * STATE + pr * 2
                        g, ahead = c + 1, 1 - half
                        state = [(pr * 2 + 2 + k) % STATE for k in range(2)]
                        par = half if pr < PAIRS - 1 else ahead
                        e_down, e_up = expert(u - LAG), expert(u + 1)
                        down(u, e_down)
                        transpose_h(u)
                        spread_C(s + 1, pr * 2 + 1, 1, half, g)
                        pe.wait_ge(S["y_copied"], u + 1)
                        transpose_x(u + 1)
                        if pr == 1:
                            pe.wait_ge(S["mo_copied"], c + 1)
                            seed()
                        add_up(u)
                        spread_C(s + 2, state[0], 0, par, g)
                        if TASKS[pr] is not None:
                            wait_taken(TASKS[pr - 1] if pr else "gate1", g if pr else c)
                            task(TASKS[pr], g)
                        if pr == 0:
                            project_out(c)
                        up(u + 1, e_up)
            add_up(MAMBA_TURNS)
            project_out(CHUNKS)
            with pe.Fori(MAMBA_TURNS, FFN_TURNS) as u:
                e_down, e_up = expert(u - LAG), expert(u + 1)
                transpose_x(u + 1)
                transpose_h(u)
                pe.wait_ge(S["y_copied"], u)
                down(u, e_down, dst=psC)
                up(u + 1, e_up)

        @block.vector
        def _(dve):
            V = nc.vector
            chain = Chain(dve, S["dve_chain"])
            one = lambda v, shape: v.to_broadcast(shape)

            def hold():
                V.memset(held[:, :], 0.0)

            for name, ahead in (("logits_taken", 1), ("norm_done", 1), ("scan_done", 2), ("hC_done", 2),
                                *((f"e_done{q}", 1) for q in range(END_BUFS))):
                dve.sem_inc(S[name], ahead)

            dve.wait_ge(S["biases_in"], 32)
            for r in range(PARTS):
                V.tensor_copy(bsplit_bf[:, r, :], bsplit[:, :]).then_inc(S["b_split"], 1)
                dve.wait_ge(S["b_split"], 2 * r + 1)
                if r < PARTS - 1:
                    V.tensor_tensor(bsplit[:, :], bsplit[:, :], bsplit_bf[:, r, :], ALU.subtract).then_inc(S["b_split"], 1)
                    dve.wait_ge(S["b_split"], 2 * r + 2)

            def step(ins):
                chain.mark(ins)
                chain.wait()

            def statistics(j):
                dve.wait_ge(S["x_in"], 16 * (j + 1) + 16)
                for q in range(GROUP):
                    chain.mark(V.bn_stats(stats[:, q, :], xn_all[:, bass.ds(j * GROUP + q, 1), :].rearrange("p o d -> p (o d)")))
                chain.wait()
                hold()
                for q in range(GROUP):
                    chain.mark(V.bn_aggr(turn_mv[:, q, :], stats[:, q, :]))
                chain.wait()
                V.tensor_copy(mean_var[:, bass.ds(j * GROUP, GROUP), :], turn_mv[:, :, :]).then_inc(S["ve_ready"], 1)

            def normalise(j):
                dve.wait_ge(S["sqrt_ready"], j + 1)
                r8 = rstd[:, bass.ds(j * GROUP, GROUP)]
                step(V.reciprocal(r8, r8))
                for q in range(GROUP):
                    t = bass.ds(j * GROUP + q, 1)
                    v = xn_all[:, t, :].rearrange("p o d -> p (o d)")
                    if q == 0:
                        dve.wait_ge(S["tr_ready"], j * GROUP + 1)
                        dve.wait_ge(S["xn_kept"], j + 1)
                    V.tensor_scalar(xn_turn[:, q, :], v, mean_var[:, t, 0], rstd[:, t], ALU.subtract, ALU.mult
                                    ).then_inc(S["xn_ready"], 1)

            big = [P, GROUP, EXPERTS]
            per_tile = lambda v: v[:, :].rearrange("p (t o) -> p t o", o=1).to_broadcast(big)
            per_expert = lambda v: v[:, :].rearrange("p (o e) -> p o e", o=1).to_broadcast(big)
            of_expert = lambda v: v[:, :].rearrange("p (e o) -> p e o", o=1).to_broadcast([P, EXPERTS, GROUP])

            def scores(j):
                dve.wait_ge(S["logits_done"], (j + 1) * GROUP)
                V.tensor_copy(logits.rearrange("p t e -> p (t e)"), psX[:, 0:GROUP * EXPERTS]).then_inc(S["logits_taken"], 1)
                dve.wait_ge(S["logits_taken"], j + 1 + 1)
                step(V.tensor_reduce(t1[:, :], logits, AX.X, ALU.max))
                V.tensor_tensor(scratch, logits, per_tile(t1), ALU.subtract).then_inc(S["scores_ready"], 1)

            def choose(top, best):
                step(V.tensor_reduce(best[:, :], probs, AX.X, ALU.max))
                step(V.tensor_tensor(scratch, probs, per_tile(best), ALU.is_ge))
                step(V.tensor_scalar(scratch, scratch, -float(EXPERTS), None, ALU.mult))
                step(V.tensor_tensor(scratch, scratch, per_expert(iota_e), ALU.add))
                step(V.tensor_reduce(t3[:, :], scratch, AX.X, ALU.min))
                step(V.tensor_tensor(top, scratch, per_tile(t3), ALU.is_equal))

            def choices(j):
                tiles = bass.ds(j * GROUP, GROUP)
                dve.wait_ge(S["exp_ready"], j + 1)
                step(V.tensor_reduce(t1[:, :], probs, AX.X, ALU.add))
                step(V.reciprocal(t1[:, :], t1[:, :]))
                step(V.tensor_tensor(probs, probs, per_tile(t1), ALU.mult))
                choose(top1, t1)
                step(V.tensor_scalar(scratch, top1, -2.0, None, ALU.mult))
                step(V.tensor_tensor(probs, probs, scratch, ALU.add))
                choose(top2, t2)
                V.tensor_tensor(scratch, top1, top2, ALU.add).then_inc(S["chosen_ready"], 1)
                step(V.tensor_tensor(t3[:, :], t1[:, :], t2[:, :], ALU.add))
                step(V.reciprocal(t3[:, :], t3[:, :]))
                step(V.tensor_tensor(weight[:, tiles, 0], t1[:, :], t3[:, :], ALU.mult))
                step(V.tensor_tensor(weight[:, tiles, 1], t2[:, :], t3[:, :], ALU.mult))

            def places(j):
                tiles = bass.ds(j * GROUP, GROUP)
                dve.wait_ge(S["counts_ready"], j + 1)
                n = GROUP * EXPERTS
                step(V.tensor_copy(count, psY[:, CHUNK:CHUNK + n].rearrange("p (t e) -> p e t", e=EXPERTS)))
                step(V.tensor_tensor_scan(upto.rearrange("p e t -> p (e t)"), not_first.rearrange("p e t -> p (e t)"),
                                          count.rearrange("p e t -> p (e t)"), 0.0, ALU.mult, ALU.add))
                step(V.tensor_tensor(count, upto, count, ALU.subtract))
                step(V.tensor_tensor(count, count, of_expert(row_next), ALU.add))
                step(V.tensor_tensor(probs, psY[:, 0:n].rearrange("p (t e) -> p t e", e=EXPERTS),
                                     count.rearrange("p e t -> p t e"), ALU.add))
                step(V.tensor_tensor(row_next[:, :].rearrange("p (e o) -> p e o", o=1),
                                     row_next[:, :].rearrange("p (e o) -> p e o", o=1), upto[:, :, GROUP - 1:GROUP], ALU.add))
                for k, top in enumerate((top1, top2)):
                    step(V.tensor_tensor(scratch, probs, top, ALU.mult))
                    step(V.tensor_reduce(place_f[:, :, k], scratch, AX.X, ALU.add))
                hold()
                V.tensor_copy(place[:, tiles, :], place_f[:, :, :]).then_inc(S["placed"], 1)

            dve.wait_ge(S["pool_consts"], CONSTS)
            STEPS_B = 1 + 3 + 2 * 6 + 2 + 4 + 6 + 4
            statistics(0)
            normalise(0)
            with dve.Fori(0, TURNS - 1) as j:
                with chain.turn(j, TURNS - 1, 2 * GROUP + 1 + STEPS_B):
                    statistics(j + 1)
                    scores(j)
                    normalise(j + 1)
                    choices(j)
                    places(j)

            def scan_of(u, n, k, half):
                s = 2 * u + k
                buf = 2 * (n // 2 % 2) + k
                if k == 0:
                    dve.wait_ge(S["pair_ready"], u + 1)
                dve.wait_ge(S["exp_done"], s + 1)
                dve.wait_ge(S["dbx_done"], s + 2 + 1)
                for hd in range(KD):
                    start = 0.0 if half == 0 else h_last[:, hd, n:n + 1]
                    a = V.tensor_tensor_scan(h_sb[:, buf, hd], decay[:, k, hd], inflow[:, k, hd], start, ALU.mult, ALU.add)
                a.then_inc(S["scan_done"], 1)

            def keep_last(u, n):
                buf = 2 * (n // 2 % 2)
                dve.wait_ge(S["scan_done"], 2 * u + 2 + 2)
                chain.mark(V.tensor_copy(h_last[:, :, n:n + 2].rearrange("p h n -> p n h"), h_sb[:, buf:buf + 2, :, CHUNK - 1]))

            def times_C(u, n, k, half):
                s = 2 * u + k
                h = h_sb[:, 2 * (n // 2 % 2) + k]
                dve.wait_ge(S["scan_done"], s + 2 + 1)
                if half == 0 and k == 0:
                    chain.wait()
                dve.wait_ge(S["repC_ready"], s + 1)
                V.tensor_tensor(h, h, psC[:, k * CHUNK:(k + 1) * CHUNK].rearrange("p (a t) -> p a t", a=1)
                                .to_broadcast([P, KD, CHUNK]), ALU.mult).then_inc(S["hC_done"], 1)

            def hidden_stats(u):
                dve.wait_ge(S["h_ready"], u + 1)
                V.bn_stats(hstats[:, :], psH[:, :]).then_inc(S["bn_done"], 1)
                dve.wait_ge(S["bn_done"], u + 1)

            def hidden_aggregate():
                V.bn_aggr(hmv[:, :], hstats[:, :]).then_inc(S["var_ready"], 1)

            def hidden_norm(u):
                dve.wait_ge(S["rstd_ready"], u + 1)
                dve.wait_ge(S["hT_done"], u + 1)
                V.tensor_scalar(h_norm[:, :], psH[:, :], hmv[:, 0:1], hrs[:, 0:1], ALU.subtract, ALU.mult
                                ).then_inc(S["norm_done"], 1)

            def pad_left(zero):
                if zero:
                    V.memset(xpad[:, :, 0:TAPS - 1], 0.0).then_inc(S["xpad_free"], 1)
                else:
                    V.tensor_copy(xpad[:, :, 0:TAPS - 1], xpad[:, :, CHUNK:]).then_inc(S["xpad_free"], 1)

            def take(name, g, par):
                if name in ("ssm0", "ssm1"):
                    hd = int(name[-1])
                    dve.wait_ge(S["ssm_ready"], 2 * g + hd + 1)
                    dve.wait_ge(S["xpad_free"], g + 1)
                    V.tensor_scalar(xpad[:, hd, TAPS - 1:], psB[:, :], b_in_sb[:, hd:hd + 1], None, ALU.add
                                    ).then_inc(S["xpad_ready"], 1)
                elif name in ("gate0", "gate1"):
                    hd = int(name[-1])
                    dve.wait_ge(S["gate_ready"], 2 * g + hd + 1)
                    V.tensor_scalar(gate_silu[par][:, hd], psB[:, :], b_in_sb[:, KD + hd:KD + hd + 1], None, ALU.add
                                    ).then_inc(S["gate_raw"], 1)
                elif name == "bc":
                    if not isinstance(g, int):
                        dve.wait_ge(S["B_stored"], 16 * g)
                    dve.wait_ge(S["bc_ready"], g + 1)
                    V.tensor_scalar(bc_f, psB[0:PARTS * BC, :], b_bc_sb[:, 0:1], None, ALU.add).then_inc(S["bc_taken"], 1)

            def copy_mo(c):
                dve.wait_ge(S["out_ready"], c + 1)
                dve.wait_ge(S["mo_stored"], c * 16 + 16)
                V.tensor_tensor(mo_stage[:, :].rearrange("p (q d) -> p q d", q=TPC), psY[:, :].rearrange("p (q d) -> p q d", q=TPC),
                                b_out_rep[:, :].rearrange("p (q d) -> p q d", q=1).to_broadcast([P, TPC, DIM]), ALU.add
                                ).then_inc(S["mo_copied"], 1)

            def convolve(g, hd):
                dve.wait_ge(S["xpad_ready"], 2 * g + hd + 1)
                for t in range(TAPS):
                    src, w = xpad[:, hd, t:t + CHUNK], conv_w_sb[:, hd, t:t + 1]
                    if t == 0:
                        a = V.tensor_scalar(mid[:, hd], src, w, conv_b_sb[:, hd:hd + 1], ALU.mult, ALU.add)
                    else:
                        chain.wait()
                        a = V.scalar_tensor_tensor(mid[:, hd], src, w, mid[:, hd], ALU.mult, ALU.add)
                    if t == TAPS - 1 and hd == KD - 1:
                        a.then_inc(S["conv_ready"], 1)
                    else:
                        chain.mark(a)

            def split_bc(g, par):
                parts = bc_parts[par]
                dve.wait_ge(S["bc_taken"], g + 1)
                chain.mark(V.tensor_copy(parts, bc_f))
                chain.wait()
                chain.mark(V.tensor_tensor(bc_rest, bc_f, parts, ALU.subtract))
                chain.wait()
                chain.mark(V.tensor_copy(bc_mid, bc_rest))
                chain.wait()
                chain.mark(V.tensor_copy(parts[BC:2 * BC, :], bc_mid[BC:2 * BC, :]))
                V.tensor_tensor(parts[2 * BC:, :], bc_rest[2 * BC:, :], bc_mid[2 * BC:, :], ALU.subtract).then_inc(S["bcp_ready"], 1)

            def finish_dt(g, par):
                dve.wait_ge(S["soft_ready"], g + 1)
                chain.mark(V.tensor_tensor(dt_sb[par], dt_sb[par], mid, ALU.add))
                chain.wait()
                dve.wait_ge(S["dbx_done"], g * STATE + 2)
                V.tensor_tensor(dtx, dt_sb[par], x_conv, ALU.mult).then_inc(S["dtx_ready"], 1)

            def gate(c, par):
                dve.wait_ge(S["sum_done"], c * PAIRS + 2)
                dve.wait_ge(S["gate_done"], c + 1)
                V.tensor_tensor(gated, psY[:, :].rearrange("p (a t) -> p a t", a=KD), gate_silu[par], ALU.mult
                                ).then_inc(S["y_gated"], 1)

            dve.wait_ge(S["w_small"], W_SMALL)
            for hd in range(KD):
                V.tensor_scalar(diagD[:, hd, :], ident[:, :], D_sb[:, hd:hd + 1], None, ALU.mult).then_inc(S["diag_ready"], 1)
            dve.wait_ge(S["scattered_first"], 16 * 2 * FIRST)
            pad_left(True)
            for name in ("ssm0", "ssm1"):
                take(name, 0, 0)
            for hd in range(KD):
                convolve(0, hd)
            scores(TURNS - 1)
            take("gate0", 0, 0)
            take("gate1", 0, 0)
            choices(TURNS - 1)
            take("bc", 0, 0)
            places(TURNS - 1)
            step(V.scalar_tensor_tensor(shift[:, :], mean_var[:, :, 0], -1.0, rstd[:, :], ALU.mult, ALU.mult))
            V.tensor_copy(pad_row[:, :], row_next[0:1, :]).then_inc(S["pads_found"], 1)
            step(V.tensor_tensor(row_base[:, :], row_next[:, :], row_base[:, :], ALU.subtract))
            step(V.tensor_tensor(in_use, row_base[:, :].rearrange("p (e o) -> p e o", o=1).to_broadcast([P, EXPERTS, TILES]),
                                 iota_tile[:, :].rearrange("p (o t) -> p o t", o=1).to_broadcast([P, EXPERTS, TILES]), ALU.is_gt))
            step(V.tensor_reduce(tiles_of[:, :], in_use, AX.X, ALU.add))
            step(V.tensor_tensor_scan(tiles_end[:, :], ones_e, tiles_of[:, :], 0.0, ALU.mult, ALU.add))
            step(V.tensor_scalar(skipped[:, :], tiles_of[:, :], -1.0, float(REGION), ALU.mult, ALU.add))
            shape = [1, LOADED, EXPERTS]
            along = lambda v: v[0:1, :].rearrange("p (o e) -> p o e", o=1).to_broadcast(shape)
            step(V.tensor_tensor(slot_cmp[0:1], slots[0:1, :].rearrange("p (t o) -> p t o", o=1).to_broadcast(shape),
                                 along(tiles_end), ALU.is_ge))
            step(V.tensor_reduce(expert_f[0:1, :], slot_cmp[0:1], AX.X, ALU.add))
            step(V.tensor_scalar(expert_f[0:1, :], expert_f[0:1, :], float(EXPERTS - 1), None, ALU.min))
            step(V.tensor_copy(expert_of[:, LAG:], expert_f[0:1, :]))
            step(V.tensor_tensor(slot_cmp[0:1], slot_cmp[0:1], along(skipped), ALU.mult))
            step(V.tensor_reduce(block_f[0:1, :], slot_cmp[0:1], AX.X, ALU.add))
            step(V.tensor_tensor(block_f[0:1, :], block_f[0:1, :], slots[0:1, :], ALU.add))
            step(V.tensor_scalar(block_f[0:1, :], block_f[0:1, :], float(P), None, ALU.mult))
            V.tensor_copy(row_of[:, :], block_f[0:1, :]).then_inc(S["tables_ready"], 1)
            split_bc(0, 0)
            chain.mark(V.tensor_scalar(skipped[:, :], skipped[:, :], float(P), None, ALU.mult))
            chain.wait()
            chain.mark(V.tensor_copy(result_row, place[:, :, :]))
            chain.wait()
            chain.mark(V.tensor_scalar(region_shift, result_row, float(REGION * P), None, ALU.is_ge))
            chain.wait()
            chain.mark(V.tensor_scalar(region_shift, region_shift, skipped[:, 0:1], None, ALU.mult))
            chain.wait()
            for e in range(2, EXPERTS):
                chain.mark(V.tensor_scalar(place_step, result_row, float(e * REGION * P), None, ALU.is_ge))
                chain.wait()
                chain.mark(V.tensor_scalar(place_step, place_step, skipped[:, e - 1:e], None, ALU.mult))
                chain.wait()
                chain.mark(V.tensor_tensor(region_shift, region_shift, place_step, ALU.add))
                chain.wait()
            chain.mark(V.tensor_tensor(result_row, result_row, region_shift, ALU.subtract))
            chain.wait()
            chain.mark(V.tensor_scalar(result_row, result_row, float(LAG * P), None, ALU.add))
            chain.wait()
            V.tensor_copy(place_y[:, :, :], result_row).then_inc(S["results_placed"], 1)
            dve.wait_ge(S["results_placed"], 1)
            finish_dt(0, 0)
            dve.wait_ge(S["seed_done"], 1)
            dve.wait_ge(S["scattered"], 16 * 2 * (TILES - FIRST))
            PER_CHUNK = KD * TAPS - 1 + 4 + 1
            with dve.Fori(0, BATCH) as b:
                with chain.turn(b, BATCH, 2 * PER_CHUNK + PAIRS):
                    for half in range(2):
                        for pr in range(PAIRS):
                            c = b * 2 + half
                            u = c * PAIRS + pr
                            g, ahead = c + 1, 1 - half
                            scan_of(u, pr * 2, 0, half)
                            scan_of(u, pr * 2 + 1, 1, half)
                            if half == 0:
                                keep_last(u, pr * 2)
                            if pr > 0 and TASKS[pr - 1] is not None:
                                take(TASKS[pr - 1], g, ahead)
                            hidden_stats(u)
                            if pr == 1:
                                copy_mo(c)
                            times_C(u, pr * 2, 0, half)
                            if pr == 0:
                                pad_left(ahead == 0)
                            if pr in (CONV_TURN - 1, CONV_TURN):
                                convolve(g, pr - CONV_TURN + 1)
                            hidden_aggregate()
                            times_C(u, pr * 2 + 1, 1, half)
                            if pr == 0:
                                gate(c, ahead)
                            hidden_norm(u)
                            if pr == TASKS.index("bc") + 1:
                                split_bc(g, ahead)
                            if pr == DT_TAKEN:
                                finish_dt(g, ahead)
            gate(CHUNKS, 1)
            copy_mo(CHUNKS)
            with dve.Fori(MAMBA_TURNS, FFN_TURNS) as u:
                hidden_stats(u)
                hold()
                hidden_aggregate()
                hidden_norm(u)

            dve.wait_ge(S["w_end"], 16 * len(end_loads))
            e_chain = Chain(dve, S["e_chain"])
            two = lambda v: v.rearrange("p (o d) -> p o d", o=1).to_broadcast([P, 2, DIM])

            def sums(k, off):
                q, n = off % END_BUFS, k + off // END_BUFS
                tile = (k * END_BUFS + off) * 2
                dve.wait_ge(S["e_mamba"], k * END_BUFS + off + 1)
                dve.wait_ge(S[f"ey_in{q}"], 64 * (n + 1))
                for y, k2, base in ((ey1, 0, exn), (ey2, 1, er1)):
                    for t in range(2):
                        e_chain.mark(V.scalar_tensor_tensor(er1[q][:, t, :], y[q][:, t, :], weight[:, bass.ds(tile + t, 1), k2],
                                                            base[q][:, t, :], ALU.mult, ALU.add))
                    e_chain.wait()
                for l, v in enumerate((er0, er1)):
                    for t in range(2):
                        e_chain.mark(V.bn_stats(estats[q][:, t, l, :], v[q][:, t, :]))
                e_chain.wait()
                hold()
                for t in range(2):
                    for l in range(2):
                        a = V.bn_aggr(emv[q][:, t, l, :], estats[q][:, t, l, :])
                a.then_inc(S["e_var"], 1)

            def scales(k, off):
                q = off % END_BUFS
                dve.wait_ge(S["e_sqrt"], k * END_BUFS + off + 1)
                e_chain.mark(V.reciprocal(ers[q], ers[q]))
                e_chain.wait()
                V.scalar_tensor_tensor(enm[q], emv[q][:, :, :, 0], -1.0, ers[q], ALU.mult, ALU.mult).then_inc(S["e_scale"], 1)

            def result(k, off):
                q = off % END_BUFS
                p = k * END_BUFS + off
                dve.wait_ge(S["e_norm"], p + 1)
                for v, gain in ((er0, e_g0), (er1, e_g1)):
                    e_chain.mark(V.tensor_tensor(v[q], v[q], two(gain), ALU.mult))
                e_chain.wait()
                e_chain.mark(V.tensor_tensor(er0[q], er0[q], er1[q], ALU.add))
                dve.wait_ge(S["e_xb"], p + 1)
                e_chain.wait()
                V.tensor_tensor(eo[q], eo[q], er0[q], ALU.add).then_inc(S[f"e_done{q}"], 1)

            PAIRS_E = TILES // 2
            PER_PAIR = 4 + 4 + 1 + 3
            sums(0, 0)
            sums(0, 1)
            scales(0, 0)
            with dve.Fori(0, (PAIRS_E - END_BUFS) // END_BUFS) as k:
                with e_chain.turn(k, (PAIRS_E - END_BUFS) // END_BUFS, END_BUFS * PER_PAIR):
                    for q in range(END_BUFS):
                        scales(k, q + 1)
                        sums(k, q + 2)
                        result(k, q)
            for p in range(PAIRS_E - END_BUFS, PAIRS_E):
                if p + 1 < PAIRS_E:
                    scales(0, p + 1)
                if p + 2 < PAIRS_E:
                    sums(0, p + 2)
                result(0, p)


_INS = ['L0_attn_x', 'L0_attn_W_in', 'L0_attn_b_in', 'L0_attn_conv_w', 'L0_attn_conv_b', 'L0_attn_W_bc', 'L0_attn_b_bc',
        'L0_attn_W_dt', 'L0_attn_b_dt', 'L0_attn_A_log', 'L0_attn_D', 'L0_attn_W_out', 'L0_attn_b_out', 'L0_attn_ln_g',
        'L0_attn_ln_b', 'L0_ffn_gate_w', 'L0_ffn_w1', 'L0_ffn_b1', 'L0_ffn_ln1_g', 'L0_ffn_ln1_b', 'L0_ffn_w2',
        'L0_ffn_b2', 'L0_ffn_ln_g', 'L0_ffn_ln_b']


def kernel(**inputs):
    import numpy as _np
    import concourse.bacc as _bacc
    from concourse import mybir as _mybir
    from concourse.bass_utils import run_bass_kernel_spmd as _run

    nc = _bacc.Bacc("TRN2", target_bir_lowering=False, num_devices=1)
    arrays, args = {}, []
    for name in _INS:
        a = _np.ascontiguousarray(inputs[name])
        arrays[name] = a
        args.append(nc.dram_tensor(name, a.shape, _mybir.dt.from_np(a.dtype), kind="ExternalInput").ap())
    args.append(nc.dram_tensor("out", (BATCH, SEQ, DIM), F32, kind="ExternalOutput").ap())
    build_program(nc, *args)
    r = _run(nc, [arrays], core_ids=[0])
    return r.results[0]["out"]
```
